# Optimizing a Trainium2 kernel written in Bass

```python
import numpy as np
import jax
import jax.numpy as jnp

def _softmax(x, axis=-1):
    return jax.nn.softmax(x, axis=axis)

def _gelu(x):
    return jax.nn.gelu(x, approximate=True)

def _silu(x):
    return jax.nn.silu(x)

def _sigmoid(x):
    return jax.nn.sigmoid(x)

def _layernorm(x, axis=-1, eps=1e-05):
    m = jnp.mean(x, axis=axis, keepdims=True)
    v = jnp.var(x, axis=axis, keepdims=True)
    return (x - m) / jnp.sqrt(v + eps)

def _scatter_add(tgt, idx, src, axis=0):
    return tgt.at[idx].add(src)

def _segment_sum(src, seg, n):
    return jax.ops.segment_sum(src, seg, n)
kernel_name = 'mk_decoder_postln_d1_seqx_r4_11403f'

def setup_inputs(seed: int=0):
    np.random.seed(seed)
    _w = jnp.asarray

    def _rec_inputs():
        import jax
        import jax.numpy as jnp
        _rk = jax.random.key(seed)
        x = 7.22e-05 + 1 * jax.random.normal(jax.random.fold_in(_rk, 1), (4, 1024, 256), jnp.float32)
        _lenS = 1024 - jax.random.randint(jax.random.fold_in(_rk, 7), (4,), 0, max(1, 1024 // 4) + 1, jnp.int32)
        _lenS2 = 154 - jax.random.randint(jax.random.fold_in(_rk, 8), (4,), 0, max(1, 154 // 4) + 1, jnp.int32)
        _ctx_1024P = jax.random.normal(jax.random.fold_in(_rk, 11), (4, 16, 256), jnp.float32)
        _ctx_1024c = jax.random.dirichlet(jax.random.fold_in(_rk, 511), 0.3 * jnp.ones((16,), jnp.float32), (4, 154))
        _ctx_1024t = jnp.einsum('bsk,bkd->bsd', _ctx_1024c, _ctx_1024P)
        _ctx_1024t = _ctx_1024t * jax.lax.rsqrt(jnp.mean(jnp.square(_ctx_1024t)) + 1e-12) * 0.953939
        ctx_1024 = 4.13588e-05 + 0.999923 * (_ctx_1024t + 0.3 * jax.random.normal(jax.random.fold_in(_rk, 611), (4, 154, 256), jnp.float32))
        fside_BxSxS2_0 = jax.random.uniform(jax.random.fold_in(_rk, 12), (4, 1024, 154), jnp.float32, 0.0, 10)
        return (x, ctx_1024, fside_BxSxS2_0)
    x, ctx_1024, fside_BxSxS2_0 = _rec_inputs()

    def _L0_attn_setup():
        import jax, jax.numpy as jnp
        import numpy as np
        B, S, H, NH = (4, 256, 256, 16)
        HD = H // NH
        CAUSAL_HEADS = 4
        META_HEADS = NH // 4
        CAUSAL_W = 0.7
        META_W = (0.9 - 0.8) / 0.2 * 0.3

        def _mha(xq, xkv, Win, bi, Wout, bout, nh):
            b, sq, h = xq.shape
            sk = xkv.shape[1]
            hd = h // nh
            q = (xq @ Win[:, :h] + bi[:h]).reshape(b, sq, nh, hd).transpose(0, 2, 1, 3)
            k = (xkv @ Win[:, h:2 * h] + bi[h:2 * h]).reshape(b, sk, nh, hd).transpose(0, 2, 1, 3)
            v = (xkv @ Win[:, 2 * h:] + bi[2 * h:]).reshape(b, sk, nh, hd).transpose(0, 2, 1, 3)
            scores = jnp.einsum('bhqd,bhkd->bhqk', q, k) / jnp.sqrt(jnp.asarray(hd, q.dtype))
            probs = jax.nn.softmax(scores, axis=-1)
            ctx = jnp.einsum('bhqk,bhkd->bhqd', probs, v)
            return ctx.transpose(0, 2, 1, 3).reshape(b, sq, h) @ Wout + bout

        def _forward(hidden_states, cons_vec, Wq, bq, Wk, bk, Wv, bv, cg_W, cg_b, am_W, am_b, ca_Win, ca_bin, ca_Wout, ca_bout, mc_Win, mc_bin, mc_Wout, mc_bout, Wo, bo):
            b, s, h = hidden_states.shape
            q = (hidden_states @ Wq + bq).reshape(b, s, NH, HD).transpose(0, 2, 1, 3)
            k = (hidden_states @ Wk + bk).reshape(b, s, NH, HD).transpose(0, 2, 1, 3)
            v = (hidden_states @ Wv + bv).reshape(b, s, NH, HD).transpose(0, 2, 1, 3)
            scores = jnp.einsum('bhqd,bhkd->bhqk', q, k) / jnp.sqrt(jnp.asarray(HD, q.dtype))
            mod = jax.nn.sigmoid(hidden_states @ cg_W + cg_b + (cons_vec @ am_W + am_b))
            scores = scores * mod.transpose(0, 2, 1)[..., None]
            probs = jax.nn.softmax(scores, axis=-1)
            ctx = jnp.einsum('bhqk,bhkd->bhqd', probs, v).transpose(0, 2, 1, 3).reshape(b, s, h)
            causal_ctx = _mha(hidden_states, hidden_states, ca_Win, ca_bin, ca_Wout, ca_bout, CAUSAL_HEADS)
            ctx = ctx * (1.0 - CAUSAL_W) + causal_ctx * CAUSAL_W
            meta_ctx = _mha(ctx, ctx, mc_Win, mc_bin, mc_Wout, mc_bout, META_HEADS)
            ctx = ctx * (1.0 - META_W) + meta_ctx * META_W
            return ctx @ Wo + bo
        key = jax.random.key(seed)
        ks = jax.random.split(key, 16)
        sc = 0.02
        d = {'hidden_states': jax.random.normal(ks[0], (B, S, H), jnp.float32), 'cons_vec': jax.random.uniform(ks[1], (16,), jnp.float32), 'Wq': jax.random.normal(ks[2], (H, H), jnp.float32) * sc, 'bq': jnp.zeros((H,), jnp.float32), 'Wk': jax.random.normal(ks[3], (H, H), jnp.float32) * sc, 'bk': jnp.zeros((H,), jnp.float32), 'Wv': jax.random.normal(ks[4], (H, H), jnp.float32) * sc, 'bv': jnp.zeros((H,), jnp.float32), 'cg_W': jax.random.normal(ks[5], (H, NH), jnp.float32) * sc, 'cg_b': jnp.zeros((NH,), jnp.float32), 'am_W': jax.random.normal(ks[6], (16, NH), jnp.float32) * sc, 'am_b': jnp.zeros((NH,), jnp.float32), 'ca_Win': jax.random.normal(ks[7], (H, 3 * H), jnp.float32) * sc, 'ca_bin': jnp.zeros((3 * H,), jnp.float32), 'ca_Wout': jax.random.normal(ks[8], (H, H), jnp.float32) * sc, 'ca_bout': jnp.zeros((H,), jnp.float32), 'mc_Win': jax.random.normal(ks[9], (H, 3 * H), jnp.float32) * sc, 'mc_bin': jnp.zeros((3 * H,), jnp.float32), 'mc_Wout': jax.random.normal(ks[10], (H, H), jnp.float32) * sc, 'mc_bout': jnp.zeros((H,), jnp.float32), 'Wo': jax.random.normal(ks[11], (H, H), jnp.float32) * sc, 'bo': jnp.zeros((H,), jnp.float32)}
        return d
    _L0_attn_all = _L0_attn_setup()
    _L0_attn_in = {k: v for k, v in _L0_attn_all.items() if k in ('cons_vec', 'Wq', 'bq', 'Wk', 'bk', 'Wv', 'bv', 'cg_W', 'cg_b', 'am_W', 'am_b', 'ca_Win', 'ca_bin', 'ca_Wout', 'ca_bout', 'mc_Win', 'mc_bin', 'mc_Wout', 'mc_bout', 'Wo', 'bo')}
    del _L0_attn_all

    def _L0_xattn_setup():
        import jax, jax.numpy as jnp
        import numpy as np
        EMBED_DIM = 256
        NUM_HEADS = 16
        HEAD_DIM = EMBED_DIM // NUM_HEADS
        B, SQ, SK = (4, 512, 512)

        def _xavier(key, shape):
            fan_in, fan_out = (shape[1], shape[0])
            limit = float(np.sqrt(6.0 / (fan_in + fan_out)))
            return jax.random.uniform(key, shape, jnp.float32, -limit, limit)
        key = jax.random.key(seed)
        ks = jax.random.split(key, 9)
        return {'query': jax.random.normal(ks[0], (B, SQ, EMBED_DIM), jnp.float32), 'key_': jax.random.normal(ks[1], (B, SK, EMBED_DIM), jnp.float32), 'value': jax.random.normal(ks[2], (B, SK, EMBED_DIM), jnp.float32), 'distances': jax.random.uniform(ks[3], (B, SQ, SK), jnp.float32, 0.01, 10.0), 'Wq': _xavier(ks[4], (EMBED_DIM, EMBED_DIM)), 'bq': jnp.zeros((EMBED_DIM,), jnp.float32), 'Wk': _xavier(ks[5], (EMBED_DIM, EMBED_DIM)), 'bk': jnp.zeros((EMBED_DIM,), jnp.float32), 'Wv': _xavier(ks[6], (EMBED_DIM, EMBED_DIM)), 'bv': jnp.zeros((EMBED_DIM,), jnp.float32), 'Wo': _xavier(ks[7], (EMBED_DIM, EMBED_DIM)), 'bo': jnp.zeros((EMBED_DIM,), jnp.float32), 'distance_scaling': jnp.asarray(1.0, jnp.float32)}
    _L0_xattn_all = _L0_xattn_setup()
    _L0_xattn_in = {k: v for k, v in _L0_xattn_all.items() if k in ('Wq', 'bq', 'Wk', 'bk', 'Wv', 'bv', 'Wo', 'bo', 'distance_scaling')}
    del _L0_xattn_all

    def _L0_ffn_setup():
        import jax, jax.numpy as jnp
        import numpy as np
        B, S, H = (4, 512, 256)
        D = 512
        E = 8
        K = 2
        key = jax.random.key(seed)
        ks = jax.random.split(key, 8)
        w = lambda k, shape: jax.random.normal(k, shape, jnp.float32) * 0.02
        return {'hidden_states': jax.random.normal(ks[0], (B, S, H), jnp.float32), 'gate_w': w(ks[1], (H, E)), 'w_gate': w(ks[2], (E, H, D)), 'w_up': w(ks[3], (E, H, D)), 'w_down': w(ks[4], (E, D, H)), 'ws_gate': w(ks[5], (H, D)), 'ws_up': w(ks[6], (H, D)), 'ws_down': w(ks[7], (D, H))}
    _L0_ffn_all = _L0_ffn_setup()
    _L0_ffn_in = {k: v for k, v in _L0_ffn_all.items() if k in ('gate_w', 'w_gate', 'w_up', 'w_down', 'ws_gate', 'ws_up', 'ws_down')}
    del _L0_ffn_all
    return {'x': x, 'ctx_1024': ctx_1024, 'fside_BxSxS2_0': fside_BxSxS2_0, 'L0_attn_cons_vec': _L0_attn_in['cons_vec'], 'L0_attn_Wq': _L0_attn_in['Wq'], 'L0_attn_bq': _L0_attn_in['bq'], 'L0_attn_Wk': _L0_attn_in['Wk'], 'L0_attn_bk': _L0_attn_in['bk'], 'L0_attn_Wv': _L0_attn_in['Wv'], 'L0_attn_bv': _L0_attn_in['bv'], 'L0_attn_cg_W': _L0_attn_in['cg_W'], 'L0_attn_cg_b': _L0_attn_in['cg_b'], 'L0_attn_am_W': _L0_attn_in['am_W'], 'L0_attn_am_b': _L0_attn_in['am_b'], 'L0_attn_ca_Win': _L0_attn_in['ca_Win'], 'L0_attn_ca_bin': _L0_attn_in['ca_bin'], 'L0_attn_ca_Wout': _L0_attn_in['ca_Wout'], 'L0_attn_ca_bout': _L0_attn_in['ca_bout'], 'L0_attn_mc_Win': _L0_attn_in['mc_Win'], 'L0_attn_mc_bin': _L0_attn_in['mc_bin'], 'L0_attn_mc_Wout': _L0_attn_in['mc_Wout'], 'L0_attn_mc_bout': _L0_attn_in['mc_bout'], 'L0_attn_Wo': _L0_attn_in['Wo'], 'L0_attn_bo': _L0_attn_in['bo'], 'L0_xattn_Wq': _L0_xattn_in['Wq'], 'L0_xattn_bq': _L0_xattn_in['bq'], 'L0_xattn_Wk': _L0_xattn_in['Wk'], 'L0_xattn_bk': _L0_xattn_in['bk'], 'L0_xattn_Wv': _L0_xattn_in['Wv'], 'L0_xattn_bv': _L0_xattn_in['bv'], 'L0_xattn_Wo': _L0_xattn_in['Wo'], 'L0_xattn_bo': _L0_xattn_in['bo'], 'L0_xattn_distance_scaling': _L0_xattn_in['distance_scaling'], 'L0_ffn_gate_w': _L0_ffn_in['gate_w'], 'L0_ffn_w_gate': _L0_ffn_in['w_gate'], 'L0_ffn_w_up': _L0_ffn_in['w_up'], 'L0_ffn_w_down': _L0_ffn_in['w_down'], 'L0_ffn_ws_gate': _L0_ffn_in['ws_gate'], 'L0_ffn_ws_up': _L0_ffn_in['ws_up'], 'L0_ffn_ws_down': _L0_ffn_in['ws_down']}

def reference(x, ctx_1024, fside_BxSxS2_0, L0_attn_cons_vec, L0_attn_Wq, L0_attn_bq, L0_attn_Wk, L0_attn_bk, L0_attn_Wv, L0_attn_bv, L0_attn_cg_W, L0_attn_cg_b, L0_attn_am_W, L0_attn_am_b, L0_attn_ca_Win, L0_attn_ca_bin, L0_attn_ca_Wout, L0_attn_ca_bout, L0_attn_mc_Win, L0_attn_mc_bin, L0_attn_mc_Wout, L0_attn_mc_bout, L0_attn_Wo, L0_attn_bo, L0_xattn_Wq, L0_xattn_bq, L0_xattn_Wk, L0_xattn_bk, L0_xattn_Wv, L0_xattn_bv, L0_xattn_Wo, L0_xattn_bo, L0_xattn_distance_scaling, L0_ffn_gate_w, L0_ffn_w_gate, L0_ffn_w_up, L0_ffn_w_down, L0_ffn_ws_gate, L0_ffn_ws_up, L0_ffn_ws_down):
    import jax
    import jax.numpy as jnp

    def _L0_attn_ref(hidden_states, cons_vec, Wq, bq, Wk, bk, Wv, bv, cg_W, cg_b, am_W, am_b, ca_Win, ca_bin, ca_Wout, ca_bout, mc_Win, mc_bin, mc_Wout, mc_bout, Wo, bo):
        import jax, jax.numpy as jnp
        import numpy as np
        B, S, H, NH = (4, 256, 256, 16)
        HD = H // NH
        CAUSAL_HEADS = 4
        META_HEADS = NH // 4
        CAUSAL_W = 0.7
        META_W = (0.9 - 0.8) / 0.2 * 0.3

        def _mha(xq, xkv, Win, bi, Wout, bout, nh):
            b, sq, h = xq.shape
            sk = xkv.shape[1]
            hd = h // nh
            q = (xq @ Win[:, :h] + bi[:h]).reshape(b, sq, nh, hd).transpose(0, 2, 1, 3)
            k = (xkv @ Win[:, h:2 * h] + bi[h:2 * h]).reshape(b, sk, nh, hd).transpose(0, 2, 1, 3)
            v = (xkv @ Win[:, 2 * h:] + bi[2 * h:]).reshape(b, sk, nh, hd).transpose(0, 2, 1, 3)
            scores = jnp.einsum('bhqd,bhkd->bhqk', q, k) / jnp.sqrt(jnp.asarray(hd, q.dtype))
            probs = jax.nn.softmax(scores, axis=-1)
            ctx = jnp.einsum('bhqk,bhkd->bhqd', probs, v)
            return ctx.transpose(0, 2, 1, 3).reshape(b, sq, h) @ Wout + bout

        def _forward(hidden_states, cons_vec, Wq, bq, Wk, bk, Wv, bv, cg_W, cg_b, am_W, am_b, ca_Win, ca_bin, ca_Wout, ca_bout, mc_Win, mc_bin, mc_Wout, mc_bout, Wo, bo):
            b, s, h = hidden_states.shape
            q = (hidden_states @ Wq + bq).reshape(b, s, NH, HD).transpose(0, 2, 1, 3)
            k = (hidden_states @ Wk + bk).reshape(b, s, NH, HD).transpose(0, 2, 1, 3)
            v = (hidden_states @ Wv + bv).reshape(b, s, NH, HD).transpose(0, 2, 1, 3)
            scores = jnp.einsum('bhqd,bhkd->bhqk', q, k) / jnp.sqrt(jnp.asarray(HD, q.dtype))
            mod = jax.nn.sigmoid(hidden_states @ cg_W + cg_b + (cons_vec @ am_W + am_b))
            scores = scores * mod.transpose(0, 2, 1)[..., None]
            probs = jax.nn.softmax(scores, axis=-1)
            ctx = jnp.einsum('bhqk,bhkd->bhqd', probs, v).transpose(0, 2, 1, 3).reshape(b, s, h)
            causal_ctx = _mha(hidden_states, hidden_states, ca_Win, ca_bin, ca_Wout, ca_bout, CAUSAL_HEADS)
            ctx = ctx * (1.0 - CAUSAL_W) + causal_ctx * CAUSAL_W
            meta_ctx = _mha(ctx, ctx, mc_Win, mc_bin, mc_Wout, mc_bout, META_HEADS)
            ctx = ctx * (1.0 - META_W) + meta_ctx * META_W
            return ctx @ Wo + bo
        return _forward(hidden_states, cons_vec, Wq, bq, Wk, bk, Wv, bv, cg_W, cg_b, am_W, am_b, ca_Win, ca_bin, ca_Wout, ca_bout, mc_Win, mc_bin, mc_Wout, mc_bout, Wo, bo)

    def _L0_xattn_ref(query, key_, value, distances, Wq, bq, Wk, bk, Wv, bv, Wo, bo, distance_scaling):
        import jax, jax.numpy as jnp
        import numpy as np
        EMBED_DIM = 256
        NUM_HEADS = 16
        HEAD_DIM = EMBED_DIM // NUM_HEADS
        B, SQ, SK = (4, 512, 512)

        def _xavier(key, shape):
            fan_in, fan_out = (shape[1], shape[0])
            limit = float(np.sqrt(6.0 / (fan_in + fan_out)))
            return jax.random.uniform(key, shape, jnp.float32, -limit, limit)
        b, sq, e = query.shape
        sk = key_.shape[1]
        h, d = (NUM_HEADS, HEAD_DIM)
        q = (query @ Wq.T + bq) * d ** (-0.5)
        k = key_ @ Wk.T + bk
        v = value @ Wv.T + bv
        q = q.reshape(b, sq, h, d).transpose(0, 2, 1, 3)
        k = k.reshape(b, sk, h, d).transpose(0, 2, 1, 3)
        v = v.reshape(b, sk, h, d).transpose(0, 2, 1, 3)
        scores = jnp.einsum('bhqd,bhkd->bhqk', q, k)
        distance_bias = -jnp.log(distances + 1e-09) * jnp.abs(distance_scaling)
        scores = scores + distance_bias[:, None, :, :]
        attn = jax.nn.softmax(scores, axis=-1)
        out = jnp.einsum('bhqk,bhkd->bhqd', attn, v)
        out = out.transpose(0, 2, 1, 3).reshape(b, sq, e)
        return out @ Wo.T + bo

    def _L0_ffn_ref(hidden_states, gate_w, w_gate, w_up, w_down, ws_gate, ws_up, ws_down):
        import jax, jax.numpy as jnp
        import numpy as np
        B, S, H = (4, 512, 256)
        D = 512
        E = 8
        K = 2
        b, s, h = hidden_states.shape
        x = hidden_states.reshape(-1, h)
        scores = jax.nn.softmax(x @ gate_w, axis=-1)
        topk_w, topk_idx = jax.lax.top_k(scores, K)
        topk_w = topk_w / (jnp.sum(topk_w, axis=-1, keepdims=True) + 1e-20)
        onehot = jax.nn.one_hot(topk_idx, E, dtype=x.dtype)
        w_per_expert = jnp.einsum('nke,nk->ne', onehot, topk_w)
        y = jnp.zeros_like(x)
        for e in range(E):
            hid = jax.nn.silu(x @ w_gate[e]) * (x @ w_up[e])
            y = y + w_per_expert[:, e:e + 1] * (hid @ w_down[e])
        shared = jax.nn.silu(x @ ws_gate) * (x @ ws_up) @ ws_down
        return (y + shared).reshape(b, s, h)
    x = _layernorm(x + _L0_attn_ref(x, L0_attn_cons_vec, L0_attn_Wq, L0_attn_bq, L0_attn_Wk, L0_attn_bk, L0_attn_Wv, L0_attn_bv, L0_attn_cg_W, L0_attn_cg_b, L0_attn_am_W, L0_attn_am_b, L0_attn_ca_Win, L0_attn_ca_bin, L0_attn_ca_Wout, L0_attn_ca_bout, L0_attn_mc_Win, L0_attn_mc_bin, L0_attn_mc_Wout, L0_attn_mc_bout, L0_attn_Wo, L0_attn_bo), axis=-1)
    x = _layernorm(x + _L0_xattn_ref(x, ctx_1024, ctx_1024, fside_BxSxS2_0, L0_xattn_Wq, L0_xattn_bq, L0_xattn_Wk, L0_xattn_bk, L0_xattn_Wv, L0_xattn_bv, L0_xattn_Wo, L0_xattn_bo, L0_xattn_distance_scaling), axis=-1)
    x = _layernorm(x + _L0_ffn_ref(x, L0_ffn_gate_w, L0_ffn_w_gate, L0_ffn_w_up, L0_ffn_w_down, L0_ffn_ws_gate, L0_ffn_ws_up, L0_ffn_ws_down), axis=-1)
    return x

_drawn_inputs = setup_inputs


def setup_inputs(seed=0):
    import zlib

    import numpy as np

    out = dict(_drawn_inputs(seed))
    spreads = {'L0_attn_bq': (0.0, 0.8),
     'L0_attn_bk': (0.0, 2.0),
     'L0_attn_bv': (0.0, 0.8),
     'L0_attn_cg_b': (0.0, 0.8),
     'L0_attn_am_b': (0.0, 0.8),
     'L0_attn_ca_bin': (0.0, 0.8),
     'L0_attn_ca_bout': (0.0, 0.448),
     'L0_attn_mc_bin': (0.0, 0.8),
     'L0_attn_mc_bout': (0.0, 0.8),
     'L0_attn_bo': (0.0, 0.1),
     'L0_xattn_bq': (0.0, 0.34),
     'L0_xattn_bk': (0.0, 2.0),
     'L0_xattn_bv': (0.0, 0.1),
     'L0_xattn_bo': (0.0, 0.1)}
    factors = {'L0_attn_cons_vec': 8.0,
     'L0_attn_Wq': 8.0,
     'L0_attn_Wk': 8.0,
     'L0_attn_Wv': 8.0,
     'L0_attn_cg_W': 8.0,
     'L0_attn_am_W': 8.0,
     'L0_attn_ca_Win': 8.0,
     'L0_attn_ca_Wout': 8.0,
     'L0_attn_mc_Win': 8.0,
     'L0_attn_mc_Wout': 8.0,
     'L0_attn_Wo': 2.763,
     'L0_ffn_gate_w': 3.859,
     'L0_ffn_w_gate': 3.365,
     'L0_ffn_w_up': 3.34,
     'L0_ffn_w_down': 3.329,
     'L0_ffn_ws_gate': 3.033,
     'L0_ffn_ws_up': 2.991,
     'L0_ffn_ws_down': 3.03}
    for name, (base, spread) in spreads.items():
        noise = np.random.default_rng([zlib.crc32(name.encode()), seed]).standard_normal(out[name].shape)
        drawn = base * np.exp(spread * noise) if base else spread * noise
        out[name] = jnp.asarray(drawn.astype(out[name].dtype))
    for name, factor in factors.items():
        out[name] = (out[name] * factor).astype(out[name].dtype)
    return out
```

```python
from contextlib import ExitStack

import concourse.bass as bass
from concourse import mybir

F32 = mybir.dt.float32
FR = mybir.dt.float32r
U32 = mybir.dt.uint32
ALU = mybir.AluOpType
ACT = mybir.ActivationFunctionType
AX = mybir.AxisListType

P = 128
B = 4
S = 1024
H = 256
KH = H // P
TOK = B * S
CH = 512
NT = CH // P
CPB = S // CH
NCH = TOK // CH
NH = 16
HD = H // NH
GH = 4
NG = NH // GH
AH = 32
BH = 4
BHD = H // BH
KC = S // P
CAUSAL_W = 0.7
META_W = (0.9 - 0.8) / 0.2 * 0.3
S2 = 154
E2 = S2 // 2
EP = 96
LOWEST = -3e38
NE = 8
D = 512
FB = D // P
EPS = 1e-5


def mm3(pe, out, la, lb, ra, rb):
    steps = [(x, y) for k in range(len(la)) for x, y in ((la[k], ra[k]), (la[k], rb[k]), (lb[k], ra[k]))]
    for n, (x, y) in enumerate(steps):
        last = pe.matmul(out, x, y, start=(n == 0), stop=(n == len(steps) - 1))
    return last


def halves(t, *rest):
    return [t[(slice(None), k, *rest)] for k in range(KH)]


def column(v):
    return v.rearrange("(c p) -> p c", p=P)


def rows(v, n=P):
    return v.rearrange("(o n) -> o n", o=1).broadcast_to([n, v.shape[0]])


class Kit:

    def __init__(self, nc, stack, name):
        self.nc, self.stack, self.name = nc, stack, name

    def sb(self, name, shape, dt=F32):
        return self.stack.enter_context(self.nc.sbuf_tensor(f"{self.name}_{name}", shape, dt))

    def ps(self, name, shape, dt=F32):
        return self.stack.enter_context(self.nc.psum_tensor(f"{self.name}_{name}", shape, dt))

    def sem(self, name):
        return self.stack.enter_context(self.nc.semaphore(f"{self.name}_{name}"))


def identity_phase(nc, ident):
    with ExitStack() as stack:
        k = Kit(nc, stack, "id")
        ones = k.sem("ones")
        done = k.sem("done")
        block = stack.enter_context(nc.Block())

        @block.vector
        def _(dve):
            dve.memset(ident[:], 1.0).then_inc(ones, 1)

        @block.gpsimd
        def _(pool):
            pool.wait_ge(ones, 1)
            pool.affine_select(out=ident[:], in_=ident[:], compare_op=ALU.is_equal, fill=0.0, base=0,
                               pattern=[[-1, P]], channel_multiplier=1).then_inc(done, 1)
            pool.wait_ge(done, 1)


def input_projections(nc, A, scr, ident):
    with ExitStack() as stack:
        k = Kit(nc, stack, "in")
        Q0, K0, G0, CQ, CK, V0, CV = (n * H for n in range(7))
        NW = 7 * H
        raw, wa, wb = k.sb("raw", [P, KH, NW]), k.sb("wa", [P, KH, NW], FR), k.sb("wb", [P, KH, NW], FR)
        cg = k.sb("cg", [P, KH, NH])
        amr = k.sb("amr", [HD + 2, NH])
        am = k.sb("am", [HD + 2, H])
        cons = k.sb("cons", [HD + 2, 1])
        gbias = k.sb("gbias", [P, KH])
        bias = k.sb("bias", [P, 4, KH])
        vbias = k.sb("vbias", [P, 2 * H])
        xt = k.sb("xt", [P, NT, H])
        xa, xb = k.sb("xa", [P, KH, CH], FR), k.sb("xb", [P, KH, CH], FR)
        mod = k.sb("mod", [P, KH, CH])
        t = k.sb("t", [P, 4, CH])
        ab = k.sb("ab", [P, 4, 2, CH])
        v16 = k.sb("v16", [P, 2, NH, AH])
        v64 = k.sb("v64", [P, 2, H])
        psx = k.ps("psx", [P, KH, CH])
        pso = k.ps("pso", [P, 2, CH])
        psg = k.ps("psg", [P, KH])
        w_in, small_in, am_in, cons_in, x_in = (k.sem(n) for n in ("w_in", "small_in", "am_in", "cons_in", "x_in"))
        cg_done, wa_done, w_done, am_done, v_set, cons_set, g_ps, g_done = (
            k.sem(n) for n in ("cg_done", "wa_done", "w_done", "am_done", "v_set", "cons_set", "g_ps", "g_done"))
        xT_ps, xa_done, xb_done = k.sem("xT_ps"), k.sem("xa_done"), k.sem("xb_done")
        mm_done, ev_act, ev_dve = k.sem("mm_done"), k.sem("ev_act"), k.sem("ev_dve")
        a_done, b_done = k.sem("a_done"), k.sem("b_done")
        part_out = [k.sem(f"part_out{n}") for n in range(4)]
        v_out = [k.sem(f"v_out{n}") for n in range(2)]
        kinds = ["mod", "q", "mod", "q"] + ["lin"] * 6 + ["v"] * NT
        wcol = [G0, Q0, G0 + P, Q0 + P, K0, K0 + P, CQ, CQ + P, CK, CK + P]
        on_act = [x in ("mod", "lin") for x in kinds]
        nth = [sum(on_act[:n]) if on_act[n] else n - sum(on_act[:n]) for n in range(len(kinds))]
        NB = len(kinds)
        NA = sum(on_act)
        ND = NB - NA
        split = [n for n in range(NB) if kinds[n] in ("q", "lin")]
        NS = len(split)
        dest = [(scr["q"], 0), (scr["q"], 1), (scr["k"], 0), (scr["k"], 1), (scr["cq"], 0), (scr["cq"], 1),
                (scr["ck"], 0), (scr["ck"], 1)]
        x_v = A["x"].rearrange("b (c t p) h -> (b c) p t h", c=CPB, p=P)
        v_v = scr["v"].rearrange("(b g s) c -> b s g c", b=B, g=NG)
        block = stack.enter_context(nc.Block())

        @block.sync
        def _(sp):
            for src, col in ((A["L0_attn_Wq"], Q0), (A["L0_attn_Wk"], K0), (A["L0_attn_Wv"], V0)):
                sp.dma_start(raw[:, :, col:col + H], src.rearrange("(k p) n -> p k n", p=P)).then_inc(w_in, 16)
            ca = A["L0_attn_ca_Win"].rearrange("(k p) n -> p k n", p=P)
            sp.dma_start(raw[:, :, CQ:CQ + 2 * H], ca[:, :, 0:2 * H]).then_inc(w_in, 16)
            sp.dma_start(raw[:, :, CV:CV + H], ca[:, :, 2 * H:3 * H]).then_inc(w_in, 16)
            sp.dma_start(cg[:], A["L0_attn_cg_W"].rearrange("(k p) n -> p k n", p=P)).then_inc(small_in, 16)
            sp.dma_start(bias[:, 0, :], column(A["L0_attn_bq"]), allow_slow_non_contiguous=True).then_inc(small_in, 16)
            sp.dma_start(bias[:, 1, :], column(A["L0_attn_bk"]), allow_slow_non_contiguous=True).then_inc(small_in, 16)
            sp.dma_start(bias[:, 2, :], column(A["L0_attn_ca_bin"][0:H]), allow_slow_non_contiguous=True).then_inc(small_in, 16)
            sp.dma_start(bias[:, 3, :], column(A["L0_attn_ca_bin"][H:2 * H]), allow_slow_non_contiguous=True).then_inc(small_in, 16)
            sp.dma_start(vbias[:, 0:H], rows(A["L0_attn_bv"])).then_inc(small_in, 16)
            sp.dma_start(vbias[:, H:2 * H], rows(A["L0_attn_ca_bin"][2 * H:3 * H])).then_inc(small_in, 16)
            sp.dma_start(amr[0:HD, :], A["L0_attn_am_W"]).then_inc(am_in, 16)
            sp.dma_start(amr[HD:HD + 1, :], A["L0_attn_am_b"].rearrange("(o n) -> o n", o=1)).then_inc(am_in, 16)
            sp.dma_start(amr[HD + 1:HD + 2, :], A["L0_attn_cg_b"].rearrange("(o n) -> o n", o=1)).then_inc(am_in, 16)
            sp.wait_ge(cons_set, 1)
            sp.dma_start(cons[0:HD, :], A["L0_attn_cons_vec"].rearrange("(p o) -> p o", o=1), allow_slow_non_contiguous=True).then_inc(cons_in, 16)
            for n in range(4):
                sp.sem_inc(part_out[n], 16)
            for n in range(2):
                sp.sem_inc(v_out[n], 32)
            with sp.Fori(0, B) as b:
                for hf in range(CPB):
                    i = 2 * b + hf
                    for s in range(NS):
                        sp.wait_ge(b_done, 4 + NS * i + s + 1)
                        dst, j = dest[s]
                        sp.dma_start(dst[:, bass.ds(b * H + j * P, P), hf * CH:(hf + 1) * CH]
                                     .rearrange("a p n -> p a n"), ab[:, s % 4]).then_inc(part_out[s % 4], 16)
                    for tt in range(NT):
                        sp.wait_ge(ev_dve, ND * i + ND - NT + tt + 1)
                        tok = hf * CH + tt * P
                        sp.dma_start(v_v[bass.ds(b, 1), tok:tok + P].rearrange("o p g c -> p (o g) c"),
                                     v16[:, tt % 2].rearrange("p (g h) c -> p g (h c)", g=NG)).then_inc(v_out[tt % 2], 16)
                        sp.dma_start(scr["cv"][bass.ds(b * S + tok, P)], v64[:, tt % 2]).then_inc(v_out[tt % 2], 16)
            for n in range(4):
                sp.wait_ge(part_out[n], 16 * (1 + NCH * NS // 4))
            for n in range(2):
                sp.wait_ge(v_out[n], 32 * (1 + NCH * NT // 2))

        @block.gpsimd
        def _(pool):
            pool.memset(cons[:], 1.0).then_inc(cons_set, 1)
            pool.memset(v16[:], 0.0).then_inc(v_set, 1)
            pool.wait_ge(v_set, 1)
            pool.memset(v16[:, :, :, HD:HD + 1], 1.0).then_inc(v_set, 1)
            pool.sem_inc(b_done, 4)
            with pool.Fori(0, B) as b:
                for hf in range(CPB):
                    i = 2 * b + hf
                    for s in range(NS):
                        pool.wait_ge(a_done, NS * i + s + 1)
                        pool.tensor_tensor(ab[:, s % 4, 1], t[:, s % 4], ab[:, s % 4, 0], ALU.subtract).then_inc(b_done, 1)

        @block.tensor
        def _(pe):
            pe.wait_ge(cons_in, 16)
            pe.wait_ge(am_done, 1)
            for j in range(KH):
                last = pe.matmul(psg[:, j:j + 1], am[:, j * P:(j + 1) * P], cons[:], start=True, stop=True)
            last.then_inc(g_ps, 1)
            pe.wait_ge(w_done, 1)
            with pe.Fori(0, B) as b:
                for hf in range(CPB):
                    i = 2 * b + hf
                    pe.wait_ge(x_in, 16 * i + 16)
                    for kh in range(KH):
                        for tt in range(NT):
                            last = pe.transpose(psx[:, kh, tt * P:(tt + 1) * P], xt[:, tt, kh * P:(kh + 1) * P], ident[:])
                    last.then_inc(xT_ps, 1)
                    pe.wait_ge(xb_done, i + 1)
                    for n in range(NB):
                        if n >= 2:
                            if on_act[n - 2]:
                                pe.wait_ge(ev_act, NA * i + nth[n - 2] + 1)
                            else:
                                pe.wait_ge(ev_dve, ND * i + nth[n - 2] + 1)
                        if kinds[n] == "v":
                            tok = slice((n - NB + NT) * P, (n - NB + NT + 1) * P)
                            mm3(pe, pso[:, n % 2], halves(xa, tok), halves(xb, tok), halves(wa, slice(V0, V0 + 2 * H)),
                                halves(wb, slice(V0, V0 + 2 * H))).then_inc(mm_done, 1)
                        else:
                            w = slice(wcol[n], wcol[n] + P)
                            mm3(pe, pso[:, n % 2], halves(wa, w), halves(wb, w), halves(xa), halves(xb)).then_inc(mm_done, 1)

        @block.scalar
        def _(act):
            def load(i):
                act.dma_start(xt[:], x_v[bass.ds(i, 1)].rearrange("o p t h -> p (o t) h")).then_inc(x_in, 16)

            def chunk(i, more):
                act.wait_ge(xT_ps, i + 1)
                act.activation(xa[:], psx[:], ACT.Copy).then_inc(xa_done, 1)
                if more:
                    load(i + 1)
                for n in range(NB):
                    if not on_act[n]:
                        continue
                    act.wait_ge(mm_done, NB * i + n + 1)
                    if kinds[n] == "mod":
                        j = n // 2
                        act.activation(mod[:, j], pso[:, n % 2], ACT.Sigmoid, bias=gbias[:, j:j + 1]).then_inc(ev_act, 1)
                    else:
                        s = split.index(n)
                        act.wait_ge(b_done, NS * i + s + 1)
                        act.activation(t[:, s % 4], pso[:, n % 2], ACT.Identity,
                                       bias=bias[:, s // 2, s % 2:s % 2 + 1]).then_inc(ev_act, 1)

            act.wait_ge(small_in, 16 * 7)
            act.wait_ge(g_done, 1)
            load(0)
            with act.Fori(0, B - 1) as b:
                for hf in range(CPB):
                    chunk(2 * b + hf, True)
            for hf in range(CPB):
                chunk(NCH - CPB + hf, hf == 0)

        @block.vector
        def _(dve):
            dve.wait_ge(small_in, 16 * 7)
            for kh in range(KH):
                dve.tensor_copy(raw[:, kh, G0:G0 + H].rearrange("p (h d) -> p h d", h=NH),
                                cg[:, kh].unsqueeze(2).broadcast_to([P, NH, HD])).then_inc(cg_done, 1)
            dve.wait_ge(am_in, 48)
            dve.tensor_copy(am[:].rearrange("p (h d) -> p h d", h=NH),
                            amr[:].unsqueeze(2).broadcast_to([HD + 2, NH, HD])).then_inc(am_done, 1)
            dve.wait_ge(w_in, 16 * 5)
            dve.wait_ge(cg_done, KH)
            dve.tensor_copy(wa[:], raw[:]).then_inc(wa_done, 1)
            dve.wait_ge(wa_done, 1)
            dve.tensor_tensor(wb[:], raw[:], wa[:].bitcast(F32), ALU.subtract).then_inc(w_done, 1)
            dve.wait_ge(g_ps, 1)
            dve.tensor_copy(gbias[:], psg[:]).then_inc(g_done, 1)
            dve.wait_ge(v_set, 2)
            with dve.Fori(0, B) as b:
                for hf in range(CPB):
                    i = 2 * b + hf
                    dve.wait_ge(xa_done, i + 1)
                    dve.tensor_tensor(xb[:], psx[:], xa[:].bitcast(F32), ALU.subtract).then_inc(xb_done, 1)
                    for n in range(NB):
                        if kinds[n] == "mod":
                            continue
                        if kinds[n] == "q":
                            s, j = split.index(n), n // 2
                            dve.wait_ge(mm_done, NB * i + n + 1)
                            dve.wait_ge(ev_act, NA * i + nth[n - 1] + 1)
                            dve.wait_ge(b_done, NS * i + s + 1)
                            dve.scalar_tensor_tensor(out=t[:, s % 4], in0=pso[:, n % 2], scalar=bias[:, 0, j:j + 1],
                                                     in1=mod[:, j], op0=ALU.add, op1=ALU.mult).then_inc(ev_dve, 1)
                            dve.wait_ge(ev_dve, ND * i + nth[n] + 1)
                        if kinds[n] == "lin":
                            s = split.index(n)
                            dve.wait_ge(ev_act, NA * i + nth[n] + 1)
                        if kinds[n] != "v":
                            dve.wait_ge(part_out[s % 4], 16 * (NS // 4 * i + s // 4 + 1))
                            dve.tensor_copy(ab[:, s % 4, 0].bitcast(FR), t[:, s % 4]).then_inc(a_done, 1)
                            continue
                        tt = n - NB + NT
                        dve.wait_ge(mm_done, NB * i + n + 1)
                        dve.wait_ge(v_out[tt % 2], 32 * (NT // 2 * i + tt // 2 + 1))
                        dve.tensor_tensor(v16[:, tt % 2, :, 0:HD], pso[:, n % 2, 0:H].rearrange("p (h d) -> p h d", h=NH),
                                          vbias[:, 0:H].rearrange("p (h d) -> p h d", h=NH), ALU.add)
                        dve.tensor_tensor(v64[:, tt % 2], pso[:, n % 2, H:2 * H], vbias[:, H:2 * H], ALU.add).then_inc(ev_dve, 1)


def attend_narrow(nc, scr, fill):
    with ExitStack() as stack:
        k = Kit(nc, stack, "an")
        ONE, LAST = 4 * HD, 6 * HD
        MROW = LAST - 1
        NM = 2 * 2 * S // P * GH // 2
        NSTEP = CPB * KC
        qs, ks = k.sb("qs", [LAST, NG, GH, S], FR), k.sb("ks", [LAST, NG, GH, S], FR)
        vs = k.sb("vs", [P, NG, KC, GH * AH])
        probs = k.sb("probs", [P, 2, GH, CH])
        ev = k.sb("ev", [P, CPB, CH])
        m2 = k.sb("m2", [P, CPB, GH * NT, 2])
        mneg, mturn = k.sb("mneg", [P, 32]), k.sb("mturn", [P, 32])
        mrows = k.sb("mrows", [P, CPB, 32], FR)
        pst = k.ps("pst", [P, 2, 2, CH])
        psm = k.ps("psm", [P, 2, CH])
        pacc = k.ps("pacc", [P, CPB, CH])
        filled, mneg_set = k.sem("filled"), k.sem("mneg_set")
        loaded = [k.sem(f"loaded{n}") for n in range(NG)]
        mrow_in = [[k.sem(f"mrow_in{n}{h}") for h in range(CPB)] for n in range(NG)]
        m_out = [k.sem(f"m_out{h}") for h in range(CPB)]
        ev_out = [k.sem(f"ev_out{h}") for h in range(CPB)]
        mx_ready, mx_done, m_chain, m_ready, row_moved = (
            k.sem(n) for n in ("mx_ready", "mx_done", "m_chain", "m_ready", "row_moved"))
        st_ready, exp_done, pv_done = (k.sem(n) for n in ("st_ready", "exp_done", "pv_done"))
        acc_ready, acc_act, acc_dve = k.sem("acc_ready"), k.sem("acc_act"), k.sem("acc_dve")
        LOADS = 9
        PV0 = NSTEP * (NG - 1) + 2
        mx_list = [(hq, j, i, kh) for hq in range(CPB) for j in range(GH) for i in range(NT) for kh in range(2)]
        NM = len(mx_list)
        PER = NM // NSTEP
        block = stack.enter_context(nc.Block())

        @block.sync
        def _(sp):
            def load(G, slot):
                sp.wait_ge(pv_done, PV0 + NSTEP * (G - NG + 1))
                for r, (qp, kp) in enumerate(((0, 0), (0, 1), (1, 0), (1, 1))):
                    for dst, src, part in ((qs, scr["q"], qp), (ks, scr["k"], kp)):
                        sp.dma_start(dst[r * HD:(r + 1) * HD, slot].bitcast(F32),
                                     src[part, bass.ds(G * GH * HD, GH * HD)].rearrange("(j d) n -> d j n", j=GH))\
                            .then_inc(loaded[slot], 16)
                sp.dma_start(vs[:, slot], scr["v"][bass.ds(G * S, S)].rearrange("(c p) n -> p c n", p=P))\
                    .then_inc(loaded[slot], 16)

            def max_row(G, slot, uses, hq):
                sp.wait_ge(m_ready, CPB * G + hq + 1)
                turned = scr["m"][hq].rearrange("(c b r) -> b c r", b=4, r=32)
                for q in range(4):
                    sp.dma_start(turned[q], mrows[32 * q:32 * q + GH * NT, hq].bitcast(F32)).then_inc(m_out[hq], 16)
                sp.wait_ge(m_out[hq], 64 * G + 64)
                sp.dma_start(qs[MROW:LAST, slot, :, hq * CH:(hq + 1) * CH].bitcast(F32),
                             scr["m"][hq:hq + 1].rearrange("o (j n) -> o j n", j=GH)).then_inc(mrow_in[slot][hq], 16)
                sp.wait_ge(mrow_in[slot][hq], 16 * uses + 16)
                sp.sem_inc(row_moved, 1)

            def store(G, qh):
                if qh == 0:
                    sp.wait_ge(acc_act, G + 2)
                else:
                    sp.wait_ge(acc_dve, G + 2)
                sp.dma_start(scr["craw"][bass.ds(G * P, P), qh * CH:(qh + 1) * CH], ev[:, qh]).then_inc(ev_out[qh], 16)

            def group(b, g, ahead):
                G = b * NG + g
                if ahead >= 2:
                    load(G + 2, (g + 2) % NG)
                if ahead >= 1:
                    max_row(G + 1, (g + 1) % NG, b + (g + 1) // NG, 0)
                store(G, 0)
                if ahead >= 1:
                    max_row(G + 1, (g + 1) % NG, b + (g + 1) // NG, 1)
                store(G, 1)

            for qh in range(CPB):
                sp.sem_inc(ev_out[qh], 16)
            load(0, 0)
            load(1, 1)
            for hq in range(CPB):
                max_row(0, 0, 0, hq)
            with sp.Fori(0, B - 1) as b:
                for g in range(NG):
                    group(b, g, 2)
            for g in range(NG):
                group(B - 1, g, NG - 1 - g)
            for qh in range(CPB):
                sp.wait_ge(ev_out[qh], 16 + 16 * B * NG)

        @block.gpsimd
        def _(pool):
            pool.memset(qs[ONE:LAST].bitcast(F32), 0.0).then_inc(filled, 1)

        @block.tensor
        def _(pe):
            def maxima(G, slot, uses, lo, hi):
                for n in range(lo, hi):
                    hq, j, i, kh = mx_list[n]
                    if n == 0:
                        pe.wait_ge(loaded[slot], 16 * LOADS * uses + 16 * LOADS)
                    pe.wait_ge(mx_done, NM * G + n + 1)
                    q0 = (hq * NT + i) * P
                    pe.matmul(psm[:, n % 2], qs[0:MROW, slot, j, q0:q0 + P], ks[0:MROW, slot, j, kh * CH:(kh + 1) * CH],
                              start=True, stop=True).then_inc(mx_ready, 1)

            def values(G, slot, s):
                qh, kc = divmod(s, KC)
                pe.wait_ge(exp_done, 2 + 2 * NSTEP * G + 2 * s + 2)
                if kc == 0:
                    pe.wait_ge(acc_act if qh == 0 else acc_dve, G + 1)
                for j in range(GH):
                    last = pe.matmul(pacc[j * AH:(j + 1) * AH, qh], vs[:, slot, kc, j * AH:(j + 1) * AH],
                                     probs[:, s % 2, j], start=(kc == 0), stop=(kc == KC - 1))
                last.then_inc(pv_done, 1)

            def group(b, g, more):
                G = b * NG + g
                nxt = (G + 1, (g + 1) % NG, b + (g + 1) // NG)
                for s in range(NSTEP):
                    qh, kc = divmod(s, KC)
                    if kc == 0:
                        pe.wait_ge(mrow_in[g][qh], 16 * b + 16)
                    for hp in range(2):
                        pe.wait_ge(exp_done, 2 * NSTEP * G + 2 * s + hp + 1)
                        for jj in range(2):
                            j = 2 * hp + jj
                            last = pe.matmul(pst[:, hp, jj], ks[:, g, j, kc * P:(kc + 1) * P],
                                             qs[:, g, j, qh * CH:(qh + 1) * CH], start=True, stop=True)
                        last.then_inc(st_ready, 1)
                        if more:
                            maxima(*nxt, PER * s + hp, PER * s + hp + 1)
                    if s > 0:
                        values(G, g, s - 1)
                    if more:
                        maxima(*nxt, PER * s + PER // 2, PER * s + PER)
                values(G, g, NSTEP - 1)

            pe.sem_inc(pv_done, PV0)
            pe.wait_ge(filled, 2)
            maxima(0, 0, 0, 0, NM)
            with pe.Fori(0, B - 1) as b:
                for g in range(NG):
                    group(b, g, True)
            for g in range(NG):
                group(B - 1, g, g < NG - 1)

        @block.scalar
        def _(act):
            def group(b, g):
                G = b * NG + g
                for s in range(NSTEP):
                    for hp in range(2):
                        act.wait_ge(st_ready, 2 * NSTEP * G + 2 * s + hp + 1)
                        if hp == 0:
                            act.wait_ge(pv_done, PV0 + NSTEP * G + s - 1)
                        act.activation(probs[:, s % 2, 2 * hp:2 * hp + 2], pst[:, hp], ACT.Exp, scale=HD ** -0.5)\
                            .then_inc(exp_done, 1)
                    if s == KC + 1:
                        act.wait_ge(pv_done, PV0 + NSTEP * G + KC)
                        act.wait_ge(ev_out[0], 16 * G + 16)
                        act.activation(ev[:, 0], pacc[:, 0], ACT.Copy).then_inc(acc_act, 1)

            act.sem_inc(exp_done, 2)
            act.sem_inc(acc_act, 1)
            with act.Fori(0, B) as b:
                for g in range(NG):
                    group(b, g)

        @block.vector
        def _(dve):
            def maxima(G, lo, hi):
                for n in range(lo, hi):
                    hq, j, i, kh = mx_list[n]
                    dve.wait_ge(mx_ready, NM * G + n + 1)
                    dve.tensor_reduce(m2[:, hq, j * NT + i, kh:kh + 1], psm[:, n % 2], AX.X, ALU.max).then_inc(mx_done, 1)

            def finish(G, hq, first):
                dve.wait_ge(mx_done, 2 + NM * G + (hq + 1) * NM // CPB)
                dve.tensor_reduce(mneg[:, 0:GH * NT], m2[:, hq], AX.X, ALU.max, negate=True).then_inc(m_chain, 1)
                dve.wait_ge(m_chain, 2 * (CPB * G + hq) + 1)
                dve.transpose(mturn[:], mneg[:]).then_inc(m_chain, 1)
                dve.wait_ge(m_chain, 2 * (CPB * G + hq) + 2)
                if not first:
                    dve.wait_ge(row_moved, CPB * (G - 1) + hq + 1)
                dve.tensor_copy(mrows[:, hq], mturn[:]).then_inc(m_ready, 1)

            def group(b, g, more):
                G = b * NG + g
                if more:
                    for hq in range(CPB):
                        maxima(G + 1, hq * NM // CPB, (hq + 1) * NM // CPB)
                        finish(G + 1, hq, False)
                dve.wait_ge(pv_done, PV0 + NSTEP * G + NSTEP)
                dve.wait_ge(ev_out[1], 16 * G + 16)
                dve.tensor_copy(ev[:, 1], pacc[:, 1]).then_inc(acc_dve, 1)

            dve.sem_inc(mx_done, 2)
            dve.sem_inc(acc_dve, 1)
            dve.memset(ks[ONE:LAST].bitcast(F32), 1.0).then_inc(filled, 1)
            dve.memset(mneg[:], 0.0).then_inc(mneg_set, 1)
            dve.wait_ge(mneg_set, 1)
            for hq in range(CPB):
                maxima(0, hq * NM // CPB, (hq + 1) * NM // CPB)
                finish(0, hq, True)
            with dve.Fori(0, B - 1) as b:
                for g in range(NG):
                    group(b, g, True)
            for g in range(NG):
                group(B - 1, g, g < NG - 1)


def attend_wide(nc, src, name):
    with ExitStack() as stack:
        k = Kit(nc, stack, name)
        HP = 2
        NP = BH // HP
        NSTEP = CPB * KC
        MROW = P - 1
        ONES = 32
        PV0 = NSTEP * (NP - 1) + 2
        LOADS = 7
        qs, ks = k.sb("qs", [P, NP, 2, HP, S], FR), k.sb("ks", [P, NP, 2, HP, S], FR)
        vs = k.sb("vs", [P, NP, KC, HP * BHD])
        ones = k.sb("ones", [P, ONES])
        probs = k.sb("probs", [P, 2, HP, CH])
        ev, evd = k.sb("ev", [P, CPB, CH]), k.sb("evd", [HP * ONES, CPB, CH])
        m2 = k.sb("m2", [P, CPB, HP * NT, 2])
        mneg, mturn = k.sb("mneg", [P, 32]), k.sb("mturn", [P, 32])
        mrows = k.sb("mrows", [P, CPB, 32], FR)
        pst = k.ps("pst", [P, 2, HP, CH])
        psm = k.ps("psm", [P, 2, CH])
        pacc = k.ps("pacc", [P, CH])
        pden = k.ps("pden", [P, CH])
        filled, mneg_set = k.sem("filled"), k.sem("mneg_set")
        loaded = [k.sem(f"loaded{n}") for n in range(NP)]
        mrow_in = [[k.sem(f"mrow_in{n}{h}") for h in range(CPB)] for n in range(NP)]
        m_out = [k.sem(f"m_out{h}") for h in range(CPB)]
        ev_out = [k.sem(f"ev_out{h}") for h in range(CPB)]
        mx_ready, mx_done, m_chain, m_ready, row_moved = (
            k.sem(n) for n in ("mx_ready", "mx_done", "m_chain", "m_ready", "row_moved"))
        st_ready, exp_done, pv_done, acc_out, den_out = (
            k.sem(n) for n in ("st_ready", "exp_done", "pv_done", "acc_out", "den_out"))
        mx_list = [(hq, j, i, kh) for hq in range(CPB) for j in range(HP) for i in range(NT) for kh in range(2)]
        NM = len(mx_list)
        HALF = NM // CPB
        FROM = 6
        upto = [0 if s < FROM else -(-(s - FROM + 1) * NM // (NSTEP - FROM)) for s in range(NSTEP)]
        block = stack.enter_context(nc.Block())

        @block.sync
        def _(sp):
            def load(G, slot):
                sp.wait_ge(pv_done, PV0 + NSTEP * (G - NP + 1))
                for dst, src_, n, r, part in ((qs, "q", 0, 0, 0), (ks, "k", 0, 0, 0), (qs, "q", 0, 1, 0), (ks, "k", 0, 1, 1),
                                              (qs, "q", 1, 0, 1), (ks, "k", 1, 0, 0)):
                    sp.dma_start(dst[r * BHD:(r + 1) * BHD, slot, n].bitcast(F32),
                                 src[src_][part, bass.ds(G * P, P)].rearrange("(j d) n -> d j n", j=HP))\
                        .then_inc(loaded[slot], 16)

            def load_v(b, slot):
                sp.dma_start(vs[:, slot], src["v"][bass.ds(b * S, S), slot * P:(slot + 1) * P]
                             .rearrange("(c p) n -> p c n", p=P)).then_inc(loaded[slot], 16)

            def max_row(G, slot, uses, hq):
                sp.wait_ge(m_ready, CPB * G + hq + 1)
                turned = src["m"][hq].rearrange("(c b r) -> b c r", b=4, r=32)
                for q in range(4):
                    sp.dma_start(turned[q], mrows[32 * q:32 * q + HP * NT, hq].bitcast(F32)).then_inc(m_out[hq], 16)
                sp.wait_ge(m_out[hq], 64 * G + 64)
                sp.dma_start(qs[MROW:P, slot, 1, :, hq * CH:(hq + 1) * CH].bitcast(F32),
                             src["m"][hq:hq + 1].rearrange("o (j n) -> o j n", j=HP)).then_inc(mrow_in[slot][hq], 16)
                sp.wait_ge(mrow_in[slot][hq], 16 * uses + 16)
                sp.sem_inc(row_moved, 1)

            def store(G, qh):
                sp.wait_ge(acc_out, CPB * G + qh + 2)
                sp.wait_ge(den_out, CPB * G + qh + 2)
                sp.dma_start(src["out"][bass.ds(G * P, P), qh * CH:(qh + 1) * CH], ev[:, qh]).then_inc(ev_out[qh], 16)
                for j in range(HP):
                    sp.dma_start(src["den"][bass.ds(G * HP + j, 1), qh * CH:(qh + 1) * CH],
                                 evd[j * ONES:j * ONES + 1, qh]).then_inc(ev_out[qh], 16)

            def group(b, g, more):
                G = b * NP + g
                if more:
                    load(G + 1, (g + 1) % NP)
                    load_v(b + (g + 1) // NP, (g + 1) % NP)
                store(G, 0)
                if more:
                    max_row(G + 1, (g + 1) % NP, b + (g + 1) // NP, 0)
                store(G, 1)
                if more:
                    max_row(G + 1, (g + 1) % NP, b + (g + 1) // NP, 1)

            for qh in range(CPB):
                sp.sem_inc(ev_out[qh], 48)
            load(0, 0)
            load_v(0, 0)
            for hq in range(CPB):
                max_row(0, 0, 0, hq)
            with sp.Fori(0, B - 1) as b:
                for g in range(NP):
                    group(b, g, True)
            for g in range(NP):
                group(B - 1, g, g < NP - 1)
            for qh in range(CPB):
                sp.wait_ge(ev_out[qh], 48 + 48 * B * NP)

        @block.gpsimd
        def _(pool):
            pool.memset(qs[BHD:P, :, 1].bitcast(F32), 0.0).then_inc(filled, 1)

        @block.tensor
        def _(pe):
            def maxima(G, slot, uses, lo, hi):
                for n in range(lo, hi):
                    hq, j, i, kh = mx_list[n]
                    if n == 0:
                        pe.wait_ge(loaded[slot], 16 * LOADS * uses + 16 * LOADS)
                    pe.wait_ge(mx_done, NM * G + n + 1)
                    q0 = (hq * NT + i) * P
                    pe.matmul(psm[:, n % 2], qs[:, slot, 0, j, q0:q0 + P], ks[:, slot, 0, j, kh * CH:(kh + 1) * CH],
                              start=True, stop=True).then_inc(mx_ready, 1)

            def values(G, slot, s):
                qh, kc = divmod(s, KC)
                pe.wait_ge(exp_done, 2 + NSTEP * G + s + 1)
                if kc == 0:
                    pe.wait_ge(acc_out, CPB * G + qh + 1)
                    pe.wait_ge(den_out, CPB * G + qh + 1)
                for j in range(HP):
                    pe.matmul(pacc[j * BHD:(j + 1) * BHD], vs[:, slot, kc, j * BHD:(j + 1) * BHD], probs[:, s % 2, j],
                              start=(kc == 0), stop=(kc == KC - 1))
                for j in range(HP):
                    last = pe.matmul(pden[j * ONES:(j + 1) * ONES], ones[:], probs[:, s % 2, j],
                                     start=(kc == 0), stop=(kc == KC - 1))
                last.then_inc(pv_done, 1)

            def group(b, g, more):
                G = b * NP + g
                nxt = (G + 1, (g + 1) % NP, b + (g + 1) // NP)
                for s in range(NSTEP):
                    qh, kc = divmod(s, KC)
                    if kc == 0:
                        pe.wait_ge(mrow_in[g][qh], 16 * b + 16)
                    pe.wait_ge(exp_done, NSTEP * G + s + 1)
                    for j in range(HP):
                        for n in range(2):
                            last = pe.matmul(pst[:, s % 2, j], ks[:, g, n, j, kc * P:(kc + 1) * P],
                                             qs[:, g, n, j, qh * CH:(qh + 1) * CH], start=(n == 0), stop=(n == 1))
                    last.then_inc(st_ready, 1)
                    lo, hi = (upto[s - 1] if s else 0), upto[s]
                    if more:
                        maxima(*nxt, lo, (lo + hi) // 2)
                    if s > 0:
                        values(G, g, s - 1)
                    if more:
                        maxima(*nxt, (lo + hi) // 2, hi)
                values(G, g, NSTEP - 1)

            pe.sem_inc(pv_done, PV0)
            pe.wait_ge(filled, 3)
            maxima(0, 0, 0, 0, NM)
            with pe.Fori(0, B - 1) as b:
                for g in range(NP):
                    group(b, g, True)
            for g in range(NP):
                group(B - 1, g, g < NP - 1)

        @block.scalar
        def _(act):
            def copy_out(G, qh):
                act.wait_ge(pv_done, PV0 + NSTEP * G + KC * (qh + 1))
                act.wait_ge(ev_out[qh], 48 * G + 48)
                act.activation(ev[:, qh], pacc[:], ACT.Copy).then_inc(acc_out, 1)

            act.sem_inc(exp_done, 2)
            act.sem_inc(acc_out, 1)
            with act.Fori(0, B) as b:
                for g in range(NP):
                    G = b * NP + g
                    for s in range(NSTEP):
                        act.wait_ge(st_ready, NSTEP * G + s + 1)
                        act.wait_ge(pv_done, PV0 + NSTEP * G + s - 1)
                        act.activation(probs[:, s % 2], pst[:, s % 2], ACT.Exp, scale=BHD ** -0.5).then_inc(exp_done, 1)
                        if s == KC:
                            copy_out(G, 0)
                    copy_out(G, 1)

        @block.vector
        def _(dve):
            def maxima(G, lo, hi):
                for n in range(lo, hi):
                    hq, j, i, kh = mx_list[n]
                    dve.wait_ge(mx_ready, NM * G + n + 1)
                    dve.tensor_reduce(m2[:, hq, j * NT + i, kh:kh + 1], psm[:, n % 2], AX.X, ALU.max).then_inc(mx_done, 1)
                    if n % HALF == HALF - 1:
                        finish(G, hq)

            def finish(G, hq):
                dve.wait_ge(mx_done, 2 + NM * G + (hq + 1) * HALF)
                dve.tensor_reduce(mneg[:, 0:HP * NT], m2[:, hq], AX.X, ALU.max, negate=True).then_inc(m_chain, 1)
                dve.wait_ge(m_chain, 2 * (CPB * G + hq) + 1)
                dve.transpose(mturn[:], mneg[:]).then_inc(m_chain, 1)
                dve.wait_ge(m_chain, 2 * (CPB * G + hq) + 2)
                if not (isinstance(G, int) and G == 0):
                    dve.wait_ge(row_moved, CPB * (G - 1) + hq + 1)
                dve.tensor_copy(mrows[:, hq], mturn[:]).then_inc(m_ready, 1)

            def copy_out(G, qh):
                dve.wait_ge(pv_done, PV0 + NSTEP * G + KC * (qh + 1))
                dve.wait_ge(ev_out[qh], 48 * G + 48)
                dve.tensor_copy(evd[:, qh], pden[0:HP * ONES]).then_inc(den_out, 1)

            def group(b, g, more):
                G = b * NP + g
                for s in range(NSTEP):
                    if s == KC:
                        copy_out(G, 0)
                    if more:
                        maxima(G + 1, upto[s - 1] if s else 0, upto[s])
                copy_out(G, 1)

            dve.sem_inc(mx_done, 2)
            dve.sem_inc(den_out, 1)
            dve.memset(ks[BHD:P, :, 1].bitcast(F32), 1.0).then_inc(filled, 1)
            dve.memset(ones[:], 1.0).then_inc(filled, 1)
            dve.memset(mneg[:], 0.0).then_inc(mneg_set, 1)
            dve.wait_ge(mneg_set, 1)
            maxima(0, 0, NM)
            with dve.Fori(0, B - 1) as b:
                for g in range(NP):
                    group(b, g, True)
            for g in range(NP):
                group(B - 1, g, g < NP - 1)


def selector_steps(pool, sel, blocks, made):
    for n, (row0, width, col0) in enumerate(blocks):
        view = sel[0:32, n]
        pool.affine_select(out=view, in_=view, compare_op=ALU.is_ge, fill=0.0, base=col0 + width * row0,
                           pattern=[[1, P]], channel_multiplier=-width).then_inc(made, 1)
        pool.wait_ge(made, 2 * n + 2)
        pool.affine_select(out=view, in_=view, compare_op=ALU.is_ge, fill=0.0, base=width - 1 - col0 - width * row0,
                           pattern=[[-1, P]], channel_multiplier=width).then_inc(made, 1)
        pool.wait_ge(made, 2 * n + 3)


def join_attention(nc, A, scr):
    with ExitStack() as stack:
        k = Kit(nc, stack, "jo")
        NR = NH + BH
        raw = k.sb("raw", [P, KH, 4 * H])
        wa, wb = k.sb("wa", [P, KH, 4 * H], FR), k.sb("wb", [P, KH, 4 * H], FR)
        W0, Q0, K0, V0 = 0, H, 2 * H, 3 * H
        boraw, bo = k.sb("boraw", [P, KH]), k.sb("bo", [P, KH])
        bias = k.sb("bias", [P, 2, KH])
        vbias = k.sb("vbias", [P, H])
        self32, sel = k.sb("self32", [32, 4, P]), k.sb("sel", [P, 4, P], FR)
        den, rden = k.sb("den", [NR, 2, CH]), k.sb("rden", [NR, 2, CH])
        rsplit = k.sb("rsplit", [P, CH], FR)
        r16, c64 = k.sb("r16", [P, 2, KH, CH]), k.sb("c64", [P, 2, KH, CH])
        rn, cn = k.sb("rn", [P, 2, KH, CH]), k.sb("cn", [P, 2, KH, CH])
        cna, cnb = k.sb("cna", [P, KH, CH], FR), k.sb("cnb", [P, KH, CH], FR)
        t1 = k.sb("t1", [P, KH, CH])
        comb = k.sb("comb", [P, 2, KH, CH])
        coa, cob = k.sb("coa", [P, 2, KH, CH], FR), k.sb("cob", [P, 2, KH, CH], FR)
        t = k.sb("t", [P, 4, CH])
        ab = k.sb("ab", [P, 4, 2, CH])
        v64 = k.sb("v64", [P, 2, H])
        pb, pw, po = k.ps("pb", [P, 2, CH]), k.ps("pw", [P, KH, CH]), k.ps("po", [P, 2, CH])
        w_in, small_in = k.sem("w_in"), k.sem("small_in")
        raw_in = [k.sem(f"raw_in{n}") for n in range(2)]
        wa_done, w_done, bo_done, sel_set, sel_made, sel_done, rs_zero = (k.sem(n) for n in (
            "wa_done", "w_done", "bo_done", "sel_set", "sel_made", "sel_done", "rs_zero"))
        r_chain, r_ready, pb_ready, pb_done = (k.sem(n) for n in ("r_chain", "r_ready", "pb_ready", "pb_done"))
        cna_done, cnb_done, pw_ready, t1_done, comb_done, coa_done, cob_done = (k.sem(n) for n in (
            "cna_done", "cnb_done", "pw_ready", "t1_done", "comb_done", "coa_done", "cob_done"))
        po_ready, t_done, a_done, b_done, v_done = (k.sem(n) for n in ("po_ready", "t_done", "a_done", "b_done", "v_done"))
        comb_out = [k.sem(f"comb_out{n}") for n in range(2)]
        part_out = [k.sem(f"part_out{n}") for n in range(4)]
        v_out = [k.sem(f"v_out{n}") for n in range(2)]
        RAWS = NH + 3
        craw_v = scr["craw"].rearrange("(x r) n -> x r n", r=AH)
        dest = [(scr["mq"], 0), (scr["mq"], 1), (scr["mk"], 0), (scr["mk"], 1)]
        block = stack.enter_context(nc.Block())

        @block.sync
        def _(sp):
            mc = A["L0_attn_mc_Win"].rearrange("(k p) n -> p k n", p=P)
            sp.dma_start(raw[:, :, W0:W0 + H], A["L0_attn_ca_Wout"].rearrange("(k p) n -> p k n", p=P)).then_inc(w_in, 16)
            sp.dma_start(raw[:, :, Q0:Q0 + 3 * H], mc).then_inc(w_in, 16)
            sp.dma_start(boraw[:], column(A["L0_attn_ca_bout"]), allow_slow_non_contiguous=True).then_inc(small_in, 16)
            sp.dma_start(bias[:, 0], column(A["L0_attn_mc_bin"][0:H]), allow_slow_non_contiguous=True).then_inc(small_in, 16)
            sp.dma_start(bias[:, 1], column(A["L0_attn_mc_bin"][H:2 * H]), allow_slow_non_contiguous=True).then_inc(small_in, 16)
            sp.dma_start(vbias[:], rows(A["L0_attn_mc_bin"][2 * H:3 * H])).then_inc(small_in, 16)
            for n in range(4):
                sp.sem_inc(part_out[n], 16)
            for n in range(2):
                sp.sem_inc(v_out[n], 16)
                sp.sem_inc(comb_out[n], 16)

            def load(b, hf):
                sp.wait_ge(pb_done, 4 * (2 * b + hf) + 4)
                cols = slice(hf * CH, (hf + 1) * CH)
                for h in range(NH):
                    p0 = h % 8 * HD
                    sp.dma_start(r16[p0:p0 + HD, hf, h // 8], scr["craw"][bass.ds(b * NH * AH + h * AH, HD), cols])\
                        .then_inc(raw_in[hf], 16)
                sp.dma_start(den[0:NH, hf], craw_v[bass.ds(b * NH, NH), HD, cols]).then_inc(raw_in[hf], 16)
                sp.dma_start(den[NH:NR, hf], scr["cden"][bass.ds(b * BH, BH), cols]).then_inc(raw_in[hf], 16)
                sp.dma_start(c64[:, hf], scr["cout"][bass.ds(b * H, H), cols].rearrange("(c p) n -> p c n", p=P))\
                    .then_inc(raw_in[hf], 16)

            def batch(b, more):
                for hf in range(CPB):
                    i = 2 * b + hf
                    cols = slice(hf * CH, (hf + 1) * CH)
                    sp.wait_ge(comb_done, KH * i + KH)
                    sp.dma_start(scr["comb"][bass.ds(b * H, H), cols].rearrange("(c p) n -> p c n", p=P), comb[:, hf])\
                        .then_inc(comb_out[hf], 16)
                if more:
                    for hf in range(CPB):
                        load(b + 1, hf)
                for hf in range(CPB):
                    i = 2 * b + hf
                    cols = slice(hf * CH, (hf + 1) * CH)
                    for s in range(4):
                        sp.wait_ge(b_done, 4 + 4 * i + s + 1)
                        dst, j = dest[s]
                        sp.dma_start(dst[:, bass.ds(b * H + j * P, P), cols].rearrange("a p n -> p a n"), ab[:, s])\
                            .then_inc(part_out[s], 16)
                    for tt in range(NT):
                        sp.wait_ge(v_done, NT * i + tt + 1)
                        sp.dma_start(scr["mv"][bass.ds(b * S + hf * CH + tt * P, P)], v64[:, tt % 2]).then_inc(v_out[tt % 2], 16)

            for hf in range(CPB):
                load(0, hf)
            with sp.Fori(0, B - 1) as b:
                batch(b, True)
            batch(B - 1, False)
            for n in range(4):
                sp.wait_ge(part_out[n], 16 + 16 * NCH)
            for n in range(2):
                sp.wait_ge(v_out[n], 16 + 16 * NCH * NT // 2)
                sp.wait_ge(comb_out[n], 16 + 16 * B)

        @block.gpsimd
        def _(pool):
            pool.memset(self32[:], 1.0).then_inc(sel_made, 1)
            pool.wait_ge(sel_made, 1)
            selector_steps(pool, self32, ((0, HD, 0), (0, HD, P), (NH, BHD, 0), (NH, BHD, P)), sel_made)
            pool.sem_inc(b_done, 4)
            with pool.Fori(0, B) as b:
                for hf in range(CPB):
                    i = 2 * b + hf
                    for c in range(KH):
                        pool.wait_ge(cna_done, KH * i + c + 1)
                        pool.tensor_tensor(cnb[:, c], cn[:, hf, c], cna[:, c].bitcast(F32), ALU.subtract).then_inc(cnb_done, 1)
                    pool.wait_ge(comb_out[hf], 16 * b + 16)
                    for c in range(KH):
                        pool.wait_ge(t1_done, KH * i + c + 1)
                        pool.wait_ge(pb_done, 8 + 4 * i + KH + c + 1)
                        pool.tensor_tensor(comb[:, hf, c], t1[:, c], rn[:, hf, c], ALU.add).then_inc(comb_done, 1)
                    for c in range(KH):
                        pool.wait_ge(coa_done, KH * i + c + 1)
                        pool.tensor_tensor(cob[:, hf, c], comb[:, hf, c], coa[:, hf, c].bitcast(F32), ALU.subtract)\
                            .then_inc(cob_done, 1)
                for hf in range(CPB):
                    i = 2 * b + hf
                    for s in range(4):
                        pool.wait_ge(a_done, 4 * i + s + 1)
                        pool.tensor_tensor(ab[:, s, 1], t[:, s], ab[:, s, 0], ALU.subtract).then_inc(b_done, 1)

        @block.tensor
        def _(pe):
            pe.wait_ge(w_done, 1)
            pe.wait_ge(sel_done, 2)
            with pe.Fori(0, B) as b:
                for hf in range(CPB):
                    i = 2 * b + hf
                    pe.wait_ge(r_ready, i + 1)
                    for m, n in enumerate((2, 3, 0, 1)):
                        pe.wait_ge(pb_done, 8 + 4 * i + m - 1)
                        pe.matmul(pb[:, m % 2], sel[:, n], rsplit[:], start=True, stop=True).then_inc(pb_ready, 1)
                    pe.wait_ge(cnb_done, KH * i + KH)
                    for c in range(KH):
                        w = slice(W0 + c * P, W0 + (c + 1) * P)
                        mm3(pe, pw[:, c], halves(wa, w), halves(wb, w), halves(cna), halves(cnb)).then_inc(pw_ready, 1)
                for hf in range(CPB):
                    i = 2 * b + hf
                    pe.wait_ge(cob_done, KH * i + KH)
                    xa, xb = [coa[:, hf, c] for c in range(KH)], [cob[:, hf, c] for c in range(KH)]
                    for n in range(4 + NT):
                        if 2 <= n < 6:
                            pe.wait_ge(t_done, 4 * i + n - 1)
                        elif n >= 6:
                            pe.wait_ge(v_done, NT * i + n - 5)
                        if n < 4:
                            w = slice(Q0 + n * P, Q0 + (n + 1) * P)
                            mm3(pe, po[:, n % 2], halves(wa, w), halves(wb, w), xa, xb).then_inc(po_ready, 1)
                        else:
                            tok = slice((n - 4) * P, (n - 3) * P)
                            mm3(pe, po[:, n % 2, 0:H], [x[:, tok] for x in xa], [x[:, tok] for x in xb],
                                halves(wa, slice(V0, V0 + H)), halves(wb, slice(V0, V0 + H))).then_inc(po_ready, 1)
                    pe.wait_ge(v_done, NT * i + NT)

        @block.scalar
        def _(act):
            act.wait_ge(small_in, 64)
            act.wait_ge(bo_done, 1)
            with act.Fori(0, B) as b:
                for hf in range(CPB):
                    i = 2 * b + hf
                    for c in range(KH):
                        act.wait_ge(pb_done, 8 + 4 * i + c + 1)
                        act.activation(cna[:, c], cn[:, hf, c], ACT.Copy).then_inc(cna_done, 1)
                    for c in range(KH):
                        act.wait_ge(pw_ready, KH * i + c + 1)
                        act.activation(t1[:, c], pw[:, c], ACT.Identity, bias=bo[:, c:c + 1], scale=CAUSAL_W).then_inc(t1_done, 1)
                for hf in range(CPB):
                    i = 2 * b + hf
                    for s in range(4):
                        act.wait_ge(po_ready, (4 + NT) * i + s + 1)
                        act.wait_ge(b_done, 4 * i + s + 1)
                        act.activation(t[:, s], po[:, s % 2], ACT.Identity, bias=bias[:, s // 2, s % 2:s % 2 + 1])\
                            .then_inc(t_done, 1)

        @block.vector
        def _(dve):
            dve.sem_inc(pb_done, 8)
            dve.memset(rsplit[:].bitcast(F32), 0.0).then_inc(rs_zero, 1)
            dve.memset(sel[:].bitcast(F32), 0.0).then_inc(sel_set, 1)
            dve.wait_ge(w_in, 32)
            dve.tensor_copy(wa[:], raw[:]).then_inc(wa_done, 1)
            dve.wait_ge(wa_done, 1)
            dve.tensor_tensor(wb[:], raw[:], wa[:].bitcast(F32), ALU.subtract).then_inc(w_done, 1)
            dve.wait_ge(small_in, 64)
            dve.tensor_scalar(bo[:], boraw[:], CAUSAL_W, None, ALU.mult).then_inc(bo_done, 1)
            dve.wait_ge(sel_made, 9)
            dve.wait_ge(sel_set, 1)
            dve.tensor_copy(sel[0:32], self32[:]).then_inc(sel_done, 1)
            dve.tensor_copy(sel[32:64], self32[:]).then_inc(sel_done, 1)
            dve.wait_ge(rs_zero, 1)
            with dve.Fori(0, B) as b:
                for hf in range(CPB):
                    i = 2 * b + hf
                    dve.wait_ge(raw_in[hf], 16 * RAWS * (b + 1))
                    dve.reciprocal(rden[:, hf], den[:, hf]).then_inc(r_chain, 1)
                    dve.wait_ge(r_chain, 2 * i + 1)
                    dve.tensor_copy(rsplit[0:NR], rden[:, hf]).then_inc(r_chain, 1)
                    dve.wait_ge(r_chain, 2 * i + 2)
                    dve.tensor_tensor(rsplit[32:32 + NR], rden[:, hf], rsplit[0:NR].bitcast(F32), ALU.subtract)\
                        .then_inc(r_ready, 1)
                    for m, n in enumerate((2, 3, 0, 1)):
                        dve.wait_ge(pb_ready, 4 * i + m + 1)
                        if n >= 2:
                            dve.tensor_tensor(cn[:, hf, n - 2], c64[:, hf, n - 2], pb[:, m % 2], ALU.mult).then_inc(pb_done, 1)
                        else:
                            dve.scalar_tensor_tensor(out=rn[:, hf, n], in0=r16[:, hf, n], scalar=1.0 - CAUSAL_W,
                                                     in1=pb[:, m % 2], op0=ALU.mult, op1=ALU.mult).then_inc(pb_done, 1)
                    for c in range(KH):
                        dve.wait_ge(comb_done, KH * i + c + 1)
                        dve.tensor_copy(coa[:, hf, c], comb[:, hf, c]).then_inc(coa_done, 1)
                for hf in range(CPB):
                    i = 2 * b + hf
                    for s in range(4):
                        dve.wait_ge(t_done, 4 * i + s + 1)
                        dve.wait_ge(part_out[s], 16 * i + 16)
                        dve.tensor_copy(ab[:, s, 0].bitcast(FR), t[:, s]).then_inc(a_done, 1)
                    for tt in range(NT):
                        dve.wait_ge(po_ready, (4 + NT) * i + 4 + tt + 1)
                        dve.wait_ge(v_out[tt % 2], 16 * (NT // 2 * i + tt // 2 + 1))
                        dve.tensor_tensor(v64[:, tt % 2], po[:, tt % 2, 0:H], vbias[:], ALU.add).then_inc(v_done, 1)


def project_and_norm(nc, A, scr, ident, cross, keep=None):
    with ExitStack() as stack:
        k = Kit(nc, stack, "pc" if cross else "ps")
        NR, width = (NH, HD) if cross else (BH, BHD)
        NW = H if cross else 3 * H
        Y0, W0, Q0 = 0, H, 2 * H
        raw = k.sb("raw", [P, KH, NW])
        wa, wb = k.sb("wa", [P, KH, NW], FR), k.sb("wb", [P, KH, NW], FR)
        small_raw, small = k.sb("small_raw", [P, 2, KH]), k.sb("small", [P, 2, KH])
        obias = k.sb("obias", [P, H])
        eps = k.sb("eps", [P, 1])
        self32, sel = k.sb("self32", [32, KH, P]), k.sb("sel", [P, KH, P], FR)
        den, rden = k.sb("den", [NR, 2, CH]), k.sb("rden", [NR, 2, CH])
        rsplit = k.sb("rsplit", [P, CH], FR)
        c64 = k.sb("c64", [P, 2, KH, CH])
        xt = k.sb("xt", [P, 2, NT, H])
        cn = k.sb("cn", [P, KH, CH])
        cna, cnb = k.sb("cna", [P, 2, KH, CH], FR), k.sb("cnb", [P, 2, KH, CH], FR)
        res = k.sb("res", [P, 2, H])
        stats, mv, rstd = k.sb("stats", [P, 2, 6]), k.sb("mv", [P, 2, 2]), k.sb("rstd", [P, 2, 2])
        x1 = k.sb("x1", [P, 2, NT, H])
        if not cross:
            comb = k.sb("comb", [P, 2, KH, CH])
            t1, z = k.sb("t1", [P, KH, CH]), k.sb("z", [P, KH, CH])
            za, zb = k.sb("za", [P, 2, KH, CH], FR), k.sb("zb", [P, 2, KH, CH], FR)
            xa, xb = k.sb("xa", [P, KH, CH], FR), k.sb("xb", [P, KH, CH], FR)
            t, ab = k.sb("t", [P, KH, CH]), k.sb("ab", [P, KH, 2, CH])
        pb, pw, po, px = (k.ps("pb", [P, 2, CH]), k.ps("pw", [P, KH, CH]), k.ps("po", [P, 2, CH]), k.ps("px", [P, KH, CH]))
        w_in, small_in = k.sem("w_in"), k.sem("small_in")
        raw_in = [k.sem(f"raw_in{n}") for n in range(2)]
        names = ("wa_done", "w_done", "small_done", "sel_set", "sel_made", "sel_done", "rs_zero", "eps_set",
                 "r_chain", "r_ready", "pb_ready", "pb_done", "cna_done", "cnb_done", "pw_ready", "t1_done", "z_done",
                 "za_done", "zb_done", "xo_done", "y_ready", "y_done", "n_chain", "stats_seen", "var_done", "std_done", "x1_done",
                 "xT_ready", "xa_done", "xb_done", "po_ready", "t_done", "a_done", "b_done")
        (wa_done, w_done, small_done, sel_set, sel_made, sel_done, rs_zero, eps_set, r_chain, r_ready, pb_ready, pb_done,
         cna_done, cnb_done, pw_ready, t1_done, z_done, za_done, zb_done, xo_done, y_ready, y_done, n_chain, stats_seen, var_done,
         std_done, x1_done, xT_ready, xa_done, xb_done, po_ready, t_done, a_done, b_done) = (k.sem(n) for n in names)
        x1_out = [k.sem(f"x1_out{n}") for n in range(2)]
        part_out = [k.sem(f"part_out{n}") for n in range(2)]
        RAWS = (NH + 2) if cross else 4
        wname = "L0_xattn_Wo" if cross else "L0_attn_Wo"
        residual = scr["x1"] if cross else A["x"].rearrange("b s h -> (b s) h")
        block = stack.enter_context(nc.Block())

        @block.sync
        def _(sp):
            sp.dma_start(raw[:, :, Y0:Y0 + H], A[wname].rearrange("(k p) n -> p k n", p=P)).then_inc(w_in, 16)
            sp.dma_start(obias[:], rows(A["L0_xattn_bo" if cross else "L0_attn_bo"])).then_inc(small_in, 16)
            if not cross:
                sp.dma_start(raw[:, :, W0:W0 + H], A["L0_attn_mc_Wout"].rearrange("(k p) n -> p k n", p=P)).then_inc(w_in, 16)
                sp.dma_start(raw[:, :, Q0:Q0 + H], A["L0_xattn_Wq"].rearrange("(k p) n -> p k n", p=P)).then_inc(w_in, 16)
                sp.dma_start(small_raw[:, 0], column(A["L0_attn_mc_bout"]), allow_slow_non_contiguous=True).then_inc(small_in, 16)
                sp.dma_start(small_raw[:, 1], column(A["L0_xattn_bq"]), allow_slow_non_contiguous=True).then_inc(small_in, 16)
            for n in range(2):
                sp.sem_inc(x1_out[n], 16)
                sp.sem_inc(part_out[n], 16)

            def load(b, hf):
                sp.wait_ge(x1_done, NT * (2 * b + hf) + NT)
                cols = slice(hf * CH, (hf + 1) * CH)
                if cross:
                    for h in range(NH):
                        p0 = h % 8 * HD
                        sp.dma_start(c64[p0:p0 + HD, hf, h // 8], scr["craw"][bass.ds(b * NH * AH + h * AH, HD), cols])\
                            .then_inc(raw_in[hf], 16)
                    sp.dma_start(den[:, hf], scr["craw"].rearrange("(x r) n -> x r n", r=AH)[bass.ds(b * NH, NH), HD, cols])\
                        .then_inc(raw_in[hf], 16)
                else:
                    sp.dma_start(c64[:, hf], scr["cout"][bass.ds(b * H, H), cols].rearrange("(c p) n -> p c n", p=P))\
                        .then_inc(raw_in[hf], 16)
                    sp.dma_start(comb[:, hf], scr["comb"][bass.ds(b * H, H), cols].rearrange("(c p) n -> p c n", p=P))\
                        .then_inc(raw_in[hf], 16)
                    sp.dma_start(den[:, hf], scr["cden"][bass.ds(b * BH, BH), cols]).then_inc(raw_in[hf], 16)
                sp.dma_start(xt[:, hf], residual[bass.ds(b * S + hf * CH, CH)].rearrange("(t p) h -> p t h", p=P))\
                    .then_inc(raw_in[hf], 16)

            def batch(b, more):
                if more:
                    for hf in range(CPB):
                        load(b + 1, hf)
                if cross:
                    return
                for hf in range(CPB):
                    sp.wait_ge(x1_done, 8 + NT * (2 * b + hf) + NT)
                    sp.dma_start(scr["x1"][bass.ds(b * S + hf * CH, CH)].rearrange("(t p) h -> p t h", p=P), x1[:, hf])\
                        .then_inc(x1_out[hf], 16)
                for hf in range(CPB):
                    for s in range(KH):
                        sp.wait_ge(b_done, 2 + KH * (2 * b + hf) + s + 1)
                        sp.dma_start(scr["xq"][:, bass.ds(b * H + s * P, P), hf * CH:(hf + 1) * CH]
                                     .rearrange("a p n -> p a n"), ab[:, s]).then_inc(part_out[s], 16)

            for hf in range(CPB):
                load(0, hf)
            with sp.Fori(0, B - 1) as b:
                batch(b, True)
            batch(B - 1, False)
            if not cross:
                for n in range(2):
                    sp.wait_ge(x1_out[n], 16 + 16 * B)
                    sp.wait_ge(part_out[n], 16 + 16 * NCH)

        @block.gpsimd
        def _(pool):
            pool.memset(self32[:], 1.0).then_inc(sel_made, 1)
            pool.wait_ge(sel_made, 1)
            selector_steps(pool, self32, ((0, width, 0), (0, width, P)), sel_made)
            pool.sem_inc(b_done, 2)
            pool.wait_ge(small_in, 16 if cross else 48)
            with pool.Fori(0, B) as b:
                for hf in range(CPB):
                    i = 2 * b + hf
                    for c in range(KH):
                        pool.wait_ge(cna_done, KH * i + c + 1)
                        pool.tensor_tensor(cnb[:, hf, c], cn[:, c], cna[:, hf, c].bitcast(F32), ALU.subtract).then_inc(cnb_done, 1)
                    pool.wait_ge(raw_in[hf], 16 * RAWS * (b + 1))
                    pool.tensor_tensor(xt[:, hf], xt[:, hf], obias[:].unsqueeze(1).broadcast_to([P, NT, H]), ALU.add)\
                        .then_inc(xo_done, 1)
                    if not cross:
                        for c in range(KH):
                            pool.wait_ge(za_done, KH * i + c + 1)
                            pool.tensor_tensor(zb[:, hf, c], z[:, c], za[:, hf, c].bitcast(F32), ALU.subtract).then_inc(zb_done, 1)
                if not cross:
                    for hf in range(CPB):
                        for s in range(KH):
                            pool.wait_ge(a_done, KH * (2 * b + hf) + s + 1)
                            pool.tensor_tensor(ab[:, s, 1], t[:, s], ab[:, s, 0], ALU.subtract).then_inc(b_done, 1)

        @block.tensor
        def _(pe):
            pe.wait_ge(w_done, 1)
            pe.wait_ge(sel_done, 2)
            with pe.Fori(0, B) as b:
                for hf in range(CPB):
                    i = 2 * b + hf
                    pe.wait_ge(r_ready, i + 1)
                    for n in range(KH):
                        pe.wait_ge(pb_done, 2 + 2 * i + n - 1)
                        pe.matmul(pb[:, n], sel[:, n], rsplit[:], start=True, stop=True).then_inc(pb_ready, 1)
                    if not cross:
                        pe.wait_ge(cnb_done, KH * i + KH)
                        for c in range(KH):
                            w = slice(W0 + c * P, W0 + (c + 1) * P)
                            mm3(pe, pw[:, c], halves(wa, w), halves(wb, w), [cna[:, hf, x] for x in range(KH)],
                                [cnb[:, hf, x] for x in range(KH)]).then_inc(pw_ready, 1)
                for hf in range(CPB):
                    i = 2 * b + hf
                    if cross:
                        pe.wait_ge(cnb_done, KH * i + KH)
                        la, lb = [cna[:, hf, c] for c in range(KH)], [cnb[:, hf, c] for c in range(KH)]
                    else:
                        pe.wait_ge(zb_done, KH * i + KH)
                        la, lb = [za[:, hf, c] for c in range(KH)], [zb[:, hf, c] for c in range(KH)]
                    for tt in range(NT):
                        pe.wait_ge(y_done, NT * i + tt + 1)
                        tok = slice(tt * P, (tt + 1) * P)
                        mm3(pe, po[:, tt % 2, 0:H], [x[:, tok] for x in la], [x[:, tok] for x in lb],
                            halves(wa, slice(Y0, Y0 + H)), halves(wb, slice(Y0, Y0 + H))).then_inc(y_ready, 1)
                for hf in range(CPB):
                    i = 2 * b + hf
                    pe.wait_ge(y_done, 2 + NT * (2 * b + CPB))
                    pe.wait_ge(xb_done, i + 1)
                    pe.wait_ge(x1_done, 8 + NT * i + NT)
                    for kh in range(KH):
                        for tt in range(NT):
                            last = pe.transpose(px[:, kh, tt * P:(tt + 1) * P], x1[:, hf, tt, kh * P:(kh + 1) * P], ident[:])
                    last.then_inc(xT_ready, 1)
                    if not cross:
                        pe.wait_ge(xb_done, i + 2)
                        for n in range(KH):
                            pe.wait_ge(t_done, KH * i + n + 1)
                            w = slice(Q0 + n * P, Q0 + (n + 1) * P)
                            mm3(pe, po[:, n], halves(wa, w), halves(wb, w), halves(xa), halves(xb)).then_inc(po_ready, 1)
                        if hf == CPB - 1:
                            pe.wait_ge(t_done, 2 + KH * i + KH)

        @block.scalar
        def _(act):
            act.sem_inc(t_done, 2)
            act.wait_ge(small_in, 16 if cross else 48)
            act.wait_ge(eps_set, 1)
            if not cross:
                act.wait_ge(small_done, 2)
            with act.Fori(0, B) as b:
                for hf in range(CPB):
                    i = 2 * b + hf
                    for c in range(KH):
                        act.wait_ge(pb_done, 2 + 2 * i + c + 1)
                        act.activation(cna[:, hf, c], cn[:, c], ACT.Copy).then_inc(cna_done, 1)
                    if not cross:
                        for c in range(KH):
                            act.wait_ge(pw_ready, KH * i + c + 1)
                            act.activation(t1[:, c], pw[:, c], ACT.Identity, bias=small[:, 0, c:c + 1], scale=META_W)\
                                .then_inc(t1_done, 1)
                for hf in range(CPB):
                    i = 2 * b + hf
                    for tt in range(NT):
                        act.wait_ge(var_done, NT * i + tt + 1)
                        act.activation(rstd[:, tt % 2, 0:1], mv[:, tt % 2, 1:2], ACT.Sqrt, bias=eps[:]).then_inc(std_done, 1)
                for hf in range(CPB):
                    i = 2 * b + hf
                    act.wait_ge(xT_ready, i + 1)
                    dst = keep[0][:, :, bass.ds(b * S + hf * CH, CH)] if cross else xa[:]
                    act.activation(dst, px[:], ACT.Copy).then_inc(xa_done, 1)
                    if not cross:
                        for s in range(KH):
                            act.wait_ge(po_ready, KH * i + s + 1)
                            act.wait_ge(b_done, KH * i + s + 1)
                            act.activation(t[:, s], po[:, s], ACT.Identity, bias=small[:, 1, s:s + 1], scale=HD ** -0.5)\
                                .then_inc(t_done, 1)

        @block.vector
        def _(dve):
            dve.sem_inc(pb_done, 2)
            dve.sem_inc(y_done, 2)
            dve.sem_inc(x1_done, 8)
            dve.sem_inc(xb_done, 1)
            dve.memset(rsplit[:].bitcast(F32), 0.0).then_inc(rs_zero, 1)
            dve.memset(sel[:].bitcast(F32), 0.0).then_inc(sel_set, 1)
            dve.memset(eps[:], EPS).then_inc(eps_set, 1)
            dve.wait_ge(w_in, 16 if cross else 48)
            dve.tensor_copy(wa[:], raw[:]).then_inc(wa_done, 1)
            dve.wait_ge(wa_done, 1)
            dve.tensor_tensor(wb[:], raw[:], wa[:].bitcast(F32), ALU.subtract).then_inc(w_done, 1)
            if not cross:
                dve.wait_ge(small_in, 48)
                dve.tensor_scalar(small[:, 0], small_raw[:, 0], META_W, None, ALU.mult).then_inc(small_done, 1)
                dve.tensor_scalar(small[:, 1], small_raw[:, 1], HD ** -0.5, None, ALU.mult).then_inc(small_done, 1)
            dve.wait_ge(sel_made, 5)
            dve.wait_ge(sel_set, 1)
            dve.tensor_copy(sel[0:32], self32[:]).then_inc(sel_done, 1)
            dve.tensor_copy(sel[32:64], self32[:]).then_inc(sel_done, 1)
            dve.wait_ge(rs_zero, 1)
            with dve.Fori(0, B) as b:
                for hf in range(CPB):
                    i = 2 * b + hf
                    dve.wait_ge(raw_in[hf], 16 * RAWS * (b + 1))
                    dve.reciprocal(rden[:, hf], den[:, hf]).then_inc(r_chain, 1)
                    dve.wait_ge(r_chain, 2 * i + 1)
                    dve.tensor_copy(rsplit[0:NR], rden[:, hf]).then_inc(r_chain, 1)
                    dve.wait_ge(r_chain, 2 * i + 2)
                    dve.tensor_tensor(rsplit[32:32 + NR], rden[:, hf], rsplit[0:NR].bitcast(F32), ALU.subtract)\
                        .then_inc(r_ready, 1)
                    for n in range(KH):
                        dve.wait_ge(pb_ready, 2 * i + n + 1)
                        if cross and hf:
                            dve.wait_ge(xo_done, i)
                        dve.tensor_tensor(cn[:, n], c64[:, hf, n], pb[:, n], ALU.mult).then_inc(pb_done, 1)
                    if not cross:
                        for c in range(KH):
                            dve.wait_ge(t1_done, KH * i + c + 1)
                            dve.scalar_tensor_tensor(out=z[:, c], in0=comb[:, hf, c], scalar=1.0 - META_W, in1=t1[:, c],
                                                     op0=ALU.mult, op1=ALU.add).then_inc(z_done, 1)
                            dve.wait_ge(z_done, KH * i + c + 1)
                            dve.tensor_copy(za[:, hf, c], z[:, c]).then_inc(za_done, 1)
                for hf in range(CPB):
                    i = 2 * b + hf
                    dve.wait_ge(xo_done, i + 1)
                    if not cross:
                        dve.wait_ge(x1_out[hf], 16 * b + 16)
                    for tt in range(NT + 1):
                        if tt < NT:
                            n = NT * i + tt
                            dve.wait_ge(y_ready, n + 1)
                            dve.wait_ge(x1_done, 8 + n - 1)
                            dve.tensor_tensor(res[:, tt % 2], po[:, tt % 2, 0:H], xt[:, hf, tt], ALU.add).then_inc(y_done, 1)
                            dve.wait_ge(y_done, 2 + n + 1)
                            dve.bn_stats(stats[:, tt % 2], res[:, tt % 2]).then_inc(n_chain, 1)
                            dve.wait_ge(n_chain, 2 * NT * i + max(1, 2 * tt))
                            dve.sem_inc(stats_seen, 1)
                            dve.bn_aggr(mv[:, tt % 2], stats[:, tt % 2]).then_inc(var_done, 1)
                        if tt > 0:
                            u, m = tt - 1, NT * i + tt - 1
                            dve.wait_ge(std_done, m + 1)
                            dve.reciprocal(rstd[:, u % 2, 1:2], rstd[:, u % 2, 0:1]).then_inc(n_chain, 1)
                            dve.wait_ge(n_chain, 2 * NT * i + min(2 * u + 3, 2 * NT))
                            dve.tensor_scalar(x1[:, hf, u], res[:, u % 2], mv[:, u % 2, 0:1], rstd[:, u % 2, 1:2],
                                              ALU.subtract, ALU.mult).then_inc(x1_done, 1)
                            if cross:
                                dve.wait_ge(x1_done, 8 + m + 1)
                                dve.tensor_copy(keep[2][:, bass.ds(NT * i + u, 1)].squeeze(1), x1[:, hf, u])
                for hf in range(CPB):
                    i = 2 * b + hf
                    dve.wait_ge(xa_done, i + 1)
                    if cross:
                        tok = bass.ds(b * S + hf * CH, CH)
                        dve.tensor_tensor(keep[1][:, :, tok], px[:], keep[0][:, :, tok].bitcast(F32), ALU.subtract)\
                            .then_inc(xb_done, 1)
                        continue
                    dve.tensor_tensor(xb[:], px[:], xa[:].bitcast(F32), ALU.subtract).then_inc(xb_done, 1)
                    for s in range(KH):
                        dve.wait_ge(t_done, 2 + KH * i + s + 1)
                        dve.wait_ge(part_out[s], 16 * i + 16)
                        dve.tensor_copy(ab[:, s, 0].bitcast(FR), t[:, s]).then_inc(a_done, 1)


def context_projections(nc, A, scr, ident, dist, distT):
    with ExitStack() as stack:
        k = Kit(nc, stack, "cx")
        NE_ = 2 * B
        HB = NE_ // 2
        raw = k.sb("raw", [P, KH, 2 * H])
        wa, wb = k.sb("wa", [P, KH, 2 * H], FR), k.sb("wb", [P, KH, 2 * H], FR)
        kbias, vbias = k.sb("kbias", [P, KH]), k.sb("vbias", [P, H])
        scaling, negated, nabs, tiny = (k.sb(n, [P, 1]) for n in ("scaling", "negated", "nabs", "tiny"))
        ctx = k.sb("ctx", [E2, NE_, H])
        xa, xb = k.sb("xa", [P, KH, NE_, EP], FR), k.sb("xb", [P, KH, NE_, EP], FR)
        t, ab = k.sb("t", [P, 4, HB, EP]), k.sb("ab", [P, 4, 2, HB, EP])
        v16 = k.sb("v16", [EP, NE_, NH, AH])
        px, po, pd = k.ps("px", [P, 2, HB, P]), k.ps("po", [P, 2, CH]), k.ps("pd", [P, 2, NT, P])
        w_in, small_in, scale_in, ctx_in = k.sem("w_in"), k.sem("small_in"), k.sem("scale_in"), k.sem("ctx_in")
        dist_in = [k.sem(f"dist_in{b}") for b in range(B)]
        names = ("zeroed", "ones_set", "wa_done", "w_done", "s_chain", "ln_done", "scaled", "px_ready", "xa_done",
                 "xb_done", "k_ready", "t_done", "a_done", "b_done", "v_ready", "v_done", "pd_ready", "pd_act", "pd_dve",
                 "stored")
        (zeroed, ones_set, wa_done, w_done, s_chain, ln_done, scaled, px_ready, xa_done, xb_done, k_ready, t_done, a_done,
         b_done, v_ready, v_done, pd_ready, pd_act, pd_dve, stored) = (k.sem(n) for n in names)
        k_units = [(j, u) for j in range(KH) for u in range(2)]
        x_units = [(kh, u) for kh in range(KH) for u in range(2)]
        d_units = [(b, e, hq) for b in range(B) for e in range(2) for hq in range(CPB)]
        block = stack.enter_context(nc.Block())

        @block.sync
        def _(sp):
            sp.dma_start(ctx[:], A["ctx_1024"].rearrange("b (c e) h -> e (b c) h", c=2)).then_inc(ctx_in, 16)
            for n, w in enumerate(("Wk", "Wv")):
                sp.dma_start(raw[:, :, n * H:(n + 1) * H], A["L0_xattn_" + w].rearrange("(k p) n -> p k n", p=P)).then_inc(w_in, 16)
            for b in range(B):
                sp.dma_start(dist[:, b], A["fside_BxSxS2_0"][b].rearrange("(t p) n -> p t n", p=P)).then_inc(dist_in[b], 16)
            sp.dma_start(scaling[:], rows(A["L0_xattn_distance_scaling"])).then_inc(scale_in, 16)
            sp.dma_start(kbias[:], column(A["L0_xattn_bk"]), allow_slow_non_contiguous=True).then_inc(small_in, 16)
            sp.dma_start(vbias[:], rows(A["L0_xattn_bv"])).then_inc(small_in, 16)
            for s, (j, u) in enumerate(k_units):
                sp.wait_ge(b_done, s + 1)
                for part in range(2):
                    for n in range(2):
                        row = (2 * u + n) * H + j * P
                        sp.dma_start(scr["xk"][part, row:row + P], ab[:, s, part, 2 * n:2 * n + 2].rearrange("p e n -> p (e n)"))\
                            .then_inc(stored, 16)
            for n in range(NE_):
                sp.wait_ge(v_done, n + 1)
                sp.dma_start(scr["xv"].rearrange("(b g e p) c -> b e p g c", b=B, g=NG, e=2)[n // 2, n % 2],
                             v16[:, n].rearrange("p (g h) c -> p g (h c)", g=NG)).then_inc(stored, 16)
            sp.wait_ge(stored, 16 * (4 * len(k_units) + NE_))

        @block.gpsimd
        def _(pool):
            pool.memset(xa[:].bitcast(F32), 0.0).then_inc(zeroed, 1)
            pool.memset(xb[:].bitcast(F32), 0.0).then_inc(zeroed, 1)
            pool.memset(t[:], 0.0).then_inc(zeroed, 1)
            pool.memset(v16[:], 0.0).then_inc(zeroed, 1)
            pool.memset(distT[:], 0.0).then_inc(zeroed, 1)
            pool.wait_ge(zeroed, 5)
            pool.memset(v16[0:E2, :, :, HD:HD + 1], 1.0).then_inc(ones_set, 1)
            for s in range(len(k_units)):
                pool.wait_ge(a_done, s + 1)
                pool.tensor_tensor(ab[:, s, 1], t[:, s], ab[:, s, 0], ALU.subtract).then_inc(b_done, 1)

        @block.tensor
        def _(pe):
            pe.wait_ge(ctx_in, 16)
            for n, (kh, u) in enumerate(x_units):
                if n >= 2:
                    pe.wait_ge(xb_done, n - 1)
                for e in range(HB):
                    last = pe.transpose(px[:, n % 2, e, 0:E2], ctx[:, HB * u + e, kh * P:(kh + 1) * P], ident[0:E2, 0:E2])
                last.then_inc(px_ready, 1)
            pe.wait_ge(xb_done, len(x_units))
            pe.wait_ge(w_done, 1)
            for n, (j, u) in enumerate(k_units):
                if n >= 2:
                    pe.wait_ge(t_done, n - 1)
                w, blocks = slice(j * P, (j + 1) * P), slice(HB * u, HB * u + HB)
                mm3(pe, po[:, n % 2, 0:HB * EP].rearrange("p (e n) -> p e n", n=EP), halves(wa, w), halves(wb, w),
                    halves(xa, blocks), halves(xb, blocks)).then_inc(k_ready, 1)
            for n in range(NE_):
                if n < 2:
                    pe.wait_ge(t_done, len(k_units) - 1 + n)
                else:
                    pe.wait_ge(v_done, n - 1)
                w = slice(H, 2 * H)
                mm3(pe, po[0:EP, n % 2, 0:H], halves(xa, n), halves(xb, n), halves(wa, w), halves(wb, w)).then_inc(v_ready, 1)
            for n, (b, e, hq) in enumerate(d_units):
                pe.wait_ge(scaled, b + 1)
                if n >= 2:
                    pe.wait_ge((pd_act, pd_dve)[n % 2], n // 2)
                for i in range(NT):
                    last = pe.transpose(pd[0:E2, n % 2, i], dist[:, b, hq * NT + i, e * E2:(e + 1) * E2], ident[:])
                last.then_inc(pd_ready, 1)

        @block.scalar
        def _(act):
            act.wait_ge(zeroed, 5)
            for n, (kh, u) in enumerate(x_units):
                act.wait_ge(px_ready, n + 1)
                act.activation(xa[:, kh, HB * u:HB * u + HB, 0:E2], px[:, n % 2, :, 0:E2], ACT.Copy).then_inc(xa_done, 1)
            act.wait_ge(s_chain, 1)
            for b in range(B):
                act.wait_ge(dist_in[b], 16)
                act.activation(dist[:, b], dist[:, b], ACT.Ln, bias=tiny[:]).then_inc(ln_done, 1)
            act.wait_ge(small_in, 32)
            for n, (j, u) in enumerate(k_units):
                act.wait_ge(k_ready, n + 1)
                act.activation(t[:, n, :, 0:E2], po[:, n % 2, 0:HB * EP].rearrange("p (e n) -> p e n", n=EP)[:, :, 0:E2],
                               ACT.Identity, bias=kbias[:, j:j + 1]).then_inc(t_done, 1)
            for n, (b, e, hq) in enumerate(d_units):
                if n % 2 == 0:
                    act.wait_ge(pd_ready, n + 1)
                    act.activation(distT[0:E2, b, e, hq * CH:(hq + 1) * CH], pd[0:E2, n % 2].rearrange("p i n -> p (i n)"),
                                   ACT.Copy).then_inc(pd_act, 1)

        @block.vector
        def _(dve):
            dve.memset(tiny[:], 1e-9).then_inc(s_chain, 1)
            dve.wait_ge(w_in, 32)
            dve.tensor_copy(wa[:], raw[:]).then_inc(wa_done, 1)
            dve.wait_ge(wa_done, 1)
            dve.tensor_tensor(wb[:], raw[:], wa[:].bitcast(F32), ALU.subtract).then_inc(w_done, 1)
            for n, (kh, u) in enumerate(x_units):
                dve.wait_ge(xa_done, n + 1)
                blocks = slice(HB * u, HB * u + HB)
                dve.tensor_tensor(xb[:, kh, blocks, 0:E2], px[:, n % 2, :, 0:E2], xa[:, kh, blocks, 0:E2].bitcast(F32), ALU.subtract)\
                    .then_inc(xb_done, 1)
            dve.wait_ge(scale_in, 16)
            dve.tensor_scalar(negated[:], scaling[:], -1.0, None, ALU.mult).then_inc(s_chain, 1)
            dve.wait_ge(s_chain, 2)
            dve.tensor_tensor(nabs[:], scaling[:], negated[:], ALU.min).then_inc(s_chain, 1)
            dve.wait_ge(s_chain, 3)
            for b in range(B):
                dve.wait_ge(ln_done, b + 1)
                dve.tensor_scalar(dist[:, b], dist[:, b], nabs[:, 0:1], None, ALU.mult).then_inc(scaled, 1)
            for n in range(len(k_units)):
                dve.wait_ge(t_done, n + 1)
                dve.tensor_copy(ab[:, n, 0].bitcast(FR), t[:, n]).then_inc(a_done, 1)
            dve.wait_ge(ones_set, 1)
            dve.wait_ge(small_in, 32)
            for n in range(NE_):
                dve.wait_ge(v_ready, n + 1)
                dve.tensor_tensor(v16[0:E2, n, :, 0:HD], po[0:E2, n % 2, 0:H].rearrange("p (h d) -> p h d", h=NH),
                                  vbias[0:E2].rearrange("p (h d) -> p h d", h=NH), ALU.add).then_inc(v_done, 1)
            for n, (b, e, hq) in enumerate(d_units):
                if n % 2:
                    dve.wait_ge(pd_ready, n + 1)
                    dve.tensor_copy(distT[0:E2, b, e, hq * CH:(hq + 1) * CH], pd[0:E2, n % 2].rearrange("p i n -> p (i n)"))\
                        .then_inc(pd_dve, 1)


def attend_cross(nc, scr, dist, distT):
    with ExitStack() as stack:
        k = Kit(nc, stack, "ac")
        ONE, LAST = 4 * HD, 6 * HD
        MROW = LAST - 1
        NSTEP = CPB * 2
        qs, ks = k.sb("qs", [LAST, NG, GH, S], FR), k.sb("ks", [LAST, NG, GH, 2, EP], FR)
        vs = k.sb("vs", [EP, NG, 2, GH * AH])
        probs = k.sb("probs", [EP, 2, GH, CH])
        ev = k.sb("ev", [P, CPB, CH])
        bias = k.sb("bias", [P, S // P, S2])
        m1 = k.sb("m1", [P, CPB, GH * NT])
        mneg, mturn = k.sb("mneg", [P, 32]), k.sb("mturn", [P, 32])
        mrows = k.sb("mrows", [P, CPB, 32], FR)
        pst = k.ps("pst", [P, 2, 2, CH])
        psm = k.ps("psm", [P, 2, 2, 2, P])
        pacc = k.ps("pacc", [P, CPB, CH])
        filled, zeroed, mneg_set, bias_done, mx_seen = (
            k.sem(n) for n in ("filled", "zeroed", "mneg_set", "bias_done", "mx_seen"))
        loaded = [k.sem(f"loaded{n}") for n in range(NG)]
        mrow_in = [[k.sem(f"mrow_in{n}{h}") for h in range(CPB)] for n in range(NG)]
        m_out = [k.sem(f"m_out{h}") for h in range(CPB)]
        ev_out = [k.sem(f"ev_out{h}") for h in range(CPB)]
        mx_ready, mx_done, m_chain, m_ready, row_moved = (
            k.sem(n) for n in ("mx_ready", "mx_done", "m_chain", "m_ready", "row_moved"))
        st_ready, add_done, exp_done, pv_done, acc_out = (
            k.sem(n) for n in ("st_ready", "add_done", "exp_done", "pv_done", "acc_out"))
        LOADS = 9
        PV0 = NSTEP * (NG - 1) + 2
        mx_list = [(hq, jp, i) for hq in range(CPB) for jp in range(GH // 2) for i in range(NT)]
        NM = len(mx_list)
        PER = NM // NSTEP
        block = stack.enter_context(nc.Block())

        @block.sync
        def _(sp):
            def load(G, slot):
                sp.wait_ge(pv_done, PV0 + NSTEP * (G - NG + 1))
                for r, (qp, kp) in enumerate(((0, 0), (0, 1), (1, 0), (1, 1))):
                    sp.dma_start(qs[r * HD:(r + 1) * HD, slot].bitcast(F32),
                                 scr["xq"][qp, bass.ds(G * GH * HD, GH * HD)].rearrange("(j d) n -> d j n", j=GH))\
                        .then_inc(loaded[slot], 16)
                    sp.dma_start(ks[r * HD:(r + 1) * HD, slot].rearrange("p j e n -> p j (e n)").bitcast(F32),
                                 scr["xk"][kp, bass.ds(G * GH * HD, GH * HD)].rearrange("(j d) n -> d j n", j=GH))\
                        .then_inc(loaded[slot], 16)
                sp.dma_start(vs[:, slot], scr["xv"][bass.ds(G * 2 * EP, 2 * EP)].rearrange("(e p) n -> p e n", p=EP))\
                    .then_inc(loaded[slot], 16)

            def max_row(G, slot, uses, hq):
                sp.wait_ge(m_ready, CPB * G + hq + 1)
                turned = scr["m"][hq].rearrange("(c b r) -> b c r", b=4, r=32)
                for q in range(4):
                    sp.dma_start(turned[q], mrows[32 * q:32 * q + GH * NT, hq].bitcast(F32)).then_inc(m_out[hq], 16)
                sp.wait_ge(m_out[hq], 64 * G + 64)
                sp.dma_start(qs[MROW:LAST, slot, :, hq * CH:(hq + 1) * CH].bitcast(F32),
                             scr["m"][hq:hq + 1].rearrange("o (j n) -> o j n", j=GH)).then_inc(mrow_in[slot][hq], 16)
                sp.wait_ge(mrow_in[slot][hq], 16 * uses + 16)
                sp.sem_inc(row_moved, 1)

            def store(G, qh):
                sp.wait_ge(acc_out, CPB * G + qh + 3)
                sp.dma_start(scr["craw"][bass.ds(G * P, P), qh * CH:(qh + 1) * CH], ev[:, qh]).then_inc(ev_out[qh], 16)

            def group(b, g, ahead):
                G = b * NG + g
                if ahead >= 2:
                    load(G + 2, (g + 2) % NG)
                if ahead >= 1:
                    max_row(G + 1, (g + 1) % NG, b + (g + 1) // NG, 0)
                store(G, 0)
                if ahead >= 1:
                    max_row(G + 1, (g + 1) % NG, b + (g + 1) // NG, 1)
                store(G, 1)

            for qh in range(CPB):
                sp.sem_inc(ev_out[qh], 16)
            load(0, 0)
            load(1, 1)
            for hq in range(CPB):
                max_row(0, 0, 0, hq)
            with sp.Fori(0, B - 1) as b:
                for g in range(NG):
                    group(b, g, 2)
            for g in range(NG):
                group(B - 1, g, NG - 1 - g)
            for qh in range(CPB):
                sp.wait_ge(ev_out[qh], 16 + 16 * B * NG)

        @block.gpsimd
        def _(pool):
            pool.memset(qs[ONE:LAST].bitcast(F32), 0.0).then_inc(filled, 1)

        @block.tensor
        def _(pe):
            def maxima(G, slot, uses, lo, hi):
                for n in range(lo, hi):
                    hq, jp, i = mx_list[n]
                    if n == 0:
                        pe.wait_ge(loaded[slot], 16 * LOADS * uses + 16 * LOADS)
                    pe.wait_ge(mx_done, 2 * (NM * G + n + 1))
                    q0 = (hq * NT + i) * P
                    for jj in range(2):
                        j = 2 * jp + jj
                        last = pe.matmul(psm[:, n % 2, jj, :, 0:EP], qs[0:MROW, slot, j, q0:q0 + P],
                                         ks[0:MROW, slot, j], start=True, stop=True)
                    last.then_inc(mx_ready, 1)

            def values(G, slot, s):
                qh, e = divmod(s, 2)
                pe.wait_ge(exp_done, NSTEP * G + s + 1)
                if e == 0:
                    pe.wait_ge(acc_out, CPB * G + qh + 1)
                for j in range(GH):
                    last = pe.matmul(pacc[j * AH:(j + 1) * AH, qh], vs[:, slot, e, j * AH:(j + 1) * AH],
                                     probs[:, s % 2, j], start=(e == 0), stop=(e == 1))
                last.then_inc(pv_done, 1)

            def group(b, g, more):
                G = b * NG + g
                nxt = (G + 1, (g + 1) % NG, b + (g + 1) // NG)
                for s in range(NSTEP):
                    qh, e = divmod(s, 2)
                    if e == 0:
                        pe.wait_ge(mrow_in[g][qh], 16 * b + 16)
                    for hp in range(2):
                        pe.wait_ge(add_done, 2 * NSTEP * G + 2 * s + hp + 1)
                        for jj in range(2):
                            j = 2 * hp + jj
                            last = pe.matmul(pst[0:EP, hp, jj], ks[:, g, j, e], qs[:, g, j, qh * CH:(qh + 1) * CH],
                                             start=True, stop=True)
                        last.then_inc(st_ready, 1)
                        if more:
                            maxima(*nxt, PER * s + hp, PER * s + hp + 1)
                    if s > 0:
                        values(G, g, s - 1)
                    if more:
                        maxima(*nxt, PER * s + 2, PER * s + PER)
                values(G, g, NSTEP - 1)

            pe.sem_inc(pv_done, PV0)
            pe.wait_ge(filled, 2)
            maxima(0, 0, 0, 0, NM)
            with pe.Fori(0, B - 1) as b:
                for g in range(NG):
                    group(b, g, True)
            for g in range(NG):
                group(B - 1, g, g < NG - 1)

        @block.scalar
        def _(act):
            def copy_out(G, qh):
                act.wait_ge(pv_done, PV0 + NSTEP * G + 2 * qh + 2)
                act.wait_ge(ev_out[qh], 16 * G + 16)
                act.activation(ev[:, qh], pacc[:, qh], ACT.Copy).then_inc(acc_out, 1)

            act.sem_inc(acc_out, 2)
            with act.Fori(0, B) as b:
                for g in range(NG):
                    G = b * NG + g
                    for s in range(NSTEP):
                        act.wait_ge(add_done, 2 + 2 * (NSTEP * G + s + 1))
                        act.activation(probs[:, s % 2], probs[:, s % 2], ACT.Exp).then_inc(exp_done, 1)
                        if s == 3:
                            copy_out(G, 0)
                    copy_out(G, 1)

        @block.vector
        def _(dve):
            def take_bias(b):
                src = dist[:, b] if isinstance(b, int) else dist[:, bass.ds(b, 1)].rearrange("p o t n -> p (o t) n")
                dve.tensor_copy(bias[:], src).then_inc(bias_done, 1)

            def maxima(G, lo, hi):
                for n in range(lo, hi):
                    hq, jp, i = mx_list[n]
                    dve.wait_ge(mx_ready, NM * G + n + 1)
                    dve.sem_inc(mx_seen, 1)
                    for jj in range(2):
                        col = (2 * jp + jj) * NT + i
                        scores = psm[:, n % 2, jj, :, 0:E2]
                        dve.tensor_tensor_reduce(out=scores, in0=scores, in1=bias[:, hq * NT + i].rearrange("p (e n) -> p e n", e=2), scale=1.0, scalar=LOWEST, op0=ALU.add,
                                                 op1=ALU.max, accum_out=m1[:, hq, col:col + 1]).then_inc(mx_done, 1)
                    if n % (NM // CPB) == NM // CPB - 1:
                        finish(G, hq)

            def finish(G, hq):
                dve.wait_ge(mx_done, 4 + 2 * (NM * G + (hq + 1) * NM // CPB))
                dve.tensor_scalar(mneg[:, 0:GH * NT], m1[:, hq], -1.0, None, ALU.mult).then_inc(m_chain, 1)
                dve.wait_ge(m_chain, 2 * (CPB * G + hq) + 1)
                dve.transpose(mturn[:], mneg[:]).then_inc(m_chain, 1)
                dve.wait_ge(m_chain, 2 * (CPB * G + hq) + 2)
                if not (isinstance(G, int) and G == 0):
                    dve.wait_ge(row_moved, CPB * (G - 1) + hq + 1)
                dve.tensor_copy(mrows[:, hq], mturn[:]).then_inc(m_ready, 1)

            def group(b, g, more):
                G = b * NG + g
                if more and g == NG - 1:
                    take_bias(b + 1)
                    dve.wait_ge(bias_done, b + 2)
                for s in range(NSTEP):
                    qh, e = divmod(s, 2)
                    for hp in range(2):
                        dve.wait_ge(st_ready, 2 * NSTEP * G + 2 * s + hp + 1)
                        if hp == 0:
                            dve.wait_ge(pv_done, PV0 + NSTEP * G + s - 1)
                        cols = slice(qh * CH, (qh + 1) * CH)
                        added = distT[:, b, e, cols] if isinstance(b, int) else \
                            distT[:, bass.ds(b, 1), e, cols].rearrange("p o n -> p (o n)")
                        dve.tensor_tensor(probs[:, s % 2, 2 * hp:2 * hp + 2], pst[0:EP, hp],
                                          added.unsqueeze(1).broadcast_to([EP, 2, CH]), ALU.add).then_inc(add_done, 1)
                        if more:
                            maxima(G + 1, PER * s + hp * PER // 2, PER * s + (hp + 1) * PER // 2)

            dve.sem_inc(mx_done, 4)
            dve.sem_inc(add_done, 2)
            dve.memset(ks[ONE:LAST].bitcast(F32), 0.0).then_inc(zeroed, 1)
            dve.wait_ge(zeroed, 1)
            dve.memset(mneg[:], 0.0).then_inc(mneg_set, 1)
            dve.wait_ge(mneg_set, 1)
            dve.memset(ks[ONE:LAST, :, :, :, 0:E2].bitcast(F32), 1.0).then_inc(filled, 1)
            take_bias(0)
            dve.wait_ge(bias_done, 1)
            maxima(0, 0, NM)
            with dve.Fori(0, B - 1) as b:
                for g in range(NG):
                    group(b, g, True)
            for g in range(NG):
                group(B - 1, g, g < NG - 1)


def route(nc, A, ident, xa, xb, weight):
    with ExitStack() as stack:
        k = Kit(nc, stack, "ro")
        TT = TOK // P
        raw, wa, wb = k.sb("raw", [P, KH, NE]), k.sb("wa", [P, KH, NE], FR), k.sb("wb", [P, KH, NE], FR)
        lt = k.sb("lt", [NE, 2, CH])
        grid = [P, TT, NE]
        logits, prob, masked, equal, ranked, first, second = (
            k.sb(n, grid) for n in ("logits", "prob", "masked", "equal", "ranked", "first", "second"))
        rank = k.sb("rank", [P, NE])
        top, total, high1, high2, pick, share1, share2 = (
            k.sb(n, [P, TT]) for n in ("top", "total", "high1", "high2", "pick", "share1", "share2"))
        pl, pt = k.ps("pl", [NE, 2, CH]), k.ps("pt", [P, 2, CH // NE, NE])
        w_in, wa_done, w_done, rank_set, l_ready, l_done, t_ready, t_done, chain, exp_done = (k.sem(n) for n in (
            "w_in", "wa_done", "w_done", "rank_set", "l_ready", "l_done", "t_ready", "t_done", "chain", "exp_done"))
        block = stack.enter_context(nc.Block())

        @block.sync
        def _(sp):
            sp.dma_start(raw[:], A["L0_ffn_gate_w"].rearrange("(k p) n -> p k n", p=P)).then_inc(w_in, 16)

        @block.gpsimd
        def _(pool):
            for e in range(NE):
                pool.memset(rank[:, e:e + 1], float(NE - e)).then_inc(rank_set, 1)
            pool.memset(weight[:, NE], 1.0).then_inc(rank_set, 1)

        @block.tensor
        def _(pe):
            def turn(c):
                pe.wait_ge(l_done, c + 1)
                if c >= 2:
                    pe.wait_ge(t_done, c - 1)
                for tt in range(NT):
                    last = pe.transpose(pt[:, c % 2, tt], lt[:, c % 2, tt * P:(tt + 1) * P], ident[0:NE, 0:NE])
                last.then_inc(t_ready, 1)

            pe.wait_ge(w_done, 1)
            for c in range(NCH):
                if c >= 2:
                    pe.wait_ge(l_done, c - 1)
                tok = slice(c * CH, (c + 1) * CH)
                mm3(pe, pl[:, c % 2], halves(wa), halves(wb), halves(xa, tok), halves(xb, tok)).then_inc(l_ready, 1)
                if c >= 1:
                    turn(c - 1)
            turn(NCH - 1)

        @block.scalar
        def _(act):
            for c in range(NCH):
                act.wait_ge(l_ready, c + 1)
                if c >= 2:
                    act.wait_ge(t_ready, c - 1)
                act.activation(lt[:, c % 2], pl[:, c % 2], ACT.Copy).then_inc(l_done, 1)
            act.wait_ge(chain, 2)
            act.activation(prob[:], prob[:], ACT.Exp).then_inc(exp_done, 1)

        @block.vector
        def _(dve):
            count = [0]

            def link(instruction):
                instruction.then_inc(chain, 1)
                count[0] += 1
                dve.wait_ge(chain, count[0])

            def over(v):
                return v[:].unsqueeze(2).broadcast_to(grid)

            def pick_first(src, high, onehot):
                link(dve.tensor_reduce(high[:], src[:], AX.X, ALU.max))
                link(dve.tensor_tensor(equal[:], src[:], over(high), ALU.is_equal))
                link(dve.tensor_tensor(ranked[:], equal[:], rank[:].unsqueeze(1).broadcast_to(grid), ALU.mult))
                link(dve.tensor_reduce(pick[:], ranked[:], AX.X, ALU.max))
                link(dve.tensor_tensor(onehot[:], ranked[:], over(pick), ALU.is_equal))

            dve.wait_ge(w_in, 16)
            dve.tensor_copy(wa[:], raw[:]).then_inc(wa_done, 1)
            dve.wait_ge(wa_done, 1)
            dve.tensor_tensor(wb[:], raw[:], wa[:].bitcast(F32), ALU.subtract).then_inc(w_done, 1)
            for c in range(NCH):
                dve.wait_ge(t_ready, c + 1)
                dve.tensor_copy(logits[:, c * NT:(c + 1) * NT], pt[:, c % 2, 0:NT]).then_inc(t_done, 1)
            dve.wait_ge(t_done, NCH)
            link(dve.tensor_reduce(top[:], logits[:], AX.X, ALU.max))
            link(dve.tensor_tensor(prob[:], logits[:], over(top), ALU.subtract))
            dve.wait_ge(exp_done, 1)
            link(dve.tensor_reduce(total[:], prob[:], AX.X, ALU.add))
            link(dve.reciprocal(total[:], total[:]))
            link(dve.tensor_tensor(prob[:], prob[:], over(total), ALU.mult))
            dve.wait_ge(rank_set, NE + 1)
            pick_first(prob, high1, first)
            link(dve.scalar_tensor_tensor(out=masked[:], in0=first[:], scalar=-2.0, in1=prob[:], op0=ALU.mult, op1=ALU.add))
            pick_first(masked, high2, second)
            link(dve.tensor_tensor(total[:], high1[:], high2[:], ALU.add))
            link(dve.tensor_scalar(total[:], total[:], 1e-20, None, ALU.add))
            link(dve.reciprocal(total[:], total[:]))
            link(dve.tensor_tensor(share1[:], high1[:], total[:], ALU.mult))
            link(dve.tensor_tensor(share2[:], high2[:], total[:], ALU.mult))
            link(dve.tensor_tensor(first[:], first[:], over(share1), ALU.mult))
            link(dve.tensor_tensor(second[:], second[:], over(share2), ALU.mult))
            link(dve.tensor_tensor(weight[:, 0:NE].rearrange("p e t -> p t e"), first[:], second[:], ALU.add))


def run_experts(nc, A, xa, xb, acc, weight):
    with ExitStack() as stack:
        k = Kit(nc, stack, "ex")
        G0, U0, D0 = 0, KH * D, 2 * KH * D
        NW = D0 + FB * H
        PIECE = NW // NCH
        raw = k.sb("raw", [P, 2, NW])
        wa, wb = k.sb("wa", [P, 2, NW], FR), k.sb("wb", [P, 2, NW], FR)
        gated, hid = k.sb("gated", [P, 2, CH]), k.sb("hid", [P, 2, CH])
        ha, hb = k.sb("ha", [P, FB, CH], FR), k.sb("hb", [P, FB, CH], FR)
        pg, pu, py = k.ps("pg", [P, 2, CH]), k.ps("pu", [P, 2, CH]), k.ps("py", [P, NT, CH])
        w_in = [k.sem(f"w_in{n}") for n in range(2)]
        piece_a, piece_b, g_ready, u_ready, gated_done, hid_done, a_done, b_done, y_ready, acc_done = (k.sem(n) for n in (
            "piece_a", "piece_b", "g_ready", "u_ready", "gated_done", "hid_done", "a_done", "b_done", "y_ready", "acc_done"))
        block = stack.enter_context(nc.Block())

        def matrix(w, slot, first, n, cols):
            return w[:, slot, first + n * cols:first + (n + 1) * cols]

        @block.sync
        def _(sp):
            def load(slot, gate, up, down):
                for src, at, n in ((gate, G0, KH * D), (up, U0, KH * D), (down, D0, FB * H)):
                    blocks = n // src.shape[-1]
                    sp.dma_start(raw[:, slot, at:at + n].rearrange("p (k n) -> p k n", k=blocks),
                                 src.rearrange("(k p) n -> p k n", p=P)).then_inc(w_in[slot], 16)

            def load_expert(e, slot):
                gate, up, down = (A["L0_ffn_w_" + n].rearrange("e k n -> (e k) n") for n in ("gate", "up", "down"))
                load(slot, gate[bass.ds(e * H, H)], up[bass.ds(e * H, H)], down[bass.ds(e * D, D)])

            load_expert(0, 0)
            load_expert(1, 1)
            with sp.Fori(0, NE // 2 - 1) as ep:
                for n in range(2):
                    sp.wait_ge(piece_b, NCH * (2 * ep + n + 1))
                    load_expert(2 * ep + n + 2, n)
            sp.wait_ge(piece_b, NCH * (NE - 1))
            load(0, A["L0_ffn_ws_gate"], A["L0_ffn_ws_up"], A["L0_ffn_ws_down"])

        def pieces(c):
            return bass.ds(c * PIECE, PIECE)

        @block.gpsimd
        def _(pool):
            def split(e, slot, c):
                pool.wait_ge(piece_a, NCH * e + c + 1)
                pool.tensor_tensor(wb[:, slot, pieces(c)], raw[:, slot, pieces(c)], wa[:, slot, pieces(c)].bitcast(F32),
                                   ALU.subtract).then_inc(piece_b, 1)

            def expert(e, n, more):
                with pool.Fori(0, NCH) as c:
                    t = NCH * e + c
                    for f in range(FB):
                        pool.wait_ge(a_done, FB * t + f + 1)
                        pool.tensor_tensor(hb[:, f], hid[:, f % 2], ha[:, f].bitcast(F32), ALU.subtract).then_inc(b_done, 1)
                    if more:
                        split(e + 1, 1 - n, c)

            pool.sem_inc(b_done, 2)
            with pool.Fori(0, NCH) as c:
                split(0, 0, c)
            with pool.Fori(0, NE // 2) as ep:
                for n in range(2):
                    expert(2 * ep + n, n, True)
            expert(NE, 0, False)

        @block.tensor
        def _(pe):
            def expert(e, slot):
                with pe.Fori(0, NCH) as c:
                    pe.wait_ge(piece_b, NCH * e + NCH)
                    t = NCH * e + c
                    tok = bass.ds(c * CH, CH)
                    for f in range(FB):
                        for out, first, free, ready in ((pg, G0, gated_done, g_ready), (pu, U0, hid_done, u_ready)):
                            pe.wait_ge(free, FB * t + f + 1)
                            la, lb = ([matrix(w, slot, first, n, D)[:, f * P:(f + 1) * P] for n in range(KH)] for w in (wa, wb))
                            mm3(pe, out[:, f % 2], la, lb, halves(xa, tok), halves(xb, tok)).then_inc(ready, 1)
                    pe.wait_ge(acc_done, NT * t + NT)
                    for f in range(FB):
                        pe.wait_ge(b_done, 2 + FB * t + f + 1)
                        for tt in range(NT):
                            cols = slice(tt * P, (tt + 1) * P)
                            da, db = matrix(wa, slot, D0, f, H), matrix(wb, slot, D0, f, H)
                            for n, (x, y) in enumerate(((ha, da), (ha, db), (hb, da))):
                                last = pe.matmul(py[:, tt, 0:H], x[:, f, cols], y, start=(f == 0 and n == 0),
                                                 stop=(f == FB - 1 and n == 2))
                            if f == FB - 1:
                                last.then_inc(y_ready, 1)

            with pe.Fori(0, NE // 2) as ep:
                for n in range(2):
                    expert(2 * ep + n, n)
            expert(NE, 0)

        @block.scalar
        def _(act):
            act.sem_inc(gated_done, 2)
            with act.Fori(0, NE + 1) as e:
                with act.Fori(0, NCH) as c:
                    t = NCH * e + c
                    for f in range(FB):
                        act.wait_ge(g_ready, FB * t + f + 1)
                        act.wait_ge(hid_done, FB * t + f + 1)
                        act.activation(gated[:, f % 2], pg[:, f % 2], ACT.Silu).then_inc(gated_done, 1)

        @block.vector
        def _(dve):
            def split(e, slot, c):
                dve.tensor_copy(wa[:, slot, pieces(c)], raw[:, slot, pieces(c)]).then_inc(piece_a, 1)

            def expert(e, n, more, uses):
                with dve.Fori(0, NCH) as c:
                    t = NCH * e + c
                    for f in range(FB):
                        dve.wait_ge(gated_done, 2 + FB * t + f + 1)
                        dve.wait_ge(u_ready, FB * t + f + 1)
                        dve.wait_ge(b_done, FB * t + f + 1)
                        dve.tensor_tensor(hid[:, f % 2], gated[:, f % 2], pu[:, f % 2], ALU.mult).then_inc(hid_done, 1)
                        dve.wait_ge(hid_done, 2 + FB * t + f + 1)
                        dve.tensor_copy(ha[:, f], hid[:, f % 2]).then_inc(a_done, 1)
                    if more:
                        dve.wait_ge(w_in[1 - n], 48 * uses)
                        split(e + 1, 1 - n, c)
                    for tt in range(NT):
                        dve.wait_ge(y_ready, NT * t + tt + 1)
                        tile = acc[:, bass.ds(NT * c + tt, 1)].rearrange("p o n -> p (o n)")
                        dve.scalar_tensor_tensor(out=tile, in0=py[:, tt, 0:H],
                                                 scalar=weight[:].rearrange("p e t -> p (e t)")[:, bass.ds(TOK // P * e + NT * c + tt, 1)],
                                                 in1=tile, op0=ALU.mult, op1=ALU.add).then_inc(acc_done, 1)

            dve.sem_inc(hid_done, 2)
            dve.sem_inc(acc_done, 4)
            dve.wait_ge(w_in[0], 48)
            with dve.Fori(0, NCH) as c:
                split(0, 0, c)
            with dve.Fori(0, NE // 2) as ep:
                for n in range(2):
                    expert(2 * ep + n, n, True, ep + 1 + n)
            expert(NE, 0, False, 0)


def final_norm(nc, acc, out):
    with ExitStack() as stack:
        k = Kit(nc, stack, "fn")
        TT = TOK // P
        stats, mv = k.sb("stats", [P, TT, 6]), k.sb("mv", [P, TT, 2])
        std, rstd, eps = k.sb("std", [P, TT]), k.sb("rstd", [P, TT]), k.sb("eps", [P, 1])
        eps_set, stats_done, mv_done, std_done, rstd_done, y_done, stored = (k.sem(n) for n in (
            "eps_set", "stats_done", "mv_done", "std_done", "rstd_done", "y_done", "stored"))
        block = stack.enter_context(nc.Block())

        @block.sync
        def _(sp):
            for c in range(NCH):
                sp.wait_ge(y_done, NT * (c + 1))
                sp.dma_start(out[c * CH:(c + 1) * CH].rearrange("(t p) h -> p t h", p=P), acc[:, c * NT:(c + 1) * NT])\
                    .then_inc(stored, 16)
            sp.wait_ge(stored, 16 * NCH)

        @block.scalar
        def _(act):
            act.wait_ge(eps_set, 1)
            for c in range(NCH):
                act.wait_ge(mv_done, NT * (c + 1))
                tiles = slice(c * NT, (c + 1) * NT)
                act.activation(std[:, tiles], mv[:, tiles, 1], ACT.Sqrt, bias=eps[:]).then_inc(std_done, 1)

        @block.vector
        def _(dve):
            def finish(c):
                tiles = slice(c * NT, (c + 1) * NT)
                dve.wait_ge(std_done, c + 1)
                dve.reciprocal(rstd[:, tiles], std[:, tiles]).then_inc(rstd_done, 1)
                dve.wait_ge(rstd_done, c + 1)
                for n in range(c * NT, (c + 1) * NT):
                    dve.tensor_scalar(acc[:, n], acc[:, n], mv[:, n, 0:1], rstd[:, n:n + 1], ALU.subtract, ALU.mult)\
                        .then_inc(y_done, 1)

            dve.memset(eps[:], EPS).then_inc(eps_set, 1)
            for c in range(NCH):
                for n in range(c * NT, (c + 1) * NT):
                    dve.bn_stats(stats[:, n], acc[:, n]).then_inc(stats_done, 1)
                for n in range(c * NT, (c + 1) * NT):
                    dve.wait_ge(stats_done, n + 1)
                    dve.bn_aggr(mv[:, n], stats[:, n]).then_inc(mv_done, 1)
                if c:
                    finish(c - 1)
            finish(NCH - 1)


def clear_semaphores(nc):
    nc.all_engine_barrier(sems_to_clear=range(min(nc.free_semaphores), max(nc.free_semaphores) + 1))


def decoder_layer(nc, A, out):
    scr = {name: nc.dram_tensor("scr_" + name, shape, F32, kind="Internal").ap() for name, shape in dict(
        q=[2, B * H, S], k=[2, B * H, S], v=[B * NG * S, GH * AH], m=[CPB, GH * CH], craw=[B * NH * AH, S],
        cq=[2, B * H, S], ck=[2, B * H, S], cv=[TOK, H], cm=[CPB, 2 * CH], cout=[B * H, S], cden=[B * BH, S],
        mq=[2, B * H, S], mk=[2, B * H, S], mv=[TOK, H], mm=[CPB, 2 * CH], mout=[B * H, S], mden=[B * BH, S],
        comb=[B * H, S], x1=[TOK, H], xq=[2, B * H, S], xk=[2, B * H, 2 * EP], xv=[B * NG * 2 * EP, GH * AH],
        xm=[CPB, GH * CH], xcraw=[B * NH * AH, S]).items()}

    def named(**names):
        return {key: scr[name] for key, name in names.items()}

    with ExitStack() as stack:
        ident = Kit(nc, stack, "all").sb("ident", [P, P])
        identity_phase(nc, ident)
        input_projections(nc, A, scr, ident)
        attend_narrow(nc, scr, None)
        attend_wide(nc, named(q="cq", k="ck", v="cv", m="cm", out="cout", den="cden"), "ca")
        join_attention(nc, A, scr)
        attend_wide(nc, named(q="mq", k="mk", v="mv", m="mm", out="mout", den="mden"), "mc")
        clear_semaphores(nc)
        project_and_norm(nc, A, named(comb="comb", cout="mout", cden="mden", x1="x1", xq="xq"), ident, False)
        with ExitStack() as inner:
            k = Kit(nc, inner, "bias")
            dist, distT = k.sb("dist", [P, B, S // P, S2]), k.sb("distT", [EP, B, 2, S])
            context_projections(nc, A, scr, ident, dist, distT)
            attend_cross(nc, named(xq="xq", xk="xk", xv="xv", m="xm", craw="xcraw"), dist, distT)
        k = Kit(nc, stack, "x2")
        xa, xb = k.sb("a", [P, KH, TOK], FR), k.sb("b", [P, KH, TOK], FR)
        acc = k.sb("acc", [P, TOK // P, H])
        weight = k.sb("weight", [P, NE + 1, TOK // P])
        project_and_norm(nc, A, named(craw="xcraw", x1="x1"), ident, True, (xa, xb, acc))
        clear_semaphores(nc)
        route(nc, A, ident, xa, xb, weight)
        run_experts(nc, A, xa, xb, acc, weight)
        final_norm(nc, acc, out)


INPUTS = ["x", "ctx_1024", "fside_BxSxS2_0"] + [f"L0_attn_{n}" for n in (
    "cons_vec", "Wq", "bq", "Wk", "bk", "Wv", "bv", "cg_W", "cg_b", "am_W", "am_b", "ca_Win", "ca_bin", "ca_Wout",
    "ca_bout", "mc_Win", "mc_bin", "mc_Wout", "mc_bout", "Wo", "bo")] + [f"L0_xattn_{n}" for n in (
        "Wq", "bq", "Wk", "bk", "Wv", "bv", "Wo", "bo", "distance_scaling")] + [f"L0_ffn_{n}" for n in (
            "gate_w", "w_gate", "w_up", "w_down", "ws_gate", "ws_up", "ws_down")]


def kernel(**inputs):
    import numpy as np
    import concourse.bacc as bacc
    from concourse.bass_utils import run_bass_kernel_spmd

    nc = bacc.Bacc("TRN2", target_bir_lowering=False, num_devices=1)
    arrays, dram = {}, {}
    for name in INPUTS:
        a = np.asarray(inputs[name])
        if name in ("L0_xattn_Wq", "L0_xattn_Wk", "L0_xattn_Wv", "L0_xattn_Wo"):
            a = a.T
        if a.ndim == 0:
            a = a.reshape(1)
        a = np.ascontiguousarray(a)
        arrays[f"in_{name}_dram"] = a
        dram[name] = nc.dram_tensor(f"in_{name}_dram", a.shape, mybir.dt.from_np(a.dtype), kind="ExternalInput").ap()
    out = nc.dram_tensor("out_0_dram", (B, S, H), F32, kind="ExternalOutput").ap()
    decoder_layer(nc, dram, out.rearrange("b s h -> (b s) h"))
    r = run_bass_kernel_spmd(nc, [arrays], core_ids=[0])
    return r.results[0]["out_0_dram"]
```

```python
from contextlib import ExitStack

import concourse.bass as bass
from concourse import mybir

F32 = mybir.dt.float32
FR = mybir.dt.float32r
U32 = mybir.dt.uint32
ALU = mybir.AluOpType
ACT = mybir.ActivationFunctionType
AX = mybir.AxisListType

P = 128
B = 4
S = 1024
H = 256
KH = H // P
TOK = B * S
CH = 512
NT = CH // P
CPB = S // CH
NCH = TOK // CH
NH = 16
HD = H // NH
GH = 4
NG = NH // GH
AH = 32
BH = 4
BHD = H // BH
KC = S // P
CAUSAL_W = 0.7
META_W = (0.9 - 0.8) / 0.2 * 0.3
S2 = 154
E2 = S2 // 2
EP = 96
LOWEST = -3e38
NE = 8
D = 512
FB = D // P
EPS = 1e-5


def mm3(pe, out, la, lb, ra, rb):
    steps = [(x, y) for k in range(len(la)) for x, y in ((la[k], ra[k]), (la[k], rb[k]), (lb[k], ra[k]))]
    for n, (x, y) in enumerate(steps):
        last = pe.matmul(out, x, y, start=(n == 0), stop=(n == len(steps) - 1))
    return last


def halves(t, *rest):
    return [t[(slice(None), k, *rest)] for k in range(KH)]


def column(v):
    return v.rearrange("(c p) -> p c", p=P)


def rows(v, n=P):
    return v.rearrange("(o n) -> o n", o=1).broadcast_to([n, v.shape[0]])


class Kit:

    def __init__(self, nc, stack, name):
        self.nc, self.stack, self.name = nc, stack, name

    def sb(self, name, shape, dt=F32):
        return self.stack.enter_context(self.nc.sbuf_tensor(f"{self.name}_{name}", shape, dt))

    def ps(self, name, shape, dt=F32):
        return self.stack.enter_context(self.nc.psum_tensor(f"{self.name}_{name}", shape, dt))

    def sem(self, name):
        return self.stack.enter_context(self.nc.semaphore(f"{self.name}_{name}"))


def identity_phase(nc, ident):
    with ExitStack() as stack:
        k = Kit(nc, stack, "id")
        ones = k.sem("ones")
        done = k.sem("done")
        block = stack.enter_context(nc.Block())

        @block.vector
        def _(dve):
            dve.memset(ident[:], 1.0).then_inc(ones, 1)

        @block.gpsimd
        def _(pool):
            pool.wait_ge(ones, 1)
            pool.affine_select(out=ident[:], in_=ident[:], compare_op=ALU.is_equal, fill=0.0, base=0,
                               pattern=[[-1, P]], channel_multiplier=1).then_inc(done, 1)
            pool.wait_ge(done, 1)


def input_projections(nc, A, scr, ident):
    with ExitStack() as stack:
        k = Kit(nc, stack, "in")
        Q0, K0, G0, CQ, CK, V0, CV = (n * H for n in range(7))
        NW = 7 * H
        raw, wa, wb = k.sb("raw", [P, KH, NW]), k.sb("wa", [P, KH, NW], FR), k.sb("wb", [P, KH, NW], FR)
        cg = k.sb("cg", [P, KH, NH])
        amr = k.sb("amr", [HD + 2, NH])
        am = k.sb("am", [HD + 2, H])
        cons = k.sb("cons", [HD + 2, 1])
        gbias = k.sb("gbias", [P, KH])
        bias = k.sb("bias", [P, 4, KH])
        vbias = k.sb("vbias", [P, 2 * H])
        xt = k.sb("xt", [P, NT, H])
        xa, xb = k.sb("xa", [P, CPB, KH, CH], FR), k.sb("xb", [P, CPB, KH, CH], FR)
        mod = k.sb("mod", [P, KH, CH])
        t = k.sb("t", [P, 4, CH])
        ab = k.sb("ab", [P, 4, 2, CH])
        v16 = k.sb("v16", [P, CPB, NT, NH, AH])
        v64 = k.sb("v64", [P, CPB, NT, H])
        psx = k.ps("psx", [P, KH, CH])
        pso = k.ps("pso", [P, 2, CH])
        psg = k.ps("psg", [P, KH])
        w_in, small_in, am_in, cons_in, x_in = (k.sem(n) for n in ("w_in", "small_in", "am_in", "cons_in", "x_in"))
        cg_done, wa_done, w_done, am_done, v_set, cons_set, g_ps, g_done = (
            k.sem(n) for n in ("cg_done", "wa_done", "w_done", "am_done", "v_set", "cons_set", "g_ps", "g_done"))
        xT_ps, xa_done, xb_done = k.sem("xT_ps"), k.sem("xa_done"), k.sem("xb_done")
        mm_done, ev_act, ev_dve = k.sem("mm_done"), k.sem("ev_act"), k.sem("ev_dve")
        a_done, b_done = k.sem("a_done"), k.sem("b_done")
        part_out = [k.sem(f"part_out{n}") for n in range(4)]
        v_out = [k.sem(f"v_out{n}") for n in range(2)]
        kinds = ["mod", "q", "mod", "q"] + ["lin"] * 6 + ["v"] * NT
        wcol = [G0, Q0, G0 + P, Q0 + P, K0, K0 + P, CQ, CQ + P, CK, CK + P]
        on_act = [x in ("mod", "lin") for x in kinds]
        nth = [sum(on_act[:n]) if on_act[n] else n - sum(on_act[:n]) for n in range(len(kinds))]
        NB = len(kinds)
        VS = 16 * (NT + 1)
        TURN = 8
        NA = sum(on_act)
        ND = NB - NA
        split = [n for n in range(NB) if kinds[n] in ("q", "lin")]
        NS = len(split)
        dest = [(scr["q"], 0), (scr["q"], 1), (scr["k"], 0), (scr["k"], 1), (scr["cq"], 0), (scr["cq"], 1),
                (scr["ck"], 0), (scr["ck"], 1)]
        x_v = A["x"].rearrange("b (c t p) h -> (b c) p t h", c=CPB, p=P)
        v_v = scr["v"].rearrange("(b g s) c -> b s g c", b=B, g=NG)
        block = stack.enter_context(nc.Block())

        @block.sync
        def _(sp):
            for src, col in ((A["L0_attn_Wq"], Q0), (A["L0_attn_Wk"], K0), (A["L0_attn_Wv"], V0)):
                sp.dma_start(raw[:, :, col:col + H], src.rearrange("(k p) n -> p k n", p=P)).then_inc(w_in, 16)
            ca = A["L0_attn_ca_Win"].rearrange("(k p) n -> p k n", p=P)
            sp.dma_start(raw[:, :, CQ:CQ + 2 * H], ca[:, :, 0:2 * H]).then_inc(w_in, 16)
            sp.dma_start(raw[:, :, CV:CV + H], ca[:, :, 2 * H:3 * H]).then_inc(w_in, 16)
            sp.dma_start(cg[:], A["L0_attn_cg_W"].rearrange("(k p) n -> p k n", p=P)).then_inc(small_in, 16)
            sp.dma_start(bias[:, 0, :], column(A["L0_attn_bq"]), allow_slow_non_contiguous=True).then_inc(small_in, 16)
            sp.dma_start(bias[:, 1, :], column(A["L0_attn_bk"]), allow_slow_non_contiguous=True).then_inc(small_in, 16)
            sp.dma_start(bias[:, 2, :], column(A["L0_attn_ca_bin"][0:H]), allow_slow_non_contiguous=True).then_inc(small_in, 16)
            sp.dma_start(bias[:, 3, :], column(A["L0_attn_ca_bin"][H:2 * H]), allow_slow_non_contiguous=True).then_inc(small_in, 16)
            sp.dma_start(vbias[:, 0:H], rows(A["L0_attn_bv"])).then_inc(small_in, 16)
            sp.dma_start(vbias[:, H:2 * H], rows(A["L0_attn_ca_bin"][2 * H:3 * H])).then_inc(small_in, 16)
            sp.dma_start(amr[0:HD, :], A["L0_attn_am_W"]).then_inc(am_in, 16)
            sp.dma_start(amr[HD:HD + 1, :], A["L0_attn_am_b"].rearrange("(o n) -> o n", o=1)).then_inc(am_in, 16)
            sp.dma_start(amr[HD + 1:HD + 2, :], A["L0_attn_cg_b"].rearrange("(o n) -> o n", o=1)).then_inc(am_in, 16)
            sp.wait_ge(cons_set, 1)
            sp.dma_start(cons[0:HD, :], A["L0_attn_cons_vec"].rearrange("(p o) -> p o", o=1), allow_slow_non_contiguous=True).then_inc(cons_in, 16)
            for n in range(4):
                sp.sem_inc(part_out[n], 16)
            for n in range(2):
                sp.sem_inc(v_out[n], VS)
            with sp.Fori(0, B) as b:
                for hf in range(CPB):
                    i = 2 * b + hf
                    for s in range(NS):
                        sp.wait_ge(b_done, 4 + NS * i + s + 1)
                        dst, j = dest[s]
                        sp.dma_start(dst[:, bass.ds(b * H + j * P, P), hf * CH:(hf + 1) * CH]
                                     .rearrange("a p n -> p a n"), ab[:, s % 4]).then_inc(part_out[s % 4], 16)
                    for tt in range(NT):
                        sp.wait_ge(ev_dve, 2 + ND * i + ND - NT + tt + 1)
                        tok = hf * CH + tt * P
                        sp.dma_start(v_v[bass.ds(b, 1), tok:tok + P].rearrange("o p g c -> p (o g) c"),
                                     v16[:, hf, tt].rearrange("p (g h) c -> p g (h c)", g=NG)).then_inc(v_out[hf], 16)
                    sp.dma_start(scr["cv"][bass.ds(b * S + hf * CH, CH)].rearrange("(t p) c -> p t c", p=P), v64[:, hf])\
                        .then_inc(v_out[hf], 16)
            for n in range(4):
                sp.wait_ge(part_out[n], 16 * (1 + NCH * NS // 4))
            for n in range(2):
                sp.wait_ge(v_out[n], VS * (1 + B))

        @block.gpsimd
        def _(pool):
            pool.memset(cons[:], 1.0).then_inc(cons_set, 1)
            pool.memset(v16[:], 0.0).then_inc(v_set, 1)
            pool.wait_ge(v_set, 1)
            pool.memset(v16[:, :, :, :, HD:HD + 1], 1.0).then_inc(v_set, 1)
            pool.sem_inc(b_done, 4)
            with pool.Fori(0, B) as b:
                for hf in range(CPB):
                    i = 2 * b + hf
                    for s in range(NS):
                        pool.wait_ge(a_done, NS * i + s + 1)
                        pool.tensor_tensor(ab[:, s % 4, 1], t[:, s % 4], ab[:, s % 4, 0], ALU.subtract).then_inc(b_done, 1)

        @block.tensor
        def _(pe):
            pe.wait_ge(cons_in, 16)
            pe.wait_ge(am_done, 1)
            for j in range(KH):
                last = pe.matmul(psg[:, j:j + 1], am[:, j * P:(j + 1) * P], cons[:], start=True, stop=True)
            last.then_inc(g_ps, 1)

            def turn(i):
                pe.wait_ge(x_in, 16 * i + 16)
                pe.wait_ge(xb_done, i + 1)
                for kh in range(KH):
                    for tt in range(NT):
                        last = pe.transpose(psx[:, kh, tt * P:(tt + 1) * P], xt[:, tt, kh * P:(kh + 1) * P], ident[:])
                last.then_inc(xT_ps, 1)

            def chunk(i, hf, more):
                pe.wait_ge(xb_done, i + 2)
                la, lb = halves(xa[:, hf]), halves(xb[:, hf])
                for n in range(NB):
                    if n == TURN and more:
                        turn(i + 1)
                    if n < 2:
                        pe.wait_ge(ev_dve, ND * i + n + 1)
                    else:
                        if on_act[n - 2]:
                            pe.wait_ge(ev_act, NA * i + nth[n - 2] + 1)
                        else:
                            pe.wait_ge(ev_dve, 2 + ND * i + nth[n - 2] + 1)
                    if kinds[n] == "v":
                        tok = slice((n - NB + NT) * P, (n - NB + NT + 1) * P)
                        mm3(pe, pso[:, n % 2], [x[:, tok] for x in la], [x[:, tok] for x in lb],
                            halves(wa, slice(V0, V0 + 2 * H)), halves(wb, slice(V0, V0 + 2 * H))).then_inc(mm_done, 1)
                    else:
                        w = slice(wcol[n], wcol[n] + P)
                        mm3(pe, pso[:, n % 2], halves(wa, w), halves(wb, w), la, lb).then_inc(mm_done, 1)

            turn(0)
            pe.wait_ge(w_done, 1)
            with pe.Fori(0, B - 1) as b:
                for hf in range(CPB):
                    chunk(2 * b + hf, hf, True)
            for hf in range(CPB):
                chunk(NCH - CPB + hf, hf, hf == 0)

        @block.scalar
        def _(act):
            def load(i):
                act.dma_start(xt[:], x_v[bass.ds(i, 1)].rearrange("o p t h -> p (o t) h")).then_inc(x_in, 16)

            def take(i, slot, more):
                act.wait_ge(xT_ps, i + 1)
                act.activation(xa[:, slot], psx[:], ACT.Copy).then_inc(xa_done, 1)
                if more:
                    load(i + 1)

            def chunk(i, hf, ahead):
                for n in range(NB):
                    if n == TURN and ahead:
                        take(i + 1, 1 - hf, ahead > 1)
                    if not on_act[n]:
                        continue
                    act.wait_ge(mm_done, NB * i + n + 1)
                    if kinds[n] == "mod":
                        j = n // 2
                        act.activation(mod[:, j], pso[:, n % 2], ACT.Sigmoid, bias=gbias[:, j:j + 1]).then_inc(ev_act, 1)
                    else:
                        s = split.index(n)
                        act.wait_ge(b_done, NS * i + s + 1)
                        act.activation(t[:, s % 4], pso[:, n % 2], ACT.Identity,
                                       bias=bias[:, s // 2, s % 2:s % 2 + 1]).then_inc(ev_act, 1)

            load(0)
            take(0, 0, True)
            act.wait_ge(small_in, 16 * 7)
            act.wait_ge(g_done, 1)
            with act.Fori(0, B - 1) as b:
                for hf in range(CPB):
                    chunk(2 * b + hf, hf, 2)
            for hf in range(CPB):
                chunk(NCH - CPB + hf, hf, 1 - hf)

        @block.vector
        def _(dve):
            dve.wait_ge(small_in, 16 * 7)
            dve.sem_inc(xb_done, 1)
            dve.sem_inc(ev_dve, 2)
            for kh in range(KH):
                dve.tensor_copy(raw[:, kh, G0:G0 + H].rearrange("p (h d) -> p h d", h=NH),
                                cg[:, kh].unsqueeze(2).broadcast_to([P, NH, HD])).then_inc(cg_done, 1)
            dve.wait_ge(am_in, 48)
            dve.tensor_copy(am[:].rearrange("p (h d) -> p h d", h=NH),
                            amr[:].unsqueeze(2).broadcast_to([HD + 2, NH, HD])).then_inc(am_done, 1)
            dve.wait_ge(w_in, 16 * 5)
            dve.wait_ge(cg_done, KH)
            dve.tensor_copy(wa[:], raw[:]).then_inc(wa_done, 1)
            dve.wait_ge(wa_done, 1)
            dve.tensor_tensor(wb[:], raw[:], wa[:].bitcast(F32), ALU.subtract).then_inc(w_done, 1)
            dve.wait_ge(g_ps, 1)
            dve.tensor_copy(gbias[:], psg[:]).then_inc(g_done, 1)
            dve.wait_ge(v_set, 2)

            def take(i, slot):
                dve.wait_ge(xa_done, i + 1)
                dve.tensor_tensor(xb[:, slot], psx[:], xa[:, slot].bitcast(F32), ALU.subtract).then_inc(xb_done, 1)

            take(0, 0)

            def chunk(b, hf, more):
                i = CPB * b + hf
                for n in range(NB):
                    if n == TURN and more:
                        take(i + 1, 1 - hf)
                    if kinds[n] == "mod":
                        continue
                    if kinds[n] == "q":
                        s, j = split.index(n), n // 2
                        dve.wait_ge(mm_done, NB * i + n + 1)
                        dve.wait_ge(ev_act, NA * i + nth[n - 1] + 1)
                        dve.wait_ge(b_done, NS * i + s + 1)
                        dve.scalar_tensor_tensor(out=t[:, s % 4], in0=pso[:, n % 2], scalar=bias[:, 0, j:j + 1],
                                                 in1=mod[:, j], op0=ALU.add, op1=ALU.mult).then_inc(ev_dve, 1)
                        dve.wait_ge(ev_dve, 2 + ND * i + nth[n] + 1)
                    if kinds[n] == "lin":
                        s = split.index(n)
                        dve.wait_ge(ev_act, NA * i + nth[n] + 1)
                    if kinds[n] != "v":
                        dve.wait_ge(part_out[s % 4], 16 * (NS // 4 * i + s // 4 + 1))
                        dve.tensor_copy(ab[:, s % 4, 0].bitcast(FR), t[:, s % 4]).then_inc(a_done, 1)
                        continue
                    tt = n - NB + NT
                    dve.wait_ge(mm_done, NB * i + n + 1)
                    if tt == 0:
                        dve.wait_ge(v_out[hf], VS * b + VS)
                    dve.tensor_tensor(v16[:, hf, tt, :, 0:HD], pso[:, n % 2, 0:H].rearrange("p (h d) -> p h d", h=NH),
                                      vbias[:, 0:H].rearrange("p (h d) -> p h d", h=NH), ALU.add)
                    dve.tensor_tensor(v64[:, hf, tt], pso[:, n % 2, H:2 * H], vbias[:, H:2 * H], ALU.add).then_inc(ev_dve, 1)

            with dve.Fori(0, B - 1) as b:
                for hf in range(CPB):
                    chunk(b, hf, True)
            for hf in range(CPB):
                chunk(B - 1, hf, hf == 0)


def attend_narrow(nc, scr):
    with ExitStack() as stack:
        k = Kit(nc, stack, "an")
        ONE, LAST = 4 * HD, 6 * HD
        MROW = LAST - 1
        NSTEP = CPB * KC
        RING = 3
        NST = GH * NSTEP
        qs, ks = k.sb("qs", [LAST, NG, GH, S], FR), k.sb("ks", [LAST, NG, GH, S], FR)
        vs = k.sb("vs", [P, NG, KC, GH * AH])
        probs = k.sb("probs", [P, 2, GH, CH])
        ev = k.sb("ev", [P, CPB, CH])
        m1 = k.sb("m1", [P, CPB, GH * NT])
        mneg, mturn = k.sb("mneg", [P, 32]), k.sb("mturn", [P, 32])
        mrows = k.sb("mrows", [P, CPB, 32], FR)
        pst = k.ps("pst", [P, RING, CH])
        psm = k.ps("psm", [P, 2, 2, CH])
        pacc = k.ps("pacc", [P, CH])
        filled_q, filled_k, mneg_set = k.sem("filled_q"), k.sem("filled_k"), k.sem("mneg_set")
        loaded = [k.sem(f"loaded{n}") for n in range(NG)]
        mrow_in = [[k.sem(f"mrow_in{n}{h}") for h in range(CPB)] for n in range(NG)]
        m_out = [k.sem(f"m_out{h}") for h in range(CPB)]
        ev_out = [k.sem(f"ev_out{h}") for h in range(CPB)]
        mx_ready, mx_done, m_chain, m_ready, row_moved = (
            k.sem(n) for n in ("mx_ready", "mx_done", "m_chain", "m_ready", "row_moved"))
        st_ready, exp_done, pv_done = (k.sem(n) for n in ("st_ready", "exp_done", "pv_done"))
        acc_ready, acc_act, acc_dve = k.sem("acc_ready"), k.sem("acc_act"), k.sem("acc_dve")
        LOADS = 9
        PV0 = NSTEP * (NG - 1) + 2
        mx_list = [(hq, j, i) for hq in range(CPB) for j in range(GH) for i in range(NT)]
        NM = len(mx_list)
        block = stack.enter_context(nc.Block())

        def last_use(n):
            return n - RING if n >= RING else max(m for m in range(NST) if m % RING == n) - NST

        @block.sync
        def _(sp):
            def load(G, slot):
                sp.wait_ge(pv_done, PV0 + NSTEP * (G - NG + 1))
                for r, (qp, kp) in enumerate(((0, 0), (0, 1), (1, 0), (1, 1))):
                    for dst, src, part in ((qs, scr["q"], qp), (ks, scr["k"], kp)):
                        sp.dma_start(dst[r * HD:(r + 1) * HD, slot].bitcast(F32),
                                     src[part, bass.ds(G * GH * HD, GH * HD)].rearrange("(j d) n -> d j n", j=GH))\
                            .then_inc(loaded[slot], 16)
                sp.dma_start(vs[:, slot], scr["v"][bass.ds(G * S, S)].rearrange("(c p) n -> p c n", p=P))\
                    .then_inc(loaded[slot], 16)

            def max_row(G, slot, uses, hq):
                sp.wait_ge(m_ready, CPB * G + hq + 1)
                turned = scr["m"][hq].rearrange("(c b r) -> b c r", b=4, r=32)
                for q in range(4):
                    sp.dma_start(turned[q], mrows[32 * q:32 * q + GH * NT, hq].bitcast(F32)).then_inc(m_out[hq], 16)
                sp.wait_ge(m_out[hq], 64 * G + 64)
                sp.dma_start(qs[MROW:LAST, slot, :, hq * CH:(hq + 1) * CH].bitcast(F32),
                             scr["m"][hq:hq + 1].rearrange("o (j n) -> o j n", j=GH)).then_inc(mrow_in[slot][hq], 16)
                sp.wait_ge(mrow_in[slot][hq], 16 * uses + 16)
                sp.sem_inc(row_moved, 1)

            def store(G, qh):
                if qh == 0:
                    sp.wait_ge(acc_act, G + 2)
                else:
                    sp.wait_ge(acc_dve, G + 2)
                sp.dma_start(scr["craw"][bass.ds(G * P, P), qh * CH:(qh + 1) * CH], ev[:, qh]).then_inc(ev_out[qh], 16)

            def group(b, g, ahead):
                G = b * NG + g
                if ahead >= 2:
                    load(G + 2, (g + 2) % NG)
                if ahead >= 1:
                    max_row(G + 1, (g + 1) % NG, b + (g + 1) // NG, 0)
                store(G, 0)
                if ahead >= 1:
                    max_row(G + 1, (g + 1) % NG, b + (g + 1) // NG, 1)
                store(G, 1)

            for qh in range(CPB):
                sp.sem_inc(ev_out[qh], 16)
            load(0, 0)
            load(1, 1)
            for hq in range(CPB):
                max_row(0, 0, 0, hq)
            with sp.Fori(0, B - 1) as b:
                for g in range(NG):
                    group(b, g, 2)
            for g in range(NG):
                group(B - 1, g, NG - 1 - g)
            for qh in range(CPB):
                sp.wait_ge(ev_out[qh], 16 + 16 * B * NG)

        @block.gpsimd
        def _(pool):
            for slot in range(NG):
                pool.memset(qs[ONE:LAST, slot].bitcast(F32), 0.0).then_inc(filled_q, 1)

        @block.tensor
        def _(pe):
            def maxima(G, slot, uses, n, kh):
                hq, j, i = mx_list[n]
                if n == 0 and kh == 0:
                    pe.wait_ge(filled_q, slot + 1)
                    pe.wait_ge(filled_k, slot + 1)
                    pe.wait_ge(loaded[slot], 16 * LOADS * uses + 16 * LOADS)
                if kh == 0:
                    pe.wait_ge(mx_done, NM * G + n + 1)
                q0 = (hq * NT + i) * P
                last = pe.matmul(psm[:, n % 2, kh], qs[0:MROW, slot, j, q0:q0 + P], ks[0:MROW, slot, j, kh * CH:(kh + 1) * CH],
                                 start=True, stop=True)
                if kh == 1:
                    last.then_inc(mx_ready, 1)

            def values(G, slot, s):
                qh, kc = divmod(s, KC)
                pe.wait_ge(exp_done, RING + GH * (NSTEP * G + s + 1))
                if kc == 0:
                    pe.wait_ge(*((acc_dve, G + 1) if qh == 0 else (acc_act, G + 2)))
                for j in range(GH):
                    last = pe.matmul(pacc[j * AH:(j + 1) * AH], vs[:, slot, kc, j * AH:(j + 1) * AH],
                                     probs[:, s % 2, j], start=(kc == 0), stop=(kc == KC - 1))
                last.then_inc(pv_done, 1)

            def group(b, g, more):
                G = b * NG + g
                nxt = (G + 1, (g + 1) % NG, b + (g + 1) // NG)
                for s in range(NSTEP):
                    qh, kc = divmod(s, KC)
                    if kc == 0:
                        pe.wait_ge(mrow_in[g][qh], 16 * b + 16)
                    for j in range(GH):
                        n = GH * s + j
                        pe.wait_ge(exp_done, RING + NST * G + last_use(n) + 1)
                        pe.matmul(pst[:, n % RING], ks[:, g, j, kc * P:(kc + 1) * P], qs[:, g, j, qh * CH:(qh + 1) * CH],
                                  start=True, stop=True).then_inc(st_ready, 1)
                        if s > 0 and j == 2:
                            values(G, g, s - 1)
                        if more and j % 2 == 0:
                            for kh in range(2):
                                maxima(*nxt, 2 * s + j // 2, kh)
                values(G, g, NSTEP - 1)

            pe.sem_inc(pv_done, PV0)
            for n in range(NM):
                for kh in range(2):
                    maxima(0, 0, 0, n, kh)
            with pe.Fori(0, B - 1) as b:
                for g in range(NG):
                    group(b, g, True)
            for g in range(NG):
                group(B - 1, g, g < NG - 1)

        @block.scalar
        def _(act):
            def group(b, g):
                G = b * NG + g
                for s in range(NSTEP):
                    for j in range(GH):
                        act.wait_ge(st_ready, GH * (NSTEP * G + s) + j + 1)
                        if j == 0:
                            act.wait_ge(pv_done, PV0 + NSTEP * G + s - 1)
                        act.activation(probs[:, s % 2, j], pst[:, (GH * s + j) % RING], ACT.Exp, scale=HD ** -0.5).then_inc(exp_done, 1)
                    if s == KC:
                        act.wait_ge(pv_done, PV0 + NSTEP * G + KC)
                        act.wait_ge(ev_out[0], 16 * G + 16)
                        act.activation(ev[:, 0], pacc[:], ACT.Copy).then_inc(acc_act, 1)

            act.sem_inc(exp_done, RING)
            act.sem_inc(acc_act, 1)
            with act.Fori(0, B) as b:
                for g in range(NG):
                    group(b, g)

        @block.vector
        def _(dve):
            def maxima(G, lo, hi):
                for n in range(lo, hi):
                    hq, j, i = mx_list[n]
                    dve.wait_ge(mx_ready, NM * G + n + 1)
                    col = j * NT + i
                    dve.tensor_reduce(m1[:, hq, col:col + 1], psm[:, n % 2], AX.XY, ALU.max).then_inc(mx_done, 1)

            def finish(G, hq, first):
                dve.wait_ge(mx_done, 2 + NM * G + (hq + 1) * NM // CPB)
                dve.tensor_scalar(mneg[:, 0:GH * NT], m1[:, hq], -1.0, None, ALU.mult).then_inc(m_chain, 1)
                dve.wait_ge(m_chain, 2 * (CPB * G + hq) + 1)
                dve.transpose(mturn[:], mneg[:]).then_inc(m_chain, 1)
                dve.wait_ge(m_chain, 2 * (CPB * G + hq) + 2)
                if not first:
                    dve.wait_ge(row_moved, CPB * (G - 1) + hq + 1)
                dve.tensor_copy(mrows[:, hq], mturn[:]).then_inc(m_ready, 1)

            def group(b, g, more):
                G = b * NG + g
                if more:
                    for hq in range(CPB):
                        maxima(G + 1, hq * NM // CPB, (hq + 1) * NM // CPB)
                        finish(G + 1, hq, False)
                dve.wait_ge(pv_done, PV0 + NSTEP * G + NSTEP)
                dve.wait_ge(ev_out[1], 16 * G + 16)
                dve.tensor_copy(ev[:, 1], pacc[:]).then_inc(acc_dve, 1)

            dve.sem_inc(mx_done, 2)
            dve.sem_inc(acc_dve, 1)
            dve.memset(mneg[:], 0.0).then_inc(mneg_set, 1)
            for slot in range(NG):
                dve.memset(ks[ONE:LAST, slot].bitcast(F32), 1.0).then_inc(filled_k, 1)
            dve.wait_ge(mneg_set, 1)
            for hq in range(CPB):
                maxima(0, hq * NM // CPB, (hq + 1) * NM // CPB)
                finish(0, hq, True)
            with dve.Fori(0, B - 1) as b:
                for g in range(NG):
                    group(b, g, True)
            for g in range(NG):
                group(B - 1, g, g < NG - 1)


def attend_wide(nc, src, name):
    with ExitStack() as stack:
        k = Kit(nc, stack, name)
        HP = 2
        NP = BH // HP
        NSTEP = CPB * KC
        MROW = P - 1
        RING = 4
        ADD0 = RING
        ONES = 32
        PV0 = NSTEP * (NP - 1) + RING
        LOADS = 7
        qs, ks = k.sb("qs", [P, NP, 2, HP, S], FR), k.sb("ks", [P, NP, 2, HP, S], FR)
        vs = k.sb("vs", [P, NP, KC, HP * BHD])
        ones = k.sb("ones", [P, ONES])
        probs = k.sb("probs", [P, RING, HP, CH])
        sums = k.sb("sums", [P, CPB, HP, CH])
        ev, evd = k.sb("ev", [P, CPB, CH]), k.sb("evd", [HP * ONES, CPB, CH])
        m1 = k.sb("m1", [P, CPB, HP * NT])
        mneg, mturn = k.sb("mneg", [P, 32]), k.sb("mturn", [P, 32])
        mrows = k.sb("mrows", [P, CPB, 32], FR)
        pst = k.ps("pst", [P, HP, CH])
        psm = k.ps("psm", [P, 2, 2, CH])
        pacc = k.ps("pacc", [P, CH])
        pden = k.ps("pden", [P, CH])
        filled_q, filled_k, mneg_set = k.sem("filled_q"), k.sem("filled_k"), k.sem("mneg_set")
        loaded = [k.sem(f"loaded{n}") for n in range(NP)]
        mrow_in = [[k.sem(f"mrow_in{n}{h}") for h in range(CPB)] for n in range(NP)]
        m_out = [k.sem(f"m_out{h}") for h in range(CPB)]
        ev_out = [k.sem(f"ev_out{h}") for h in range(CPB)]
        ones_set = k.sem("ones_set")
        mx_ready, mx_done, m_chain, m_ready, row_moved = (
            k.sem(n) for n in ("mx_ready", "mx_done", "m_chain", "m_ready", "row_moved"))
        st_ready, exp_done, pv_done, acc_out, den_ready, den_out = (
            k.sem(n) for n in ("st_ready", "exp_done", "pv_done", "acc_out", "den_ready", "den_out"))
        sum_done = [k.sem(f"sum_done{j}") for j in range(HP)]
        mx_list = [(hq, j, i) for hq in range(CPB) for j in range(HP) for i in range(NT)]
        NM = len(mx_list)
        HALF = NM // CPB
        FROM = 6
        upto = [0 if s < FROM else 2 * -(-(s - FROM + 1) * NM // (NSTEP - FROM)) for s in range(NSTEP)]
        block = stack.enter_context(nc.Block())

        def adds_before(G, s):
            x = s - RING
            x += x % KC == 0
            return ADD0 + (KC - 1) * (CPB * G + x // KC) + x % KC

        @block.sync
        def _(sp):
            def load(G, slot):
                sp.wait_ge(pv_done, PV0 + NSTEP * (G - NP + 1))
                for dst, src_, n, r, part in ((qs, "q", 0, 0, 0), (ks, "k", 0, 0, 0), (qs, "q", 0, 1, 0), (ks, "k", 0, 1, 1),
                                              (qs, "q", 1, 0, 1), (ks, "k", 1, 0, 0)):
                    sp.dma_start(dst[r * BHD:(r + 1) * BHD, slot, n].bitcast(F32),
                                 src[src_][part, bass.ds(G * P, P)].rearrange("(j d) n -> d j n", j=HP))\
                        .then_inc(loaded[slot], 16)

            def load_v(b, slot):
                sp.dma_start(vs[:, slot], src["v"][bass.ds(b * S, S), slot * P:(slot + 1) * P]
                             .rearrange("(c p) n -> p c n", p=P)).then_inc(loaded[slot], 16)

            def max_row(G, slot, uses, hq):
                sp.wait_ge(m_ready, CPB * G + hq + 1)
                turned = src["m"][hq].rearrange("(c b r) -> b c r", b=4, r=32)
                for q in range(4):
                    sp.dma_start(turned[q], mrows[32 * q:32 * q + HP * NT, hq].bitcast(F32)).then_inc(m_out[hq], 16)
                sp.wait_ge(m_out[hq], 64 * G + 64)
                sp.dma_start(qs[MROW:P, slot, 1, :, hq * CH:(hq + 1) * CH].bitcast(F32),
                             src["m"][hq:hq + 1].rearrange("o (j n) -> o j n", j=HP)).then_inc(mrow_in[slot][hq], 16)
                sp.wait_ge(mrow_in[slot][hq], 16 * uses + 16)
                sp.sem_inc(row_moved, 1)

            def store(G, qh):
                sp.wait_ge(acc_out, CPB * G + qh + 2)
                sp.wait_ge(den_out, CPB * G + qh + 2)
                sp.dma_start(src["out"][bass.ds(G * P, P), qh * CH:(qh + 1) * CH], ev[:, qh]).then_inc(ev_out[qh], 16)
                for j in range(HP):
                    sp.dma_start(src["den"][bass.ds(G * HP + j, 1), qh * CH:(qh + 1) * CH],
                                 evd[j * ONES:j * ONES + 1, qh]).then_inc(ev_out[qh], 16)

            def group(b, g, ahead):
                G = b * NP + g
                store(G, 0)
                if ahead >= 1:
                    max_row(G + 1, (g + 1) % NP, b + (g + 1) // NP, 0)
                if ahead >= 2:
                    load(G + NP, g)
                    load_v(b + 1, g)
                store(G, 1)
                if ahead >= 1:
                    max_row(G + 1, (g + 1) % NP, b + (g + 1) // NP, 1)

            for qh in range(CPB):
                sp.sem_inc(ev_out[qh], 48)
            for slot in range(NP):
                load(slot, slot)
                load_v(0, slot)
            for hq in range(CPB):
                max_row(0, 0, 0, hq)
            with sp.Fori(0, B - 1) as b:
                for g in range(NP):
                    group(b, g, 2)
            for g in range(NP):
                group(B - 1, g, NP - 1 - g)
            for qh in range(CPB):
                sp.wait_ge(ev_out[qh], 48 + 48 * B * NP)

        def add_up(eng, j, G, s):
            qh, kc = divmod(s, KC)
            if kc == 0:
                return
            eng.wait_ge(exp_done, 2 + HP * (NSTEP * G + s) + j + 1)
            adds = (KC - 1) * (CPB * G + qh)
            if kc == 1:
                eng.wait_ge(den_ready, CPB * G + qh + 1)
                before = probs[:, (s - 1) % RING, j]
            else:
                eng.wait_ge(sum_done[j], ADD0 + adds + kc - 1)
                before = sums[:, qh, j]
            eng.tensor_tensor(sums[:, qh, j], before, probs[:, s % RING, j], ALU.add).then_inc(sum_done[j], 1)

        @block.gpsimd
        def _(pool):
            for slot in range(NP):
                pool.memset(qs[BHD:P, slot, 1].bitcast(F32), 0.0).then_inc(filled_q, 1)
            pool.sem_inc(sum_done[1], ADD0)
            pool.wait_ge(filled_q, NP)
            with pool.Fori(0, B) as b:
                for g in range(NP):
                    for s in range(NSTEP):
                        add_up(pool, 1, b * NP + g, s)

        @block.tensor
        def _(pe):
            def maxima(G, slot, uses, lo, hi):
                for u in range(lo, hi):
                    n, kh = divmod(u, 2)
                    hq, j, i = mx_list[n]
                    if u == 0:
                        pe.wait_ge(filled_q, slot + 1)
                        pe.wait_ge(filled_k, slot + 1)
                        pe.wait_ge(loaded[slot], 16 * LOADS * uses + 16 * LOADS)
                    if kh == 0:
                        pe.wait_ge(mx_done, NM * G + n + 1)
                    q0 = (hq * NT + i) * P
                    last = pe.matmul(psm[:, n % 2, kh], qs[:, slot, 0, j, q0:q0 + P], ks[:, slot, 0, j, kh * CH:(kh + 1) * CH],
                                     start=True, stop=True)
                    if kh == 1:
                        last.then_inc(mx_ready, 1)

            def values(G, slot, s):
                qh, kc = divmod(s, KC)
                pe.wait_ge(exp_done, 2 + HP * (NSTEP * G + s + 1))
                if kc == 0:
                    pe.wait_ge(acc_out, CPB * G + qh + 1)
                for j in range(HP):
                    last = pe.matmul(pacc[j * BHD:(j + 1) * BHD], vs[:, slot, kc, j * BHD:(j + 1) * BHD], probs[:, s % RING, j],
                                     start=(kc == 0), stop=(kc == KC - 1))
                last.then_inc(pv_done, 1)

            def row_sums(G, qh):
                for j in range(HP):
                    pe.wait_ge(sum_done[j], ADD0 + (KC - 1) * (CPB * G + qh + 1))
                pe.wait_ge(den_out, CPB * G + qh + 1)
                for j in range(HP):
                    last = pe.matmul(pden[j * ONES:(j + 1) * ONES], ones[:], sums[:, qh, j], start=True, stop=True)
                last.then_inc(den_ready, 1)

            def group(b, g, more):
                G = b * NP + g
                nxt = (G + 1, (g + 1) % NP, b + (g + 1) // NP)
                for s in range(NSTEP):
                    qh, kc = divmod(s, KC)
                    if kc == 0:
                        pe.wait_ge(mrow_in[g][qh], 16 * b + 16)
                    lo, hi = (upto[s - 1] if s else 0), upto[s]
                    for j in range(HP):
                        pe.wait_ge(exp_done, HP * (NSTEP * G + s) + j + 1)
                        for n in range(2):
                            last = pe.matmul(pst[:, j], ks[:, g, n, j, kc * P:(kc + 1) * P],
                                             qs[:, g, n, j, qh * CH:(qh + 1) * CH], start=(n == 0), stop=(n == 1))
                        last.then_inc(st_ready, 1)
                        if more:
                            mid = (lo + hi) // 2
                            maxima(*nxt, *((lo, mid) if j == 0 else (mid, hi)))
                        if s > 0 and j == 1:
                            values(G, g, s - 1)
                    if s == KC + 2:
                        row_sums(G, 0)
                values(G, g, NSTEP - 1)
                row_sums(G, 1)

            pe.sem_inc(pv_done, PV0)
            pe.sem_inc(den_ready, 2)
            pe.wait_ge(ones_set, 1)
            maxima(0, 0, 0, 0, 2 * NM)
            with pe.Fori(0, B - 1) as b:
                for g in range(NP):
                    group(b, g, True)
            for g in range(NP):
                group(B - 1, g, g < NP - 1)

        @block.scalar
        def _(act):
            def copy_out(G, qh):
                act.wait_ge(pv_done, PV0 + NSTEP * G + KC * (qh + 1))
                act.wait_ge(ev_out[qh], 48 * G + 48)
                act.activation(ev[:, qh], pacc[:], ACT.Copy).then_inc(acc_out, 1)

            act.sem_inc(exp_done, 2)
            act.sem_inc(acc_out, 1)
            with act.Fori(0, B) as b:
                for g in range(NP):
                    G = b * NP + g
                    for s in range(NSTEP):
                        qh, kc = divmod(s, KC)
                        for j in range(HP):
                            act.wait_ge(st_ready, HP * (NSTEP * G + s) + j + 1)
                            if j == 0:
                                act.wait_ge(pv_done, PV0 + NSTEP * G + s - RING + 1)
                            act.wait_ge(sum_done[j], adds_before(G, s))
                            act.activation(probs[:, s % RING, j], pst[:, j], ACT.Exp, scale=BHD ** -0.5).then_inc(exp_done, 1)
                        if s == KC:
                            copy_out(G, 0)
                    copy_out(G, 1)

        @block.vector
        def _(dve):
            def maxima(G, lo, hi):
                for n in range(lo // 2, hi // 2):
                    hq, j, i = mx_list[n]
                    dve.wait_ge(mx_ready, NM * G + n + 1)
                    col = j * NT + i
                    dve.tensor_reduce(m1[:, hq, col:col + 1], psm[:, n % 2], AX.XY, ALU.max).then_inc(mx_done, 1)
                    if n % HALF == HALF - 1:
                        finish(G, hq)

            def finish(G, hq):
                dve.wait_ge(mx_done, 2 + NM * G + (hq + 1) * HALF)
                dve.tensor_scalar(mneg[:, 0:HP * NT], m1[:, hq], -1.0, None, ALU.mult).then_inc(m_chain, 1)
                dve.wait_ge(m_chain, 2 * (CPB * G + hq) + 1)
                dve.transpose(mturn[:], mneg[:]).then_inc(m_chain, 1)
                dve.wait_ge(m_chain, 2 * (CPB * G + hq) + 2)
                if not (isinstance(G, int) and G == 0):
                    dve.wait_ge(row_moved, CPB * (G - 1) + hq + 1)
                dve.tensor_copy(mrows[:, hq], mturn[:]).then_inc(m_ready, 1)

            def copy_out(G, qh):
                dve.wait_ge(den_ready, 2 + CPB * G + qh + 1)
                dve.wait_ge(ev_out[qh], 48 * G + 48)
                dve.tensor_copy(evd[:, qh], pden[0:HP * ONES]).then_inc(den_out, 1)

            def group(b, g, more):
                G = b * NP + g
                for s in range(NSTEP):
                    add_up(dve, 0, G, s)
                    if s == KC + 3:
                        copy_out(G, 0)
                    if more:
                        maxima(G + 1, upto[s - 1] if s else 0, upto[s])
                copy_out(G, 1)

            dve.sem_inc(mx_done, 2)
            dve.sem_inc(den_out, 1)
            dve.sem_inc(sum_done[0], ADD0)
            dve.memset(ones[:], 1.0).then_inc(ones_set, 1)
            dve.memset(mneg[:], 0.0).then_inc(mneg_set, 1)
            for slot in range(NP):
                dve.memset(ks[BHD:P, slot, 1].bitcast(F32), 1.0).then_inc(filled_k, 1)
            dve.wait_ge(mneg_set, 1)
            maxima(0, 0, 2 * NM)
            with dve.Fori(0, B - 1) as b:
                for g in range(NP):
                    group(b, g, True)
            for g in range(NP):
                group(B - 1, g, g < NP - 1)


def selector_steps(pool, sel, blocks, made):
    for n, (row0, width, col0) in enumerate(blocks):
        view = sel[0:32, n]
        pool.affine_select(out=view, in_=view, compare_op=ALU.is_ge, fill=0.0, base=col0 + width * row0,
                           pattern=[[1, P]], channel_multiplier=-width).then_inc(made, 1)
        pool.wait_ge(made, 2 * n + 2)
        pool.affine_select(out=view, in_=view, compare_op=ALU.is_ge, fill=0.0, base=width - 1 - col0 - width * row0,
                           pattern=[[-1, P]], channel_multiplier=width).then_inc(made, 1)
        pool.wait_ge(made, 2 * n + 3)


def join_attention(nc, A, scr):
    with ExitStack() as stack:
        k = Kit(nc, stack, "jo")
        NR = NH + BH
        raw = k.sb("raw", [P, KH, 4 * H])
        wa, wb = k.sb("wa", [P, KH, 4 * H], FR), k.sb("wb", [P, KH, 4 * H], FR)
        W0, Q0, K0, V0 = 0, H, 2 * H, 3 * H
        boraw, bo = k.sb("boraw", [P, KH]), k.sb("bo", [P, KH])
        bias = k.sb("bias", [P, 2, KH])
        vbias = k.sb("vbias", [P, H])
        self32, sel = k.sb("self32", [32, 4, P]), k.sb("sel", [P, 4, P], FR)
        den, rden = k.sb("den", [NR, 2, CH]), k.sb("rden", [NR, 2, CH])
        rsplit = k.sb("rsplit", [P, 2, CH], FR)
        r16, c64 = k.sb("r16", [P, 2, KH, CH]), k.sb("c64", [P, 2, KH, CH])
        rn, cn = k.sb("rn", [P, 2, KH, CH]), k.sb("cn", [P, 2, KH, CH])
        cna, cnb = k.sb("cna", [P, 2, KH, CH], FR), k.sb("cnb", [P, 2, KH, CH], FR)
        rb = k.sb("rb", [P, 2, KH, CH])
        comb = k.sb("comb", [P, 2, KH, CH])
        coa, cob = k.sb("coa", [P, 2, KH, CH], FR), k.sb("cob", [P, 2, KH, CH], FR)
        t = k.sb("t", [P, 4, CH])
        ab = k.sb("ab", [P, 4, 2, CH])
        v64 = k.sb("v64", [P, CPB, NT, H])
        pb, pw, po = k.ps("pb", [P, 2, CH]), k.ps("pw", [P, 2, KH, CH]), k.ps("po", [P, 2, CH])
        w_in, small_in = k.sem("w_in"), k.sem("small_in")
        raw_in = [k.sem(f"raw_in{n}") for n in range(2)]
        wa_done, w_done, bo_done, sel_set, sel_made, sel_done, rs_zero = (k.sem(n) for n in (
            "wa_done", "w_done", "bo_done", "sel_set", "sel_made", "sel_done", "rs_zero"))
        recip_done, ra_done, r_ready, pb_ready, pb_done = (
            k.sem(n) for n in ("recip_done", "ra_done", "r_ready", "pb_ready", "pb_done"))
        cna_done, cnb_done, pw_ready, rb_done, comb_done, coa_done, cob_done = (k.sem(n) for n in (
            "cna_done", "cnb_done", "pw_ready", "rb_done", "comb_done", "coa_done", "cob_done"))
        po_ready, t_done, a_done, b_done, v_done = (k.sem(n) for n in ("po_ready", "t_done", "a_done", "b_done", "v_done"))
        comb_out = [k.sem(f"comb_out{n}") for n in range(2)]
        part_out = [k.sem(f"part_out{n}") for n in range(4)]
        v_out = [k.sem(f"v_out{n}") for n in range(2)]
        RAWS = KH + 3
        craw_v = scr["craw"].rearrange("(x r) n -> x r n", r=AH)
        dest = [(scr["mq"], 0), (scr["mq"], 1), (scr["mk"], 0), (scr["mk"], 1)]
        spread = [(hf, n) for first in (KH, 0) for hf in range(CPB) for n in range(first, first + KH)]
        NSP = len(spread)
        block = stack.enter_context(nc.Block())

        @block.sync
        def _(sp):
            mc = A["L0_attn_mc_Win"].rearrange("(k p) n -> p k n", p=P)
            sp.dma_start(raw[:, :, W0:W0 + H], A["L0_attn_ca_Wout"].rearrange("(k p) n -> p k n", p=P)).then_inc(w_in, 16)
            sp.dma_start(raw[:, :, Q0:Q0 + 3 * H], mc).then_inc(w_in, 16)
            sp.dma_start(boraw[:], column(A["L0_attn_ca_bout"]), allow_slow_non_contiguous=True).then_inc(small_in, 16)
            sp.dma_start(bias[:, 0], column(A["L0_attn_mc_bin"][0:H]), allow_slow_non_contiguous=True).then_inc(small_in, 16)
            sp.dma_start(bias[:, 1], column(A["L0_attn_mc_bin"][H:2 * H]), allow_slow_non_contiguous=True).then_inc(small_in, 16)
            sp.dma_start(vbias[:], rows(A["L0_attn_mc_bin"][2 * H:3 * H])).then_inc(small_in, 16)
            for n in range(4):
                sp.sem_inc(part_out[n], 16)
            for n in range(2):
                sp.sem_inc(v_out[n], 16)
                sp.sem_inc(comb_out[n], 16)

            def load(b, hf):
                sp.wait_ge(pb_done, NSP * b + NSP)
                cols = slice(hf * CH, (hf + 1) * CH)
                for c in range(KH):
                    sp.dma_start(r16[:, hf, c], craw_v[bass.ds(b * NH + c * NH // KH, NH // KH), 0:HD, cols]).then_inc(raw_in[hf], 16)
                sp.dma_start(den[0:NH, hf], craw_v[bass.ds(b * NH, NH), HD, cols]).then_inc(raw_in[hf], 16)
                sp.dma_start(den[NH:NR, hf], scr["cden"][bass.ds(b * BH, BH), cols]).then_inc(raw_in[hf], 16)
                sp.dma_start(c64[:, hf], scr["cout"][bass.ds(b * H, H), cols].rearrange("(c p) n -> p c n", p=P))\
                    .then_inc(raw_in[hf], 16)

            def store_joined(b, hf):
                sp.wait_ge(comb_done, KH * (2 * b + hf) + KH)
                sp.dma_start(scr["comb"][bass.ds(b * H, H), hf * CH:(hf + 1) * CH].rearrange("(c p) n -> p c n", p=P),
                             comb[:, hf]).then_inc(comb_out[hf], 16)

            def store_projected(b, hf):
                i = 2 * b + hf
                for s in range(4):
                    sp.wait_ge(b_done, 4 + 4 * i + s + 1)
                    dst, j = dest[s]
                    sp.dma_start(dst[:, bass.ds(b * H + j * P, P), hf * CH:(hf + 1) * CH].rearrange("a p n -> p a n"), ab[:, s])\
                        .then_inc(part_out[s], 16)
                sp.wait_ge(v_done, NT * i + NT)
                sp.dma_start(scr["mv"][bass.ds(b * S + hf * CH, CH)].rearrange("(t p) c -> p t c", p=P), v64[:, hf])\
                    .then_inc(v_out[hf], 16)

            def batch(b, ahead):
                if ahead >= 2:
                    for hf in range(CPB):
                        load(b + 2, hf)
                for hf in range(CPB):
                    store_projected(b, hf)
                    if ahead >= 1:
                        store_joined(b + 1, hf)

            for b in range(2):
                for hf in range(CPB):
                    load(b, hf)
            for hf in range(CPB):
                store_joined(0, hf)
            with sp.Fori(0, B - 2) as b:
                batch(b, 2)
            for b in range(B - 2, B):
                batch(b, B - 1 - b)
            for n in range(4):
                sp.wait_ge(part_out[n], 16 + 16 * NCH)
            for n in range(2):
                sp.wait_ge(v_out[n], 16 + 16 * B)
                sp.wait_ge(comb_out[n], 16 + 16 * B)

        @block.gpsimd
        def _(pool):
            pool.memset(self32[:], 1.0).then_inc(sel_made, 1)
            pool.wait_ge(sel_made, 1)
            selector_steps(pool, self32, ((0, HD, 0), (0, HD, P), (NH, BHD, 0), (NH, BHD, P)), sel_made)
            pool.sem_inc(b_done, 4)

            def join(b, hf):
                for c in range(KH):
                    pool.wait_ge(coa_done, KH * (2 * b + hf) + c + 1)
                    pool.tensor_tensor(cob[:, hf, c], comb[:, hf, c], coa[:, hf, c].bitcast(F32), ALU.subtract)\
                        .then_inc(cob_done, 1)

            def project(b, hf):
                for s in range(4):
                    pool.wait_ge(a_done, 4 * (2 * b + hf) + s + 1)
                    pool.tensor_tensor(ab[:, s, 1], t[:, s], ab[:, s, 0], ALU.subtract).then_inc(b_done, 1)

            def batch(b, more):
                for hf in range(CPB):
                    project(b, hf)
                    if more:
                        join(b + 1, hf)

            for hf in range(CPB):
                join(0, hf)
            with pool.Fori(0, B - 1) as b:
                batch(b, True)
            batch(B - 1, False)

        @block.tensor
        def _(pe):
            pe.wait_ge(w_done, 1)
            pe.wait_ge(sel_done, 2)

            def spread_sums(b):
                for m, (hf, n) in enumerate(spread):
                    pe.wait_ge(r_ready, 2 * b + hf + 1)
                    pe.wait_ge(pb_done, NSP + NSP * b + m - 1)
                    pe.matmul(pb[:, m % 2], sel[:, n], rsplit[:, hf], start=True, stop=True).then_inc(pb_ready, 1)

            def join(b, hf):
                pe.wait_ge(cnb_done, KH * (2 * b + hf) + KH)
                for c in range(KH):
                    w = slice(W0 + c * P, W0 + (c + 1) * P)
                    mm3(pe, pw[:, hf, c], halves(wa, w), halves(wb, w), [cna[:, hf, x] for x in range(KH)],
                        [cnb[:, hf, x] for x in range(KH)]).then_inc(pw_ready, 1)

            def project(b, hf):
                i = 2 * b + hf
                pe.wait_ge(cob_done, KH * i + KH)
                xa, xb = [coa[:, hf, c] for c in range(KH)], [cob[:, hf, c] for c in range(KH)]
                for n in range(4 + NT):
                    if 2 <= n < 6:
                        pe.wait_ge(t_done, 4 * i + n - 1)
                    elif n >= 6:
                        pe.wait_ge(v_done, NT * i + n - 5)
                    if n < 4:
                        w = slice(Q0 + n * P, Q0 + (n + 1) * P)
                        mm3(pe, po[:, n % 2], halves(wa, w), halves(wb, w), xa, xb).then_inc(po_ready, 1)
                    else:
                        tok = slice((n - 4) * P, (n - 3) * P)
                        mm3(pe, po[:, n % 2, 0:H], [x[:, tok] for x in xa], [x[:, tok] for x in xb],
                            halves(wa, slice(V0, V0 + H)), halves(wb, slice(V0, V0 + H))).then_inc(po_ready, 1)

            def batch(b, more):
                if more:
                    spread_sums(b + 1)
                for hf in range(CPB):
                    project(b, hf)
                    if more:
                        join(b + 1, hf)
                    pe.wait_ge(v_done, NT * (2 * b + hf) + NT)

            spread_sums(0)
            for hf in range(CPB):
                join(0, hf)
            with pe.Fori(0, B - 1) as b:
                batch(b, True)
            batch(B - 1, False)

        @block.scalar
        def _(act):
            act.wait_ge(small_in, 64)
            act.wait_ge(bo_done, 1)

            def spread_sums(b):
                for m, (hf, n) in enumerate(spread):
                    act.wait_ge(pb_done, NSP + NSP * b + m + 1)
                    if n >= KH:
                        act.activation(cna[:, hf, n - KH], cn[:, hf, n - KH], ACT.Copy).then_inc(cna_done, 1)
                    else:
                        act.activation(rb[:, hf, n], rn[:, hf, n], ACT.Identity, bias=bo[:, n:n + 1]).then_inc(rb_done, 1)

            def join(b, hf):
                for c in range(KH):
                    act.wait_ge(comb_done, KH * (2 * b + hf) + c + 1)
                    act.activation(coa[:, hf, c], comb[:, hf, c], ACT.Copy).then_inc(coa_done, 1)

            def project(b, hf):
                i = 2 * b + hf
                for s in range(4):
                    act.wait_ge(po_ready, (4 + NT) * i + s + 1)
                    act.wait_ge(b_done, 4 * i + s + 1)
                    act.activation(t[:, s], po[:, s % 2], ACT.Identity, bias=bias[:, s // 2, s % 2:s % 2 + 1])\
                        .then_inc(t_done, 1)

            def batch(b, more):
                if more:
                    spread_sums(b + 1)
                for hf in range(CPB):
                    project(b, hf)
                    if more:
                        join(b + 1, hf)

            spread_sums(0)
            for hf in range(CPB):
                join(0, hf)
            with act.Fori(0, B - 1) as b:
                batch(b, True)
            batch(B - 1, False)

        @block.vector
        def _(dve):
            dve.sem_inc(pb_done, NSP)
            dve.memset(rsplit[:].bitcast(F32), 0.0).then_inc(rs_zero, 1)
            dve.memset(sel[:].bitcast(F32), 0.0).then_inc(sel_set, 1)
            dve.wait_ge(w_in, 32)
            dve.tensor_copy(wa[:], raw[:]).then_inc(wa_done, 1)
            dve.wait_ge(wa_done, 1)
            dve.tensor_tensor(wb[:], raw[:], wa[:].bitcast(F32), ALU.subtract).then_inc(w_done, 1)
            dve.wait_ge(small_in, 64)
            dve.tensor_scalar(bo[:], boraw[:], CAUSAL_W, None, ALU.mult).then_inc(bo_done, 1)
            dve.wait_ge(sel_made, 9)
            dve.wait_ge(sel_set, 1)
            dve.tensor_copy(sel[0:32], self32[:]).then_inc(sel_done, 1)
            dve.tensor_copy(sel[32:64], self32[:]).then_inc(sel_done, 1)
            dve.wait_ge(rs_zero, 1)

            def reciprocals(b):
                for hf in range(CPB):
                    dve.wait_ge(raw_in[hf], 16 * RAWS * (b + 1))
                    dve.reciprocal(rden[:, hf], den[:, hf]).then_inc(recip_done, 1)

            def spread_sums(b):
                for hf in range(CPB):
                    i = 2 * b + hf
                    dve.wait_ge(recip_done, i + 1)
                    dve.tensor_copy(rsplit[0:NR, hf], rden[:, hf]).then_inc(ra_done, 1)
                    dve.wait_ge(ra_done, i + 1)
                    dve.tensor_tensor(rsplit[32:32 + NR, hf], rden[:, hf], rsplit[0:NR, hf].bitcast(F32), ALU.subtract)\
                        .then_inc(r_ready, 1)
                for m, (hf, n) in enumerate(spread):
                    if m == NSP // 2:
                        for x in range(2 * KH):
                            dve.wait_ge(cna_done, 2 * KH * b + x + 1)
                            at = (slice(None), x // KH, x % KH)
                            dve.tensor_tensor(cnb[at], cn[at], cna[at].bitcast(F32), ALU.subtract).then_inc(cnb_done, 1)
                    dve.wait_ge(pb_ready, NSP * b + m + 1)
                    if n >= KH:
                        dve.tensor_tensor(cn[:, hf, n - KH], c64[:, hf, n - KH], pb[:, m % 2], ALU.mult).then_inc(pb_done, 1)
                    else:
                        dve.scalar_tensor_tensor(out=rn[:, hf, n], in0=r16[:, hf, n], scalar=1.0 - CAUSAL_W,
                                                 in1=pb[:, m % 2], op0=ALU.mult, op1=ALU.mult).then_inc(pb_done, 1)

            def join(b, hf):
                i = 2 * b + hf
                dve.wait_ge(comb_out[hf], 16 * b + 16)
                for c in range(KH):
                    dve.wait_ge(rb_done, KH * i + c + 1)
                    dve.wait_ge(pw_ready, KH * i + c + 1)
                    dve.scalar_tensor_tensor(out=comb[:, hf, c], in0=pw[:, hf, c], scalar=CAUSAL_W, in1=rb[:, hf, c],
                                             op0=ALU.mult, op1=ALU.add).then_inc(comb_done, 1)

            def project(b, hf):
                i = 2 * b + hf
                for s in range(4):
                    dve.wait_ge(t_done, 4 * i + s + 1)
                    dve.wait_ge(part_out[s], 16 * i + 16)
                    dve.tensor_copy(ab[:, s, 0].bitcast(FR), t[:, s]).then_inc(a_done, 1)
                dve.wait_ge(v_out[hf], 16 * b + 16)
                for tt in range(NT):
                    dve.wait_ge(po_ready, (4 + NT) * i + 4 + tt + 1)
                    dve.tensor_tensor(v64[:, hf, tt], po[:, tt % 2, 0:H], vbias[:], ALU.add).then_inc(v_done, 1)

            def batch(b, ahead):
                if ahead >= 1:
                    spread_sums(b + 1)
                for hf in range(CPB):
                    project(b, hf)
                    if ahead >= 1:
                        join(b + 1, hf)
                if ahead >= 2:
                    reciprocals(b + 2)

            reciprocals(0)
            spread_sums(0)
            for hf in range(CPB):
                join(0, hf)
            reciprocals(1)
            with dve.Fori(0, B - 2) as b:
                batch(b, 2)
            for b in range(B - 2, B):
                batch(b, B - 1 - b)


def project_and_norm(nc, A, scr, ident, cross, keep=None):
    with ExitStack() as stack:
        k = Kit(nc, stack, "pc" if cross else "ps")
        NR, width = (NH, HD) if cross else (BH, BHD)
        NW = H if cross else 3 * H
        Y0, W0, Q0 = 0, H, 2 * H
        raw = k.sb("raw", [P, KH, NW])
        wa, wb = k.sb("wa", [P, KH, NW], FR), k.sb("wb", [P, KH, NW], FR)
        small_raw, small = k.sb("small_raw", [P, 2, KH]), k.sb("small", [P, 2, KH])
        obias = k.sb("obias", [P, H])
        eps = k.sb("eps", [P, 1])
        self32, sel = k.sb("self32", [32, KH, P]), k.sb("sel", [P, KH, P], FR)
        den, rden = k.sb("den", [NR, 2, CH]), k.sb("rden", [NR, 2, CH])
        rsplit = k.sb("rsplit", [P, 2, CH], FR)
        c64 = k.sb("c64", [P, 2, KH, CH])
        xt = k.sb("xt", [P, 2, NT, H])
        cn = k.sb("cn", [P, 2, KH, CH])
        cna, cnb = k.sb("cna", [P, 2, KH, CH], FR), k.sb("cnb", [P, 2, KH, CH], FR)
        res = k.sb("res", [P, 2, H])
        stats, mv, rstd = k.sb("stats", [P, 2, 6]), k.sb("mv", [P, 2, 2]), k.sb("rstd", [P, 2, 2])
        x1 = k.sb("x1", [P, 2, NT, H])
        if not cross:
            comb = k.sb("comb", [P, 2, KH, CH])
            z = k.sb("z", [P, 2, KH, CH])
            za, zb = k.sb("za", [P, 2, KH, CH], FR), k.sb("zb", [P, 2, KH, CH], FR)
            xa, xb = k.sb("xa", [P, KH, CH], FR), k.sb("xb", [P, KH, CH], FR)
            t, ab = k.sb("t", [P, KH, CH]), k.sb("ab", [P, KH, 2, CH])
        pb, pw, po, px = (k.ps("pb", [P, 2, CH]), k.ps("pw", [P, KH, CH]), k.ps("po", [P, 2, CH]), k.ps("px", [P, KH, CH]))
        w_in, small_in = k.sem("w_in"), k.sem("small_in")
        raw_in = [k.sem(f"raw_in{n}") for n in range(2)]
        res_in = [k.sem(f"res_in{n}") for n in range(2)]
        names = ("wa_done", "w_done", "small_done", "sel_set", "sel_made", "sel_done", "rs_zero", "eps_set",
                 "recip_done", "ra_done", "r_ready", "pb_ready", "pb_done", "cna_done", "cnb_done", "pw_ready", "mixed", "z_done",
                 "za_done", "zb_done", "xo_done", "y_ready", "y_done", "n_chain", "stats_seen", "var_done", "std_done", "x1_done",
                 "xT_ready", "xa_done", "xb_done", "po_ready", "t_done", "a_done", "b_done")
        (wa_done, w_done, small_done, sel_set, sel_made, sel_done, rs_zero, eps_set, recip_done, ra_done, r_ready, pb_ready, pb_done,
         cna_done, cnb_done, pw_ready, mixed, z_done, za_done, zb_done, xo_done, y_ready, y_done, n_chain, stats_seen, var_done,
         std_done, x1_done, xT_ready, xa_done, xb_done, po_ready, t_done, a_done, b_done) = (k.sem(n) for n in names)
        x1_out = [k.sem(f"x1_out{n}") for n in range(2)]
        part_out = [k.sem(f"part_out{n}") for n in range(2)]
        RAWS = KH + 1 if cross else 3
        wname = "L0_xattn_Wo" if cross else "L0_attn_Wo"
        residual = scr["x1"] if cross else A["x"].rearrange("b s h -> (b s) h")
        block = stack.enter_context(nc.Block())

        @block.sync
        def _(sp):
            sp.dma_start(raw[:, :, Y0:Y0 + H], A[wname].rearrange("(k p) n -> p k n", p=P)).then_inc(w_in, 16)
            sp.dma_start(obias[:], rows(A["L0_xattn_bo" if cross else "L0_attn_bo"])).then_inc(small_in, 16)
            if not cross:
                sp.dma_start(raw[:, :, W0:W0 + H], A["L0_attn_mc_Wout"].rearrange("(k p) n -> p k n", p=P)).then_inc(w_in, 16)
                sp.dma_start(raw[:, :, Q0:Q0 + H], A["L0_xattn_Wq"].rearrange("(k p) n -> p k n", p=P)).then_inc(w_in, 16)
                sp.dma_start(small_raw[:, 0], column(A["L0_attn_mc_bout"]), allow_slow_non_contiguous=True).then_inc(small_in, 16)
                sp.dma_start(small_raw[:, 1], column(A["L0_xattn_bq"]), allow_slow_non_contiguous=True).then_inc(small_in, 16)
            for n in range(2):
                sp.sem_inc(x1_out[n], 16)
                sp.sem_inc(part_out[n], 16)

            def load(b, hf):
                sp.wait_ge(pb_done, 4 * b + 4)
                if not cross:
                    sp.wait_ge(mixed, 4 * b + 4)
                cols = slice(hf * CH, (hf + 1) * CH)
                if cross:
                    craw_v = scr["craw"].rearrange("(x r) n -> x r n", r=AH)
                    for c in range(KH):
                        sp.dma_start(c64[:, hf, c], craw_v[bass.ds(b * NH + c * NH // KH, NH // KH), 0:HD, cols])\
                            .then_inc(raw_in[hf], 16)
                    sp.dma_start(den[:, hf], craw_v[bass.ds(b * NH, NH), HD, cols])\
                        .then_inc(raw_in[hf], 16)
                else:
                    sp.dma_start(c64[:, hf], scr["cout"][bass.ds(b * H, H), cols].rearrange("(c p) n -> p c n", p=P))\
                        .then_inc(raw_in[hf], 16)
                    sp.dma_start(comb[:, hf], scr["comb"][bass.ds(b * H, H), cols].rearrange("(c p) n -> p c n", p=P))\
                        .then_inc(raw_in[hf], 16)
                    sp.dma_start(den[:, hf], scr["cden"][bass.ds(b * BH, BH), cols]).then_inc(raw_in[hf], 16)

            def load_residual(b, hf):
                sp.wait_ge(x1_done, NT * (2 * b + hf) + NT)
                sp.dma_start(xt[:, hf], residual[bass.ds(b * S + hf * CH, CH)].rearrange("(t p) h -> p t h", p=P))\
                    .then_inc(res_in[hf], 16)

            def batch(b, more):
                if more:
                    for hf in range(CPB):
                        load(b + 1, hf)
                    for hf in range(CPB):
                        load_residual(b + 1, hf)
                if cross:
                    return
                for hf in range(CPB):
                    sp.wait_ge(x1_done, 8 + NT * (2 * b + hf) + NT)
                    sp.dma_start(scr["x1"][bass.ds(b * S + hf * CH, CH)].rearrange("(t p) h -> p t h", p=P), x1[:, hf])\
                        .then_inc(x1_out[hf], 16)
                for hf in range(CPB):
                    for s in range(KH):
                        sp.wait_ge(b_done, 2 + KH * (2 * b + hf) + s + 1)
                        sp.dma_start(scr["xq"][:, bass.ds(b * H + s * P, P), hf * CH:(hf + 1) * CH]
                                     .rearrange("a p n -> p a n"), ab[:, s]).then_inc(part_out[s], 16)

            for hf in range(CPB):
                load(0, hf)
            for hf in range(CPB):
                load_residual(0, hf)
            with sp.Fori(0, B - 1) as b:
                batch(b, True)
            batch(B - 1, False)
            if not cross:
                for n in range(2):
                    sp.wait_ge(x1_out[n], 16 + 16 * B)
                    sp.wait_ge(part_out[n], 16 + 16 * NCH)

        @block.gpsimd
        def _(pool):
            pool.memset(self32[:], 1.0).then_inc(sel_made, 1)
            pool.wait_ge(sel_made, 1)
            selector_steps(pool, self32, ((0, width, 0), (0, width, P)), sel_made)
            pool.sem_inc(b_done, 2)
            pool.wait_ge(small_in, 16 if cross else 48)
            with pool.Fori(0, B) as b:
                for hf in range(CPB):
                    pool.wait_ge(res_in[hf], 16 * b + 16)
                    pool.tensor_tensor(xt[:, hf], xt[:, hf], obias[:].unsqueeze(1).broadcast_to([P, NT, H]), ALU.add)\
                        .then_inc(xo_done, 1)
                if not cross:
                    for hf in range(CPB):
                        for c in range(KH):
                            pool.wait_ge(za_done, KH * (2 * b + hf) + c + 1)
                            pool.tensor_tensor(zb[:, hf, c], z[:, hf, c], za[:, hf, c].bitcast(F32), ALU.subtract).then_inc(zb_done, 1)
                if not cross:
                    for hf in range(CPB):
                        for s in range(KH):
                            pool.wait_ge(a_done, KH * (2 * b + hf) + s + 1)
                            pool.tensor_tensor(ab[:, s, 1], t[:, s], ab[:, s, 0], ALU.subtract).then_inc(b_done, 1)

        @block.tensor
        def _(pe):
            pe.wait_ge(w_done, 1)
            pe.wait_ge(sel_done, 2)
            with pe.Fori(0, B) as b:
                for hf in range(CPB):
                    i = 2 * b + hf
                    pe.wait_ge(r_ready, i + 1)
                    for n in range(KH):
                        pe.wait_ge(pb_done, 4 + 2 * i + n - 1)
                        pe.matmul(pb[:, n], sel[:, n], rsplit[:, hf], start=True, stop=True).then_inc(pb_ready, 1)
                if not cross:
                    for hf in range(CPB):
                        i = 2 * b + hf
                        pe.wait_ge(cnb_done, KH * i + KH)
                        if hf:
                            pe.wait_ge(z_done, KH * i)
                        for c in range(KH):
                            w = slice(W0 + c * P, W0 + (c + 1) * P)
                            mm3(pe, pw[:, c], halves(wa, w), halves(wb, w), [cna[:, hf, x] for x in range(KH)],
                                [cnb[:, hf, x] for x in range(KH)]).then_inc(pw_ready, 1)
                for hf in range(CPB):
                    i = 2 * b + hf
                    if cross:
                        pe.wait_ge(cnb_done, KH * i + KH)
                        la, lb = [cna[:, hf, c] for c in range(KH)], [cnb[:, hf, c] for c in range(KH)]
                    else:
                        pe.wait_ge(zb_done, KH * i + KH)
                        la, lb = [za[:, hf, c] for c in range(KH)], [zb[:, hf, c] for c in range(KH)]
                    for tt in range(NT):
                        pe.wait_ge(y_done, NT * i + tt + 1)
                        tok = slice(tt * P, (tt + 1) * P)
                        mm3(pe, po[:, tt % 2, 0:H], [x[:, tok] for x in la], [x[:, tok] for x in lb],
                            halves(wa, slice(Y0, Y0 + H)), halves(wb, slice(Y0, Y0 + H))).then_inc(y_ready, 1)
                for hf in range(CPB):
                    i = 2 * b + hf
                    pe.wait_ge(y_done, 2 + NT * (2 * b + CPB))
                    pe.wait_ge(xb_done, i + 1)
                    pe.wait_ge(x1_done, 8 + NT * i + NT)
                    for kh in range(KH):
                        for tt in range(NT):
                            last = pe.transpose(px[:, kh, tt * P:(tt + 1) * P], x1[:, hf, tt, kh * P:(kh + 1) * P], ident[:])
                    last.then_inc(xT_ready, 1)
                    if not cross:
                        pe.wait_ge(xb_done, i + 2)
                        for n in range(KH):
                            pe.wait_ge(t_done, KH * i + n + 1)
                            w = slice(Q0 + n * P, Q0 + (n + 1) * P)
                            mm3(pe, po[:, n], halves(wa, w), halves(wb, w), halves(xa), halves(xb)).then_inc(po_ready, 1)
                        if hf == CPB - 1:
                            pe.wait_ge(t_done, 2 + KH * i + KH)

        @block.scalar
        def _(act):
            act.sem_inc(t_done, 2)
            act.sem_inc(mixed, 4)
            act.wait_ge(small_in, 16 if cross else 48)
            act.wait_ge(eps_set, 1)
            if not cross:
                act.wait_ge(small_done, 2)
            with act.Fori(0, B) as b:
                for hf in range(CPB):
                    i = 2 * b + hf
                    for c in range(KH):
                        act.wait_ge(pb_done, 4 + 2 * i + c + 1)
                        act.activation(cna[:, hf, c], cn[:, hf, c], ACT.Copy).then_inc(cna_done, 1)
                if not cross:
                    for hf in range(CPB):
                        for c in range(KH):
                            act.activation(z[:, hf, c], comb[:, hf, c], ACT.Identity, bias=small[:, 0, c:c + 1], scale=1.0 - META_W)\
                                .then_inc(mixed, 1)
                    for hf in range(CPB):
                        for c in range(KH):
                            act.wait_ge(z_done, KH * (2 * b + hf) + c + 1)
                            act.activation(za[:, hf, c], z[:, hf, c], ACT.Copy).then_inc(za_done, 1)
                for hf in range(CPB):
                    i = 2 * b + hf
                    for tt in range(NT):
                        act.wait_ge(var_done, NT * i + tt + 1)
                        act.activation(rstd[:, tt % 2, 0:1], mv[:, tt % 2, 1:2], ACT.Sqrt, bias=eps[:]).then_inc(std_done, 1)
                for hf in range(CPB):
                    i = 2 * b + hf
                    act.wait_ge(xT_ready, i + 1)
                    dst = keep[0][:, :, bass.ds(b * S + hf * CH, CH)] if cross else xa[:]
                    act.activation(dst, px[:], ACT.Copy).then_inc(xa_done, 1)
                    if not cross:
                        for s in range(KH):
                            act.wait_ge(po_ready, KH * i + s + 1)
                            act.wait_ge(b_done, KH * i + s + 1)
                            act.activation(t[:, s], po[:, s], ACT.Identity, bias=small[:, 1, s:s + 1], scale=HD ** -0.5)\
                                .then_inc(t_done, 1)

        @block.vector
        def _(dve):
            dve.sem_inc(pb_done, 4)
            dve.sem_inc(y_done, 2)
            dve.sem_inc(x1_done, 8)
            dve.sem_inc(xb_done, 1)
            dve.memset(rsplit[:].bitcast(F32), 0.0).then_inc(rs_zero, 1)
            dve.memset(sel[:].bitcast(F32), 0.0).then_inc(sel_set, 1)
            dve.memset(eps[:], EPS).then_inc(eps_set, 1)
            dve.wait_ge(w_in, 16 if cross else 48)
            dve.tensor_copy(wa[:], raw[:]).then_inc(wa_done, 1)
            dve.wait_ge(wa_done, 1)
            dve.tensor_tensor(wb[:], raw[:], wa[:].bitcast(F32), ALU.subtract).then_inc(w_done, 1)
            if not cross:
                dve.wait_ge(small_in, 48)
                dve.tensor_scalar(small[:, 0], small_raw[:, 0], META_W, None, ALU.mult).then_inc(small_done, 1)
                dve.tensor_scalar(small[:, 1], small_raw[:, 1], HD ** -0.5, None, ALU.mult).then_inc(small_done, 1)
            dve.wait_ge(sel_made, 5)
            dve.wait_ge(sel_set, 1)
            dve.tensor_copy(sel[0:32], self32[:]).then_inc(sel_done, 1)
            dve.tensor_copy(sel[32:64], self32[:]).then_inc(sel_done, 1)
            dve.wait_ge(rs_zero, 1)

            def reciprocals(b):
                for hf in range(CPB):
                    dve.wait_ge(raw_in[hf], 16 * RAWS * (b + 1))
                    dve.reciprocal(rden[:, hf], den[:, hf]).then_inc(recip_done, 1)

            def batch(b, more):
                for hf in range(CPB):
                    i = 2 * b + hf
                    dve.wait_ge(recip_done, i + 1)
                    dve.tensor_copy(rsplit[0:NR, hf], rden[:, hf]).then_inc(ra_done, 1)
                    dve.wait_ge(ra_done, i + 1)
                    dve.tensor_tensor(rsplit[32:32 + NR, hf], rden[:, hf], rsplit[0:NR, hf].bitcast(F32), ALU.subtract)\
                        .then_inc(r_ready, 1)
                for hf in range(CPB):
                    for n in range(KH):
                        dve.wait_ge(pb_ready, 2 * (2 * b + hf) + n + 1)
                        dve.tensor_tensor(cn[:, hf, n], c64[:, hf, n], pb[:, n], ALU.mult).then_inc(pb_done, 1)
                for hf in range(CPB):
                    for c in range(KH):
                        dve.wait_ge(cna_done, KH * (2 * b + hf) + c + 1)
                        dve.tensor_tensor(cnb[:, hf, c], cn[:, hf, c], cna[:, hf, c].bitcast(F32), ALU.subtract).then_inc(cnb_done, 1)
                if not cross:
                    for hf in range(CPB):
                        i = 2 * b + hf
                        for c in range(KH):
                            dve.wait_ge(mixed, 4 + KH * i + c + 1)
                            dve.wait_ge(pw_ready, KH * i + c + 1)
                            dve.scalar_tensor_tensor(out=z[:, hf, c], in0=pw[:, c], scalar=META_W, in1=z[:, hf, c],
                                                     op0=ALU.mult, op1=ALU.add).then_inc(z_done, 1)
                for hf in range(CPB):
                    i = 2 * b + hf
                    dve.wait_ge(xo_done, i + 1)
                    if not cross:
                        dve.wait_ge(x1_out[hf], 16 * b + 16)
                    for tt in range(NT + 1):
                        if tt < NT:
                            n = NT * i + tt
                            dve.wait_ge(y_ready, n + 1)
                            dve.wait_ge(x1_done, 8 + n - 1)
                            dve.tensor_tensor(res[:, tt % 2], po[:, tt % 2, 0:H], xt[:, hf, tt], ALU.add).then_inc(y_done, 1)
                            dve.wait_ge(y_done, 2 + n + 1)
                            dve.bn_stats(stats[:, tt % 2], res[:, tt % 2]).then_inc(n_chain, 1)
                            dve.wait_ge(n_chain, 2 * NT * i + max(1, 2 * tt))
                            dve.sem_inc(stats_seen, 1)
                            dve.bn_aggr(mv[:, tt % 2], stats[:, tt % 2]).then_inc(var_done, 1)
                        if tt > 0:
                            u, m = tt - 1, NT * i + tt - 1
                            dve.wait_ge(std_done, m + 1)
                            dve.reciprocal(rstd[:, u % 2, 1:2], rstd[:, u % 2, 0:1]).then_inc(n_chain, 1)
                            dve.wait_ge(n_chain, 2 * NT * i + min(2 * u + 3, 2 * NT))
                            dve.tensor_scalar(x1[:, hf, u], res[:, u % 2], mv[:, u % 2, 0:1], rstd[:, u % 2, 1:2],
                                              ALU.subtract, ALU.mult).then_inc(x1_done, 1)
                            if cross:
                                dve.wait_ge(x1_done, 8 + m + 1)
                                dve.tensor_copy(keep[2][:, bass.ds(NT * i + u, 1)].squeeze(1), x1[:, hf, u])
                for hf in range(CPB):
                    i = 2 * b + hf
                    dve.wait_ge(xa_done, i + 1)
                    if cross:
                        tok = bass.ds(b * S + hf * CH, CH)
                        dve.tensor_tensor(keep[1][:, :, tok], px[:], keep[0][:, :, tok].bitcast(F32), ALU.subtract)\
                            .then_inc(xb_done, 1)
                        continue
                    dve.tensor_tensor(xb[:], px[:], xa[:].bitcast(F32), ALU.subtract).then_inc(xb_done, 1)
                    for s in range(KH):
                        dve.wait_ge(t_done, 2 + KH * i + s + 1)
                        dve.wait_ge(part_out[s], 16 * i + 16)
                        dve.tensor_copy(ab[:, s, 0].bitcast(FR), t[:, s]).then_inc(a_done, 1)
                if more:
                    reciprocals(b + 1)

            reciprocals(0)
            with dve.Fori(0, B - 1) as b:
                batch(b, True)
            batch(B - 1, False)


def context_projections(nc, A, scr, ident, dist, distT):
    with ExitStack() as stack:
        k = Kit(nc, stack, "cx")
        NE_ = 2 * B
        HB = NE_ // 2
        raw = k.sb("raw", [P, KH, 2 * H])
        wa, wb = k.sb("wa", [P, KH, 2 * H], FR), k.sb("wb", [P, KH, 2 * H], FR)
        kbias, vbias = k.sb("kbias", [P, KH]), k.sb("vbias", [P, H])
        scaling, negated, nabs, tiny = (k.sb(n, [P, 1]) for n in ("scaling", "negated", "nabs", "tiny"))
        ctx = k.sb("ctx", [E2, NE_, H])
        xa, xb = k.sb("xa", [P, KH, NE_, EP], FR), k.sb("xb", [P, KH, NE_, EP], FR)
        t, ab = k.sb("t", [P, 4, HB, EP]), k.sb("ab", [P, 4, 2, HB, EP])
        v16 = k.sb("v16", [EP, NE_, NH, AH])
        px, po, pd = k.ps("px", [P, 2, HB, P]), k.ps("po", [P, 2, CH]), k.ps("pd", [P, 2, NT, P])
        w_in, small_in, scale_in, ctx_in = k.sem("w_in"), k.sem("small_in"), k.sem("scale_in"), k.sem("ctx_in")
        dist_in = [k.sem(f"dist_in{b}") for b in range(B)]
        names = ("zeroed", "ones_set", "wa_done", "w_done", "s_chain", "ln_done", "scaled", "px_ready", "xa_done",
                 "xb_done", "k_ready", "t_done", "a_done", "b_done", "v_ready", "v_done", "pd_ready", "pd_act", "pd_dve",
                 "stored")
        (zeroed, ones_set, wa_done, w_done, s_chain, ln_done, scaled, px_ready, xa_done, xb_done, k_ready, t_done, a_done,
         b_done, v_ready, v_done, pd_ready, pd_act, pd_dve, stored) = (k.sem(n) for n in names)
        k_units = [(j, u) for j in range(KH) for u in range(2)]
        x_units = [(kh, u) for kh in range(KH) for u in range(2)]
        d_units = [(b, e, hq) for b in range(B) for e in range(2) for hq in range(CPB)]
        block = stack.enter_context(nc.Block())

        @block.sync
        def _(sp):
            sp.dma_start(ctx[:], A["ctx_1024"].rearrange("b (c e) h -> e (b c) h", c=2)).then_inc(ctx_in, 16)
            for n, w in enumerate(("Wk", "Wv")):
                sp.dma_start(raw[:, :, n * H:(n + 1) * H], A["L0_xattn_" + w].rearrange("(k p) n -> p k n", p=P)).then_inc(w_in, 16)
            for b in range(B):
                sp.dma_start(dist[:, b], A["fside_BxSxS2_0"][b].rearrange("(t p) n -> p t n", p=P)).then_inc(dist_in[b], 16)
            sp.dma_start(scaling[:], rows(A["L0_xattn_distance_scaling"])).then_inc(scale_in, 16)
            sp.dma_start(kbias[:], column(A["L0_xattn_bk"]), allow_slow_non_contiguous=True).then_inc(small_in, 16)
            sp.dma_start(vbias[:], rows(A["L0_xattn_bv"])).then_inc(small_in, 16)
            for s, (j, u) in enumerate(k_units):
                sp.wait_ge(b_done, s + 1)
                for part in range(2):
                    for n in range(2):
                        row = (2 * u + n) * H + j * P
                        sp.dma_start(scr["xk"][part, row:row + P], ab[:, s, part, 2 * n:2 * n + 2].rearrange("p e n -> p (e n)"))\
                            .then_inc(stored, 16)
            for n in range(NE_):
                sp.wait_ge(v_done, n + 1)
                sp.dma_start(scr["xv"].rearrange("(b g e p) c -> b e p g c", b=B, g=NG, e=2)[n // 2, n % 2],
                             v16[:, n].rearrange("p (g h) c -> p g (h c)", g=NG)).then_inc(stored, 16)
            sp.wait_ge(stored, 16 * (4 * len(k_units) + NE_))

        @block.gpsimd
        def _(pool):
            pool.memset(xa[:].bitcast(F32), 0.0).then_inc(zeroed, 1)
            pool.memset(xb[:].bitcast(F32), 0.0).then_inc(zeroed, 1)
            pool.memset(t[:], 0.0).then_inc(zeroed, 1)
            pool.memset(v16[:], 0.0).then_inc(zeroed, 1)
            pool.memset(distT[:], 0.0).then_inc(zeroed, 1)
            pool.wait_ge(zeroed, 5)
            pool.memset(v16[0:E2, :, :, HD:HD + 1], 1.0).then_inc(ones_set, 1)
            for s in range(len(k_units)):
                pool.wait_ge(a_done, s + 1)
                pool.tensor_tensor(ab[:, s, 1], t[:, s], ab[:, s, 0], ALU.subtract).then_inc(b_done, 1)

        @block.tensor
        def _(pe):
            pe.wait_ge(ctx_in, 16)
            for n, (kh, u) in enumerate(x_units):
                if n >= 2:
                    pe.wait_ge(xb_done, n - 1)
                for e in range(HB):
                    last = pe.transpose(px[:, n % 2, e, 0:E2], ctx[:, HB * u + e, kh * P:(kh + 1) * P], ident[0:E2, 0:E2])
                last.then_inc(px_ready, 1)
            pe.wait_ge(xb_done, len(x_units))
            pe.wait_ge(w_done, 1)
            for n, (j, u) in enumerate(k_units):
                if n >= 2:
                    pe.wait_ge(t_done, n - 1)
                w, blocks = slice(j * P, (j + 1) * P), slice(HB * u, HB * u + HB)
                mm3(pe, po[:, n % 2, 0:HB * EP].rearrange("p (e n) -> p e n", n=EP), halves(wa, w), halves(wb, w),
                    halves(xa, blocks), halves(xb, blocks)).then_inc(k_ready, 1)
            for n in range(NE_):
                if n < 2:
                    pe.wait_ge(t_done, len(k_units) - 1 + n)
                else:
                    pe.wait_ge(v_done, n - 1)
                w = slice(H, 2 * H)
                mm3(pe, po[0:EP, n % 2, 0:H], halves(xa, n), halves(xb, n), halves(wa, w), halves(wb, w)).then_inc(v_ready, 1)
            for n, (b, e, hq) in enumerate(d_units):
                pe.wait_ge(scaled, b + 1)
                if n >= 2:
                    pe.wait_ge((pd_act, pd_dve)[n % 2], n // 2)
                for i in range(NT):
                    last = pe.transpose(pd[0:E2, n % 2, i], dist[:, b, hq * NT + i, e * E2:(e + 1) * E2], ident[:])
                last.then_inc(pd_ready, 1)

        @block.scalar
        def _(act):
            act.wait_ge(zeroed, 5)
            for n, (kh, u) in enumerate(x_units):
                act.wait_ge(px_ready, n + 1)
                act.activation(xa[:, kh, HB * u:HB * u + HB, 0:E2], px[:, n % 2, :, 0:E2], ACT.Copy).then_inc(xa_done, 1)
            act.wait_ge(s_chain, 1)
            for b in range(B):
                act.wait_ge(dist_in[b], 16)
                act.activation(dist[:, b], dist[:, b], ACT.Ln, bias=tiny[:]).then_inc(ln_done, 1)
            act.wait_ge(small_in, 32)
            for n, (j, u) in enumerate(k_units):
                act.wait_ge(k_ready, n + 1)
                act.activation(t[:, n, :, 0:E2], po[:, n % 2, 0:HB * EP].rearrange("p (e n) -> p e n", n=EP)[:, :, 0:E2],
                               ACT.Identity, bias=kbias[:, j:j + 1]).then_inc(t_done, 1)
            for n, (b, e, hq) in enumerate(d_units):
                if n % 2 == 0:
                    act.wait_ge(pd_ready, n + 1)
                    act.activation(distT[0:E2, b, e, hq * CH:(hq + 1) * CH], pd[0:E2, n % 2].rearrange("p i n -> p (i n)"),
                                   ACT.Copy).then_inc(pd_act, 1)

        @block.vector
        def _(dve):
            dve.memset(tiny[:], 1e-9).then_inc(s_chain, 1)
            dve.wait_ge(w_in, 32)
            dve.tensor_copy(wa[:], raw[:]).then_inc(wa_done, 1)
            dve.wait_ge(wa_done, 1)
            dve.tensor_tensor(wb[:], raw[:], wa[:].bitcast(F32), ALU.subtract).then_inc(w_done, 1)
            for n, (kh, u) in enumerate(x_units):
                dve.wait_ge(xa_done, n + 1)
                blocks = slice(HB * u, HB * u + HB)
                dve.tensor_tensor(xb[:, kh, blocks, 0:E2], px[:, n % 2, :, 0:E2], xa[:, kh, blocks, 0:E2].bitcast(F32), ALU.subtract)\
                    .then_inc(xb_done, 1)
            dve.wait_ge(scale_in, 16)
            dve.tensor_scalar(negated[:], scaling[:], -1.0, None, ALU.mult).then_inc(s_chain, 1)
            dve.wait_ge(s_chain, 2)
            dve.tensor_tensor(nabs[:], scaling[:], negated[:], ALU.min).then_inc(s_chain, 1)
            dve.wait_ge(s_chain, 3)
            for b in range(B):
                dve.wait_ge(ln_done, b + 1)
                dve.tensor_scalar(dist[:, b], dist[:, b], nabs[:, 0:1], None, ALU.mult).then_inc(scaled, 1)
            for n in range(len(k_units)):
                dve.wait_ge(t_done, n + 1)
                dve.tensor_copy(ab[:, n, 0].bitcast(FR), t[:, n]).then_inc(a_done, 1)
            dve.wait_ge(ones_set, 1)
            dve.wait_ge(small_in, 32)
            for n in range(NE_):
                dve.wait_ge(v_ready, n + 1)
                dve.tensor_tensor(v16[0:E2, n, :, 0:HD], po[0:E2, n % 2, 0:H].rearrange("p (h d) -> p h d", h=NH),
                                  vbias[0:E2].rearrange("p (h d) -> p h d", h=NH), ALU.add).then_inc(v_done, 1)
            for n, (b, e, hq) in enumerate(d_units):
                if n % 2:
                    dve.wait_ge(pd_ready, n + 1)
                    dve.tensor_copy(distT[0:E2, b, e, hq * CH:(hq + 1) * CH], pd[0:E2, n % 2].rearrange("p i n -> p (i n)"))\
                        .then_inc(pd_dve, 1)


def attend_cross(nc, scr, dist, distT):
    with ExitStack() as stack:
        k = Kit(nc, stack, "ac")
        ONE, LAST = 4 * HD, 6 * HD
        MROW = LAST - 1
        NSTEP = CPB * 2
        qs, ks = k.sb("qs", [LAST, NG, GH, S], FR), k.sb("ks", [LAST, NG, GH, 2, EP], FR)
        vs = k.sb("vs", [EP, NG, 2, GH * AH])
        probs = k.sb("probs", [EP, 2, GH, CH])
        ev = k.sb("ev", [P, CPB, CH])
        bias = k.sb("bias", [P, S // P, S2])
        m1 = k.sb("m1", [P, CPB, GH * NT])
        mneg, mturn = k.sb("mneg", [P, 32]), k.sb("mturn", [P, 32])
        mrows = k.sb("mrows", [P, CPB, 32], FR)
        pst = k.ps("pst", [P, 2, 2, CH])
        psm = k.ps("psm", [P, 2, 2, 2, P])
        pacc = k.ps("pacc", [P, CPB, CH])
        filled, zeroed, mneg_set, bias_done, mx_seen = (
            k.sem(n) for n in ("filled", "zeroed", "mneg_set", "bias_done", "mx_seen"))
        loaded = [k.sem(f"loaded{n}") for n in range(NG)]
        mrow_in = [[k.sem(f"mrow_in{n}{h}") for h in range(CPB)] for n in range(NG)]
        m_out = [k.sem(f"m_out{h}") for h in range(CPB)]
        ev_out = [k.sem(f"ev_out{h}") for h in range(CPB)]
        mx_ready, mx_done, m_chain, m_ready, row_moved = (
            k.sem(n) for n in ("mx_ready", "mx_done", "m_chain", "m_ready", "row_moved"))
        st_ready, add_done, exp_done, pv_done, acc_out = (
            k.sem(n) for n in ("st_ready", "add_done", "exp_done", "pv_done", "acc_out"))
        LOADS = 9
        PV0 = NSTEP * (NG - 1) + 2
        mx_list = [(hq, jp, i) for hq in range(CPB) for jp in range(GH // 2) for i in range(NT)]
        NM = len(mx_list)
        PER = NM // NSTEP
        block = stack.enter_context(nc.Block())

        @block.sync
        def _(sp):
            def load(G, slot):
                sp.wait_ge(pv_done, PV0 + NSTEP * (G - NG + 1))
                for r, (qp, kp) in enumerate(((0, 0), (0, 1), (1, 0), (1, 1))):
                    sp.dma_start(qs[r * HD:(r + 1) * HD, slot].bitcast(F32),
                                 scr["xq"][qp, bass.ds(G * GH * HD, GH * HD)].rearrange("(j d) n -> d j n", j=GH))\
                        .then_inc(loaded[slot], 16)
                    sp.dma_start(ks[r * HD:(r + 1) * HD, slot].rearrange("p j e n -> p j (e n)").bitcast(F32),
                                 scr["xk"][kp, bass.ds(G * GH * HD, GH * HD)].rearrange("(j d) n -> d j n", j=GH))\
                        .then_inc(loaded[slot], 16)
                sp.dma_start(vs[:, slot], scr["xv"][bass.ds(G * 2 * EP, 2 * EP)].rearrange("(e p) n -> p e n", p=EP))\
                    .then_inc(loaded[slot], 16)

            def max_row(G, slot, uses, hq):
                sp.wait_ge(m_ready, CPB * G + hq + 1)
                turned = scr["m"][hq].rearrange("(c b r) -> b c r", b=4, r=32)
                for q in range(4):
                    sp.dma_start(turned[q], mrows[32 * q:32 * q + GH * NT, hq].bitcast(F32)).then_inc(m_out[hq], 16)
                sp.wait_ge(m_out[hq], 64 * G + 64)
                sp.dma_start(qs[MROW:LAST, slot, :, hq * CH:(hq + 1) * CH].bitcast(F32),
                             scr["m"][hq:hq + 1].rearrange("o (j n) -> o j n", j=GH)).then_inc(mrow_in[slot][hq], 16)
                sp.wait_ge(mrow_in[slot][hq], 16 * uses + 16)
                sp.sem_inc(row_moved, 1)

            def store(G, qh):
                sp.wait_ge(acc_out, CPB * G + qh + 3)
                sp.dma_start(scr["craw"][bass.ds(G * P, P), qh * CH:(qh + 1) * CH], ev[:, qh]).then_inc(ev_out[qh], 16)

            def group(b, g, ahead):
                G = b * NG + g
                if ahead >= 2:
                    load(G + 2, (g + 2) % NG)
                if ahead >= 1:
                    max_row(G + 1, (g + 1) % NG, b + (g + 1) // NG, 0)
                store(G, 0)
                if ahead >= 1:
                    max_row(G + 1, (g + 1) % NG, b + (g + 1) // NG, 1)
                store(G, 1)

            for qh in range(CPB):
                sp.sem_inc(ev_out[qh], 16)
            load(0, 0)
            load(1, 1)
            for hq in range(CPB):
                max_row(0, 0, 0, hq)
            with sp.Fori(0, B - 1) as b:
                for g in range(NG):
                    group(b, g, 2)
            for g in range(NG):
                group(B - 1, g, NG - 1 - g)
            for qh in range(CPB):
                sp.wait_ge(ev_out[qh], 16 + 16 * B * NG)

        @block.gpsimd
        def _(pool):
            pool.memset(qs[ONE:LAST].bitcast(F32), 0.0).then_inc(filled, 1)

        @block.tensor
        def _(pe):
            def maxima(G, slot, uses, lo, hi):
                for n in range(lo, hi):
                    hq, jp, i = mx_list[n]
                    if n == 0:
                        pe.wait_ge(loaded[slot], 16 * LOADS * uses + 16 * LOADS)
                    pe.wait_ge(mx_done, 2 * (NM * G + n + 1))
                    q0 = (hq * NT + i) * P
                    for jj in range(2):
                        j = 2 * jp + jj
                        last = pe.matmul(psm[:, n % 2, jj, :, 0:EP], qs[0:MROW, slot, j, q0:q0 + P],
                                         ks[0:MROW, slot, j], start=True, stop=True)
                    last.then_inc(mx_ready, 1)

            def values(G, slot, s):
                qh, e = divmod(s, 2)
                pe.wait_ge(exp_done, NSTEP * G + s + 1)
                if e == 0:
                    pe.wait_ge(acc_out, CPB * G + qh + 1)
                for j in range(GH):
                    last = pe.matmul(pacc[j * AH:(j + 1) * AH, qh], vs[:, slot, e, j * AH:(j + 1) * AH],
                                     probs[:, s % 2, j], start=(e == 0), stop=(e == 1))
                last.then_inc(pv_done, 1)

            def group(b, g, more):
                G = b * NG + g
                nxt = (G + 1, (g + 1) % NG, b + (g + 1) // NG)
                for s in range(NSTEP):
                    qh, e = divmod(s, 2)
                    if e == 0:
                        pe.wait_ge(mrow_in[g][qh], 16 * b + 16)
                    for hp in range(2):
                        pe.wait_ge(add_done, 2 * NSTEP * G + 2 * s + hp + 1)
                        for jj in range(2):
                            j = 2 * hp + jj
                            last = pe.matmul(pst[0:EP, hp, jj], ks[:, g, j, e], qs[:, g, j, qh * CH:(qh + 1) * CH],
                                             start=True, stop=True)
                        last.then_inc(st_ready, 1)
                        if more:
                            maxima(*nxt, PER * s + hp, PER * s + hp + 1)
                    if s > 0:
                        values(G, g, s - 1)
                    if more:
                        maxima(*nxt, PER * s + 2, PER * s + PER)
                values(G, g, NSTEP - 1)

            pe.sem_inc(pv_done, PV0)
            pe.wait_ge(filled, 2)
            maxima(0, 0, 0, 0, NM)
            with pe.Fori(0, B - 1) as b:
                for g in range(NG):
                    group(b, g, True)
            for g in range(NG):
                group(B - 1, g, g < NG - 1)

        @block.scalar
        def _(act):
            def copy_out(G, qh):
                act.wait_ge(pv_done, PV0 + NSTEP * G + 2 * qh + 2)
                act.wait_ge(ev_out[qh], 16 * G + 16)
                act.activation(ev[:, qh], pacc[:, qh], ACT.Copy).then_inc(acc_out, 1)

            act.sem_inc(acc_out, 2)
            with act.Fori(0, B) as b:
                for g in range(NG):
                    G = b * NG + g
                    for s in range(NSTEP):
                        act.wait_ge(add_done, 2 + 2 * (NSTEP * G + s + 1))
                        act.activation(probs[:, s % 2], probs[:, s % 2], ACT.Exp).then_inc(exp_done, 1)
                        if s == 3:
                            copy_out(G, 0)
                    copy_out(G, 1)

        @block.vector
        def _(dve):
            def take_bias(b):
                src = dist[:, b] if isinstance(b, int) else dist[:, bass.ds(b, 1)].rearrange("p o t n -> p (o t) n")
                dve.tensor_copy(bias[:], src).then_inc(bias_done, 1)

            def maxima(G, lo, hi):
                for n in range(lo, hi):
                    hq, jp, i = mx_list[n]
                    dve.wait_ge(mx_ready, NM * G + n + 1)
                    dve.sem_inc(mx_seen, 1)
                    for jj in range(2):
                        col = (2 * jp + jj) * NT + i
                        scores = psm[:, n % 2, jj, :, 0:E2]
                        dve.tensor_tensor_reduce(out=scores, in0=scores, in1=bias[:, hq * NT + i].rearrange("p (e n) -> p e n", e=2), scale=1.0, scalar=LOWEST, op0=ALU.add,
                                                 op1=ALU.max, accum_out=m1[:, hq, col:col + 1]).then_inc(mx_done, 1)
                    if n % (NM // CPB) == NM // CPB - 1:
                        finish(G, hq)

            def finish(G, hq):
                dve.wait_ge(mx_done, 4 + 2 * (NM * G + (hq + 1) * NM // CPB))
                dve.tensor_scalar(mneg[:, 0:GH * NT], m1[:, hq], -1.0, None, ALU.mult).then_inc(m_chain, 1)
                dve.wait_ge(m_chain, 2 * (CPB * G + hq) + 1)
                dve.transpose(mturn[:], mneg[:]).then_inc(m_chain, 1)
                dve.wait_ge(m_chain, 2 * (CPB * G + hq) + 2)
                if not (isinstance(G, int) and G == 0):
                    dve.wait_ge(row_moved, CPB * (G - 1) + hq + 1)
                dve.tensor_copy(mrows[:, hq], mturn[:]).then_inc(m_ready, 1)

            def group(b, g, more):
                G = b * NG + g
                if more and g == NG - 1:
                    take_bias(b + 1)
                    dve.wait_ge(bias_done, b + 2)
                for s in range(NSTEP):
                    qh, e = divmod(s, 2)
                    for hp in range(2):
                        dve.wait_ge(st_ready, 2 * NSTEP * G + 2 * s + hp + 1)
                        if hp == 0:
                            dve.wait_ge(pv_done, PV0 + NSTEP * G + s - 1)
                        cols = slice(qh * CH, (qh + 1) * CH)
                        added = distT[:, b, e, cols] if isinstance(b, int) else \
                            distT[:, bass.ds(b, 1), e, cols].rearrange("p o n -> p (o n)")
                        dve.tensor_tensor(probs[:, s % 2, 2 * hp:2 * hp + 2], pst[0:EP, hp],
                                          added.unsqueeze(1).broadcast_to([EP, 2, CH]), ALU.add).then_inc(add_done, 1)
                        if more:
                            maxima(G + 1, PER * s + hp * PER // 2, PER * s + (hp + 1) * PER // 2)

            dve.sem_inc(mx_done, 4)
            dve.sem_inc(add_done, 2)
            dve.memset(ks[ONE:LAST].bitcast(F32), 0.0).then_inc(zeroed, 1)
            dve.wait_ge(zeroed, 1)
            dve.memset(mneg[:], 0.0).then_inc(mneg_set, 1)
            dve.wait_ge(mneg_set, 1)
            dve.memset(ks[ONE:LAST, :, :, :, 0:E2].bitcast(F32), 1.0).then_inc(filled, 1)
            take_bias(0)
            dve.wait_ge(bias_done, 1)
            maxima(0, 0, NM)
            with dve.Fori(0, B - 1) as b:
                for g in range(NG):
                    group(b, g, True)
            for g in range(NG):
                group(B - 1, g, g < NG - 1)


def route(nc, A, ident, xa, xb, weight):
    with ExitStack() as stack:
        k = Kit(nc, stack, "ro")
        TT = TOK // P
        raw, wa, wb = k.sb("raw", [P, KH, NE]), k.sb("wa", [P, KH, NE], FR), k.sb("wb", [P, KH, NE], FR)
        lt = k.sb("lt", [NE, 2, CH])
        grid = [P, TT, NE]
        logits, prob, masked, equal, ranked, first, second = (
            k.sb(n, grid) for n in ("logits", "prob", "masked", "equal", "ranked", "first", "second"))
        rank = k.sb("rank", [P, NE])
        top, total, high1, high2, pick, share1, share2 = (
            k.sb(n, [P, TT]) for n in ("top", "total", "high1", "high2", "pick", "share1", "share2"))
        pl, pt = k.ps("pl", [NE, 2, CH]), k.ps("pt", [P, 2, CH // NE, NE])
        w_in, wa_done, w_done, rank_set, l_ready, l_done, t_ready, t_done, chain, exp_done = (k.sem(n) for n in (
            "w_in", "wa_done", "w_done", "rank_set", "l_ready", "l_done", "t_ready", "t_done", "chain", "exp_done"))
        block = stack.enter_context(nc.Block())

        @block.sync
        def _(sp):
            sp.dma_start(raw[:], A["L0_ffn_gate_w"].rearrange("(k p) n -> p k n", p=P)).then_inc(w_in, 16)

        @block.gpsimd
        def _(pool):
            for e in range(NE):
                pool.memset(rank[:, e:e + 1], float(NE - e)).then_inc(rank_set, 1)
            pool.memset(weight[:, NE], 1.0).then_inc(rank_set, 1)

        @block.tensor
        def _(pe):
            def turn(c):
                pe.wait_ge(l_done, c + 1)
                if c >= 2:
                    pe.wait_ge(t_done, c - 1)
                for tt in range(NT):
                    last = pe.transpose(pt[:, c % 2, tt], lt[:, c % 2, tt * P:(tt + 1) * P], ident[0:NE, 0:NE])
                last.then_inc(t_ready, 1)

            pe.wait_ge(w_done, 1)
            for c in range(NCH):
                if c >= 2:
                    pe.wait_ge(l_done, c - 1)
                tok = slice(c * CH, (c + 1) * CH)
                mm3(pe, pl[:, c % 2], halves(wa), halves(wb), halves(xa, tok), halves(xb, tok)).then_inc(l_ready, 1)
                if c >= 1:
                    turn(c - 1)
            turn(NCH - 1)

        @block.scalar
        def _(act):
            for c in range(NCH):
                act.wait_ge(l_ready, c + 1)
                if c >= 2:
                    act.wait_ge(t_ready, c - 1)
                act.activation(lt[:, c % 2], pl[:, c % 2], ACT.Copy).then_inc(l_done, 1)
            act.wait_ge(chain, 2)
            act.activation(prob[:], prob[:], ACT.Exp).then_inc(exp_done, 1)

        @block.vector
        def _(dve):
            count = [0]

            def link(instruction):
                instruction.then_inc(chain, 1)
                count[0] += 1
                dve.wait_ge(chain, count[0])

            def over(v):
                return v[:].unsqueeze(2).broadcast_to(grid)

            def pick_first(src, high, onehot):
                link(dve.tensor_reduce(high[:], src[:], AX.X, ALU.max))
                link(dve.tensor_tensor(equal[:], src[:], over(high), ALU.is_equal))
                link(dve.tensor_tensor(ranked[:], equal[:], rank[:].unsqueeze(1).broadcast_to(grid), ALU.mult))
                link(dve.tensor_reduce(pick[:], ranked[:], AX.X, ALU.max))
                link(dve.tensor_tensor(onehot[:], ranked[:], over(pick), ALU.is_equal))

            dve.wait_ge(w_in, 16)
            dve.tensor_copy(wa[:], raw[:]).then_inc(wa_done, 1)
            dve.wait_ge(wa_done, 1)
            dve.tensor_tensor(wb[:], raw[:], wa[:].bitcast(F32), ALU.subtract).then_inc(w_done, 1)
            for c in range(NCH):
                dve.wait_ge(t_ready, c + 1)
                dve.tensor_copy(logits[:, c * NT:(c + 1) * NT], pt[:, c % 2, 0:NT]).then_inc(t_done, 1)
            dve.wait_ge(t_done, NCH)
            link(dve.tensor_reduce(top[:], logits[:], AX.X, ALU.max))
            link(dve.tensor_tensor(prob[:], logits[:], over(top), ALU.subtract))
            dve.wait_ge(exp_done, 1)
            link(dve.tensor_reduce(total[:], prob[:], AX.X, ALU.add))
            link(dve.reciprocal(total[:], total[:]))
            link(dve.tensor_tensor(prob[:], prob[:], over(total), ALU.mult))
            dve.wait_ge(rank_set, NE + 1)
            pick_first(prob, high1, first)
            link(dve.scalar_tensor_tensor(out=masked[:], in0=first[:], scalar=-2.0, in1=prob[:], op0=ALU.mult, op1=ALU.add))
            pick_first(masked, high2, second)
            link(dve.tensor_tensor(total[:], high1[:], high2[:], ALU.add))
            link(dve.tensor_scalar(total[:], total[:], 1e-20, None, ALU.add))
            link(dve.reciprocal(total[:], total[:]))
            link(dve.tensor_tensor(share1[:], high1[:], total[:], ALU.mult))
            link(dve.tensor_tensor(share2[:], high2[:], total[:], ALU.mult))
            link(dve.tensor_tensor(first[:], first[:], over(share1), ALU.mult))
            link(dve.tensor_tensor(second[:], second[:], over(share2), ALU.mult))
            link(dve.tensor_tensor(weight[:, 0:NE].rearrange("p e t -> p t e"), first[:], second[:], ALU.add))


def run_experts(nc, A, xa, xb, acc, weight):
    with ExitStack() as stack:
        k = Kit(nc, stack, "ex")
        G0, U0, D0 = 0, KH * D, 2 * KH * D
        NW = D0 + FB * H
        PIECE = NW // NCH
        raw = k.sb("raw", [P, 2, NW])
        wa, wb = k.sb("wa", [P, 2, NW], FR), k.sb("wb", [P, 2, NW], FR)
        gated, hid = k.sb("gated", [P, 2, CH]), k.sb("hid", [P, 2, CH])
        ha, hb = k.sb("ha", [P, FB, CH], FR), k.sb("hb", [P, FB, CH], FR)
        pg, pu, py = k.ps("pg", [P, 2, CH]), k.ps("pu", [P, 2, CH]), k.ps("py", [P, NT, CH])
        w_in = [k.sem(f"w_in{n}") for n in range(2)]
        piece_a, piece_b, g_ready, u_ready, gated_done, hid_done, a_done, b_done, y_ready, acc_done = (k.sem(n) for n in (
            "piece_a", "piece_b", "g_ready", "u_ready", "gated_done", "hid_done", "a_done", "b_done", "y_ready", "acc_done"))
        block = stack.enter_context(nc.Block())

        def matrix(w, slot, first, n, cols):
            return w[:, slot, first + n * cols:first + (n + 1) * cols]

        @block.sync
        def _(sp):
            def load(slot, gate, up, down):
                for src, at, n in ((gate, G0, KH * D), (up, U0, KH * D), (down, D0, FB * H)):
                    blocks = n // src.shape[-1]
                    sp.dma_start(raw[:, slot, at:at + n].rearrange("p (k n) -> p k n", k=blocks),
                                 src.rearrange("(k p) n -> p k n", p=P)).then_inc(w_in[slot], 16)

            def load_expert(e, slot):
                gate, up, down = (A["L0_ffn_w_" + n].rearrange("e k n -> (e k) n") for n in ("gate", "up", "down"))
                load(slot, gate[bass.ds(e * H, H)], up[bass.ds(e * H, H)], down[bass.ds(e * D, D)])

            load_expert(0, 0)
            load_expert(1, 1)
            with sp.Fori(0, NE // 2 - 1) as ep:
                for n in range(2):
                    sp.wait_ge(piece_b, NCH * (2 * ep + n + 1))
                    load_expert(2 * ep + n + 2, n)
            sp.wait_ge(piece_b, NCH * (NE - 1))
            load(0, A["L0_ffn_ws_gate"], A["L0_ffn_ws_up"], A["L0_ffn_ws_down"])

        def pieces(c):
            return bass.ds(c * PIECE, PIECE)

        @block.gpsimd
        def _(pool):
            def split(e, slot, c):
                pool.wait_ge(piece_a, NCH * e + c + 1)
                pool.tensor_tensor(wb[:, slot, pieces(c)], raw[:, slot, pieces(c)], wa[:, slot, pieces(c)].bitcast(F32),
                                   ALU.subtract).then_inc(piece_b, 1)

            def expert(e, n, more):
                with pool.Fori(0, NCH) as c:
                    t = NCH * e + c
                    for f in range(FB):
                        pool.wait_ge(a_done, FB * t + f + 1)
                        pool.tensor_tensor(hb[:, f], hid[:, f % 2], ha[:, f].bitcast(F32), ALU.subtract).then_inc(b_done, 1)
                    if more:
                        split(e + 1, 1 - n, c)

            pool.sem_inc(b_done, 2)
            with pool.Fori(0, NCH) as c:
                split(0, 0, c)
            with pool.Fori(0, NE // 2) as ep:
                for n in range(2):
                    expert(2 * ep + n, n, True)
            expert(NE, 0, False)

        @block.tensor
        def _(pe):
            def expert(e, slot):
                with pe.Fori(0, NCH) as c:
                    pe.wait_ge(piece_b, NCH * e + NCH)
                    t = NCH * e + c
                    tok = bass.ds(c * CH, CH)
                    for f in range(FB):
                        for out, first, free, ready in ((pg, G0, gated_done, g_ready), (pu, U0, hid_done, u_ready)):
                            pe.wait_ge(free, FB * t + f + 1)
                            la, lb = ([matrix(w, slot, first, n, D)[:, f * P:(f + 1) * P] for n in range(KH)] for w in (wa, wb))
                            mm3(pe, out[:, f % 2], la, lb, halves(xa, tok), halves(xb, tok)).then_inc(ready, 1)
                    pe.wait_ge(acc_done, NT * t + NT)
                    for f in range(FB):
                        pe.wait_ge(b_done, 2 + FB * t + f + 1)
                        for tt in range(NT):
                            cols = slice(tt * P, (tt + 1) * P)
                            da, db = matrix(wa, slot, D0, f, H), matrix(wb, slot, D0, f, H)
                            for n, (x, y) in enumerate(((ha, da), (ha, db), (hb, da))):
                                last = pe.matmul(py[:, tt, 0:H], x[:, f, cols], y, start=(f == 0 and n == 0),
                                                 stop=(f == FB - 1 and n == 2))
                            if f == FB - 1:
                                last.then_inc(y_ready, 1)

            with pe.Fori(0, NE // 2) as ep:
                for n in range(2):
                    expert(2 * ep + n, n)
            expert(NE, 0)

        @block.scalar
        def _(act):
            act.sem_inc(gated_done, 2)
            with act.Fori(0, NE + 1) as e:
                with act.Fori(0, NCH) as c:
                    t = NCH * e + c
                    for f in range(FB):
                        act.wait_ge(g_ready, FB * t + f + 1)
                        act.wait_ge(hid_done, FB * t + f + 1)
                        act.activation(gated[:, f % 2], pg[:, f % 2], ACT.Silu).then_inc(gated_done, 1)

        @block.vector
        def _(dve):
            def split(e, slot, c):
                dve.tensor_copy(wa[:, slot, pieces(c)], raw[:, slot, pieces(c)]).then_inc(piece_a, 1)

            def expert(e, n, more, uses):
                with dve.Fori(0, NCH) as c:
                    t = NCH * e + c
                    for f in range(FB):
                        dve.wait_ge(gated_done, 2 + FB * t + f + 1)
                        dve.wait_ge(u_ready, FB * t + f + 1)
                        dve.wait_ge(b_done, FB * t + f + 1)
                        dve.tensor_tensor(hid[:, f % 2], gated[:, f % 2], pu[:, f % 2], ALU.mult).then_inc(hid_done, 1)
                        dve.wait_ge(hid_done, 2 + FB * t + f + 1)
                        dve.tensor_copy(ha[:, f], hid[:, f % 2]).then_inc(a_done, 1)
                    if more:
                        dve.wait_ge(w_in[1 - n], 48 * uses)
                        split(e + 1, 1 - n, c)
                    for tt in range(NT):
                        dve.wait_ge(y_ready, NT * t + tt + 1)
                        tile = acc[:, bass.ds(NT * c + tt, 1)].rearrange("p o n -> p (o n)")
                        dve.scalar_tensor_tensor(out=tile, in0=py[:, tt, 0:H],
                                                 scalar=weight[:].rearrange("p e t -> p (e t)")[:, bass.ds(TOK // P * e + NT * c + tt, 1)],
                                                 in1=tile, op0=ALU.mult, op1=ALU.add).then_inc(acc_done, 1)

            dve.sem_inc(hid_done, 2)
            dve.sem_inc(acc_done, 4)
            dve.wait_ge(w_in[0], 48)
            with dve.Fori(0, NCH) as c:
                split(0, 0, c)
            with dve.Fori(0, NE // 2) as ep:
                for n in range(2):
                    expert(2 * ep + n, n, True, ep + 1 + n)
            expert(NE, 0, False, 0)


def final_norm(nc, acc, out):
    with ExitStack() as stack:
        k = Kit(nc, stack, "fn")
        TT = TOK // P
        stats, mv = k.sb("stats", [P, TT, 6]), k.sb("mv", [P, TT, 2])
        std, rstd, eps = k.sb("std", [P, TT]), k.sb("rstd", [P, TT]), k.sb("eps", [P, 1])
        eps_set, stats_done, mv_done, std_done, rstd_done, y_done, stored = (k.sem(n) for n in (
            "eps_set", "stats_done", "mv_done", "std_done", "rstd_done", "y_done", "stored"))
        block = stack.enter_context(nc.Block())

        @block.sync
        def _(sp):
            for c in range(NCH):
                sp.wait_ge(y_done, NT * (c + 1))
                sp.dma_start(out[c * CH:(c + 1) * CH].rearrange("(t p) h -> p t h", p=P), acc[:, c * NT:(c + 1) * NT])\
                    .then_inc(stored, 16)
            sp.wait_ge(stored, 16 * NCH)

        @block.scalar
        def _(act):
            act.wait_ge(eps_set, 1)
            for c in range(NCH):
                act.wait_ge(mv_done, NT * (c + 1))
                tiles = slice(c * NT, (c + 1) * NT)
                act.activation(std[:, tiles], mv[:, tiles, 1], ACT.Sqrt, bias=eps[:]).then_inc(std_done, 1)

        @block.vector
        def _(dve):
            def finish(c):
                tiles = slice(c * NT, (c + 1) * NT)
                dve.wait_ge(std_done, c + 1)
                dve.reciprocal(rstd[:, tiles], std[:, tiles]).then_inc(rstd_done, 1)
                dve.wait_ge(rstd_done, c + 1)
                for n in range(c * NT, (c + 1) * NT):
                    dve.tensor_scalar(acc[:, n], acc[:, n], mv[:, n, 0:1], rstd[:, n:n + 1], ALU.subtract, ALU.mult)\
                        .then_inc(y_done, 1)

            dve.memset(eps[:], EPS).then_inc(eps_set, 1)
            for c in range(NCH):
                for n in range(c * NT, (c + 1) * NT):
                    dve.bn_stats(stats[:, n], acc[:, n]).then_inc(stats_done, 1)
                for n in range(c * NT, (c + 1) * NT):
                    dve.wait_ge(stats_done, n + 1)
                    dve.bn_aggr(mv[:, n], stats[:, n]).then_inc(mv_done, 1)
                if c:
                    finish(c - 1)
            finish(NCH - 1)


def clear_semaphores(nc):
    nc.all_engine_barrier(sems_to_clear=range(min(nc.free_semaphores), max(nc.free_semaphores) + 1))


def decoder_layer(nc, A, out):
    scr = {name: nc.dram_tensor("scr_" + name, shape, F32, kind="Internal").ap() for name, shape in dict(
        q=[2, B * H, S], k=[2, B * H, S], v=[B * NG * S, GH * AH], m=[CPB, GH * CH], craw=[B * NH * AH, S],
        cq=[2, B * H, S], ck=[2, B * H, S], cv=[TOK, H], cm=[CPB, 2 * CH], cout=[B * H, S], cden=[B * BH, S],
        mq=[2, B * H, S], mk=[2, B * H, S], mv=[TOK, H], mm=[CPB, 2 * CH], mout=[B * H, S], mden=[B * BH, S],
        comb=[B * H, S], x1=[TOK, H], xq=[2, B * H, S], xk=[2, B * H, 2 * EP], xv=[B * NG * 2 * EP, GH * AH],
        xm=[CPB, GH * CH], xcraw=[B * NH * AH, S]).items()}

    def named(**names):
        return {key: scr[name] for key, name in names.items()}

    with ExitStack() as stack:
        ident = Kit(nc, stack, "all").sb("ident", [P, P])
        identity_phase(nc, ident)
        input_projections(nc, A, scr, ident)
        attend_narrow(nc, scr)
        attend_wide(nc, named(q="cq", k="ck", v="cv", m="cm", out="cout", den="cden"), "ca")
        join_attention(nc, A, scr)
        attend_wide(nc, named(q="mq", k="mk", v="mv", m="mm", out="mout", den="mden"), "mc")
        clear_semaphores(nc)
        project_and_norm(nc, A, named(comb="comb", cout="mout", cden="mden", x1="x1", xq="xq"), ident, False)
        with ExitStack() as inner:
            k = Kit(nc, inner, "bias")
            dist, distT = k.sb("dist", [P, B, S // P, S2]), k.sb("distT", [EP, B, 2, S])
            context_projections(nc, A, scr, ident, dist, distT)
            attend_cross(nc, named(xq="xq", xk="xk", xv="xv", m="xm", craw="xcraw"), dist, distT)
        k = Kit(nc, stack, "x2")
        xa, xb = k.sb("a", [P, KH, TOK], FR), k.sb("b", [P, KH, TOK], FR)
        acc = k.sb("acc", [P, TOK // P, H])
        weight = k.sb("weight", [P, NE + 1, TOK // P])
        project_and_norm(nc, A, named(craw="xcraw", x1="x1"), ident, True, (xa, xb, acc))
        clear_semaphores(nc)
        route(nc, A, ident, xa, xb, weight)
        run_experts(nc, A, xa, xb, acc, weight)
        final_norm(nc, acc, out)


INPUTS = ["x", "ctx_1024", "fside_BxSxS2_0"] + [f"L0_attn_{n}" for n in (
    "cons_vec", "Wq", "bq", "Wk", "bk", "Wv", "bv", "cg_W", "cg_b", "am_W", "am_b", "ca_Win", "ca_bin", "ca_Wout",
    "ca_bout", "mc_Win", "mc_bin", "mc_Wout", "mc_bout", "Wo", "bo")] + [f"L0_xattn_{n}" for n in (
        "Wq", "bq", "Wk", "bk", "Wv", "bv", "Wo", "bo", "distance_scaling")] + [f"L0_ffn_{n}" for n in (
            "gate_w", "w_gate", "w_up", "w_down", "ws_gate", "ws_up", "ws_down")]


def kernel(**inputs):
    import numpy as np
    import concourse.bacc as bacc
    from concourse.bass_utils import run_bass_kernel_spmd

    nc = bacc.Bacc("TRN2", target_bir_lowering=False, num_devices=1)
    arrays, dram = {}, {}
    for name in INPUTS:
        a = np.asarray(inputs[name])
        if name in ("L0_xattn_Wq", "L0_xattn_Wk", "L0_xattn_Wv", "L0_xattn_Wo"):
            a = a.T
        if a.ndim == 0:
            a = a.reshape(1)
        a = np.ascontiguousarray(a)
        arrays[f"in_{name}_dram"] = a
        dram[name] = nc.dram_tensor(f"in_{name}_dram", a.shape, mybir.dt.from_np(a.dtype), kind="ExternalInput").ap()
    out = nc.dram_tensor("out_0_dram", (B, S, H), F32, kind="ExternalOutput").ap()
    decoder_layer(nc, dram, out.rearrange("b s h -> (b s) h"))
    r = run_bass_kernel_spmd(nc, [arrays], core_ids=[0])
    return r.results[0]["out_0_dram"]
```

```python
from contextlib import ExitStack

import concourse.bass as bass
from concourse import mybir

F32 = mybir.dt.float32
FR = mybir.dt.float32r
U32 = mybir.dt.uint32
ALU = mybir.AluOpType
ACT = mybir.ActivationFunctionType
AX = mybir.AxisListType

P = 128
B = 4
S = 1024
H = 256
KH = H // P
TOK = B * S
CH = 512
NT = CH // P
CPB = S // CH
NCH = TOK // CH
NH = 16
HD = H // NH
GH = 4
NG = NH // GH
AH = 32
BH = 4
BHD = H // BH
KC = S // P
CAUSAL_W = 0.7
META_W = (0.9 - 0.8) / 0.2 * 0.3
S2 = 154
E2 = S2 // 2
EP = 96
LOWEST = -3e38
NE = 8
D = 512
FB = D // P
EPS = 1e-5


def mm3(pe, out, la, lb, ra, rb):
    steps = [(x, y) for k in range(len(la)) for x, y in ((la[k], ra[k]), (la[k], rb[k]), (lb[k], ra[k]))]
    for n, (x, y) in enumerate(steps):
        last = pe.matmul(out, x, y, start=(n == 0), stop=(n == len(steps) - 1))
    return last


def halves(t, *rest):
    return [t[(slice(None), k, *rest)] for k in range(KH)]


def column(v):
    return v.rearrange("(c p) -> p c", p=P)


def rows(v, n=P):
    return v.rearrange("(o n) -> o n", o=1).broadcast_to([n, v.shape[0]])


class Kit:

    def __init__(self, nc, stack, name):
        self.nc, self.stack, self.name = nc, stack, name

    def sb(self, name, shape, dt=F32):
        return self.stack.enter_context(self.nc.sbuf_tensor(f"{self.name}_{name}", shape, dt))

    def ps(self, name, shape, dt=F32):
        return self.stack.enter_context(self.nc.psum_tensor(f"{self.name}_{name}", shape, dt))

    def sem(self, name):
        return self.stack.enter_context(self.nc.semaphore(f"{self.name}_{name}"))


def identity_phase(nc, ident):
    with ExitStack() as stack:
        k = Kit(nc, stack, "id")
        ones = k.sem("ones")
        done = k.sem("done")
        block = stack.enter_context(nc.Block())

        @block.vector
        def _(dve):
            dve.memset(ident[:], 1.0).then_inc(ones, 1)

        @block.gpsimd
        def _(pool):
            pool.wait_ge(ones, 1)
            pool.affine_select(out=ident[:], in_=ident[:], compare_op=ALU.is_equal, fill=0.0, base=0,
                               pattern=[[-1, P]], channel_multiplier=1).then_inc(done, 1)
            pool.wait_ge(done, 1)


def input_projections(nc, A, scr, ident):
    with ExitStack() as stack:
        k = Kit(nc, stack, "in")
        Q0, K0, G0, CQ, CK, V0, CV = (n * H for n in range(7))
        NW = 7 * H
        raw, wa, wb = k.sb("raw", [P, KH, NW]), k.sb("wa", [P, KH, NW], FR), k.sb("wb", [P, KH, NW], FR)
        cg = k.sb("cg", [P, KH, NH])
        amr = k.sb("amr", [HD + 2, NH])
        am = k.sb("am", [HD + 2, H])
        cons = k.sb("cons", [HD + 2, 1])
        gbias = k.sb("gbias", [P, KH])
        bias = k.sb("bias", [P, 4, KH])
        vbias = k.sb("vbias", [P, 2 * H])
        xt = k.sb("xt", [P, NT, H])
        xa, xb = k.sb("xa", [P, CPB, KH, CH], FR), k.sb("xb", [P, CPB, KH, CH], FR)
        mod = k.sb("mod", [P, KH, CH])
        t = k.sb("t", [P, 4, CH])
        ab = k.sb("ab", [P, 4, 2, CH])
        v16 = k.sb("v16", [P, CPB, NT, NH, AH])
        v64 = k.sb("v64", [P, CPB, NT, H])
        psx = k.ps("psx", [P, KH, CH])
        pso = k.ps("pso", [P, 2, CH])
        psg = k.ps("psg", [P, KH])
        w_in, small_in, am_in, cons_in, x_in = (k.sem(n) for n in ("w_in", "small_in", "am_in", "cons_in", "x_in"))
        cg_done, wa_done, w_done, am_done, v_set, cons_set, g_ps, g_done = (
            k.sem(n) for n in ("cg_done", "wa_done", "w_done", "am_done", "v_set", "cons_set", "g_ps", "g_done"))
        xT_ps, xa_done, xb_done = k.sem("xT_ps"), k.sem("xa_done"), k.sem("xb_done")
        mm_done, ev_act, ev_dve = k.sem("mm_done"), k.sem("ev_act"), k.sem("ev_dve")
        a_done, b_done = k.sem("a_done"), k.sem("b_done")
        part_out = [k.sem(f"part_out{n}") for n in range(4)]
        v_out = [k.sem(f"v_out{n}") for n in range(2)]
        kinds = ["mod", "q", "mod", "q"] + ["lin"] * 6 + ["v"] * NT
        wcol = [G0, Q0, G0 + P, Q0 + P, K0, K0 + P, CQ, CQ + P, CK, CK + P]
        on_act = [x in ("mod", "lin") for x in kinds]
        nth = [sum(on_act[:n]) if on_act[n] else n - sum(on_act[:n]) for n in range(len(kinds))]
        NB = len(kinds)
        VS = 16 * (NT + 1)
        TURN = 8
        NA = sum(on_act)
        ND = NB - NA
        split = [n for n in range(NB) if kinds[n] in ("q", "lin")]
        NS = len(split)
        dest = [(scr["q"], 0), (scr["q"], 1), (scr["k"], 0), (scr["k"], 1), (scr["cq"], 0), (scr["cq"], 1),
                (scr["ck"], 0), (scr["ck"], 1)]
        x_v = A["x"].rearrange("b (c t p) h -> (b c) p t h", c=CPB, p=P)
        v_v = scr["v"].rearrange("(b g s) c -> b s g c", b=B, g=NG)
        block = stack.enter_context(nc.Block())

        @block.sync
        def _(sp):
            for src, col in ((A["L0_attn_Wq"], Q0), (A["L0_attn_Wk"], K0), (A["L0_attn_Wv"], V0)):
                sp.dma_start(raw[:, :, col:col + H], src.rearrange("(k p) n -> p k n", p=P)).then_inc(w_in, 16)
            ca = A["L0_attn_ca_Win"].rearrange("(k p) n -> p k n", p=P)
            sp.dma_start(raw[:, :, CQ:CQ + 2 * H], ca[:, :, 0:2 * H]).then_inc(w_in, 16)
            sp.dma_start(raw[:, :, CV:CV + H], ca[:, :, 2 * H:3 * H]).then_inc(w_in, 16)
            sp.dma_start(cg[:], A["L0_attn_cg_W"].rearrange("(k p) n -> p k n", p=P)).then_inc(small_in, 16)
            sp.dma_start(bias[:, 0, :], column(A["L0_attn_bq"]), allow_slow_non_contiguous=True).then_inc(small_in, 16)
            sp.dma_start(bias[:, 1, :], column(A["L0_attn_bk"]), allow_slow_non_contiguous=True).then_inc(small_in, 16)
            sp.dma_start(bias[:, 2, :], column(A["L0_attn_ca_bin"][0:H]), allow_slow_non_contiguous=True).then_inc(small_in, 16)
            sp.dma_start(bias[:, 3, :], column(A["L0_attn_ca_bin"][H:2 * H]), allow_slow_non_contiguous=True).then_inc(small_in, 16)
            sp.dma_start(vbias[:, 0:H], rows(A["L0_attn_bv"])).then_inc(small_in, 16)
            sp.dma_start(vbias[:, H:2 * H], rows(A["L0_attn_ca_bin"][2 * H:3 * H])).then_inc(small_in, 16)
            sp.dma_start(amr[0:HD, :], A["L0_attn_am_W"]).then_inc(am_in, 16)
            sp.dma_start(amr[HD:HD + 1, :], A["L0_attn_am_b"].rearrange("(o n) -> o n", o=1)).then_inc(am_in, 16)
            sp.dma_start(amr[HD + 1:HD + 2, :], A["L0_attn_cg_b"].rearrange("(o n) -> o n", o=1)).then_inc(am_in, 16)
            sp.wait_ge(cons_set, 1)
            sp.dma_start(cons[0:HD, :], A["L0_attn_cons_vec"].rearrange("(p o) -> p o", o=1), allow_slow_non_contiguous=True).then_inc(cons_in, 16)
            for n in range(4):
                sp.sem_inc(part_out[n], 16)
            for n in range(2):
                sp.sem_inc(v_out[n], VS)
            with sp.Fori(0, B) as b:
                for hf in range(CPB):
                    i = 2 * b + hf
                    for s in range(NS):
                        sp.wait_ge(b_done, 4 + NS * i + s + 1)
                        dst, j = dest[s]
                        sp.dma_start(dst[:, bass.ds(b * H + j * P, P), hf * CH:(hf + 1) * CH]
                                     .rearrange("a p n -> p a n"), ab[:, s % 4]).then_inc(part_out[s % 4], 16)
                    for tt in range(NT):
                        sp.wait_ge(ev_dve, 2 + ND * i + ND - NT + tt + 1)
                        tok = hf * CH + tt * P
                        sp.dma_start(v_v[bass.ds(b, 1), tok:tok + P].rearrange("o p g c -> p (o g) c"),
                                     v16[:, hf, tt].rearrange("p (g h) c -> p g (h c)", g=NG)).then_inc(v_out[hf], 16)
                    sp.dma_start(scr["cv"][bass.ds(b * S + hf * CH, CH)].rearrange("(t p) c -> p t c", p=P), v64[:, hf])\
                        .then_inc(v_out[hf], 16)
            for n in range(4):
                sp.wait_ge(part_out[n], 16 * (1 + NCH * NS // 4))
            for n in range(2):
                sp.wait_ge(v_out[n], VS * (1 + B))

        @block.gpsimd
        def _(pool):
            pool.memset(cons[:], 1.0).then_inc(cons_set, 1)
            pool.memset(v16[:], 0.0).then_inc(v_set, 1)
            pool.wait_ge(v_set, 1)
            pool.memset(v16[:, :, :, :, HD:HD + 1], 1.0).then_inc(v_set, 1)
            pool.sem_inc(b_done, 4)
            with pool.Fori(0, B) as b:
                for hf in range(CPB):
                    i = 2 * b + hf
                    for s in range(NS):
                        pool.wait_ge(a_done, NS * i + s + 1)
                        pool.tensor_tensor(ab[:, s % 4, 1], t[:, s % 4], ab[:, s % 4, 0], ALU.subtract).then_inc(b_done, 1)

        @block.tensor
        def _(pe):
            pe.wait_ge(cons_in, 16)
            pe.wait_ge(am_done, 1)
            for j in range(KH):
                last = pe.matmul(psg[:, j:j + 1], am[:, j * P:(j + 1) * P], cons[:], start=True, stop=True)
            last.then_inc(g_ps, 1)

            def turn(i):
                pe.wait_ge(x_in, 16 * i + 16)
                pe.wait_ge(xb_done, i + 1)
                for kh in range(KH):
                    for tt in range(NT):
                        last = pe.transpose(psx[:, kh, tt * P:(tt + 1) * P], xt[:, tt, kh * P:(kh + 1) * P], ident[:])
                last.then_inc(xT_ps, 1)

            def chunk(i, hf, more):
                pe.wait_ge(xb_done, i + 2)
                la, lb = halves(xa[:, hf]), halves(xb[:, hf])
                for n in range(NB):
                    if n == TURN and more:
                        turn(i + 1)
                    if n < 2:
                        pe.wait_ge(ev_dve, ND * i + n + 1)
                    else:
                        if on_act[n - 2]:
                            pe.wait_ge(ev_act, NA * i + nth[n - 2] + 1)
                        else:
                            pe.wait_ge(ev_dve, 2 + ND * i + nth[n - 2] + 1)
                    if kinds[n] == "v":
                        tok = slice((n - NB + NT) * P, (n - NB + NT + 1) * P)
                        mm3(pe, pso[:, n % 2], [x[:, tok] for x in la], [x[:, tok] for x in lb],
                            halves(wa, slice(V0, V0 + 2 * H)), halves(wb, slice(V0, V0 + 2 * H))).then_inc(mm_done, 1)
                    else:
                        w = slice(wcol[n], wcol[n] + P)
                        mm3(pe, pso[:, n % 2], halves(wa, w), halves(wb, w), la, lb).then_inc(mm_done, 1)

            turn(0)
            pe.wait_ge(w_done, 1)
            with pe.Fori(0, B - 1) as b:
                for hf in range(CPB):
                    chunk(2 * b + hf, hf, True)
            for hf in range(CPB):
                chunk(NCH - CPB + hf, hf, hf == 0)

        @block.scalar
        def _(act):
            def load(i):
                act.dma_start(xt[:], x_v[bass.ds(i, 1)].rearrange("o p t h -> p (o t) h")).then_inc(x_in, 16)

            def take(i, slot, more):
                act.wait_ge(xT_ps, i + 1)
                act.activation(xa[:, slot], psx[:], ACT.Copy).then_inc(xa_done, 1)
                if more:
                    load(i + 1)

            def chunk(i, hf, ahead):
                for n in range(NB):
                    if n == TURN and ahead:
                        take(i + 1, 1 - hf, ahead > 1)
                    if not on_act[n]:
                        continue
                    act.wait_ge(mm_done, NB * i + n + 1)
                    if kinds[n] == "mod":
                        j = n // 2
                        act.activation(mod[:, j], pso[:, n % 2], ACT.Sigmoid, bias=gbias[:, j:j + 1]).then_inc(ev_act, 1)
                    else:
                        s = split.index(n)
                        act.wait_ge(b_done, NS * i + s + 1)
                        act.activation(t[:, s % 4], pso[:, n % 2], ACT.Identity,
                                       bias=bias[:, s // 2, s % 2:s % 2 + 1]).then_inc(ev_act, 1)

            load(0)
            take(0, 0, True)
            act.wait_ge(small_in, 16 * 7)
            act.wait_ge(g_done, 1)
            with act.Fori(0, B - 1) as b:
                for hf in range(CPB):
                    chunk(2 * b + hf, hf, 2)
            for hf in range(CPB):
                chunk(NCH - CPB + hf, hf, 1 - hf)

        @block.vector
        def _(dve):
            dve.wait_ge(small_in, 16 * 7)
            dve.sem_inc(xb_done, 1)
            dve.sem_inc(ev_dve, 2)
            for kh in range(KH):
                dve.tensor_copy(raw[:, kh, G0:G0 + H].rearrange("p (h d) -> p h d", h=NH),
                                cg[:, kh].unsqueeze(2).broadcast_to([P, NH, HD])).then_inc(cg_done, 1)
            dve.wait_ge(am_in, 48)
            dve.tensor_copy(am[:].rearrange("p (h d) -> p h d", h=NH),
                            amr[:].unsqueeze(2).broadcast_to([HD + 2, NH, HD])).then_inc(am_done, 1)
            dve.wait_ge(w_in, 16 * 5)
            dve.wait_ge(cg_done, KH)
            dve.tensor_copy(wa[:], raw[:]).then_inc(wa_done, 1)
            dve.wait_ge(wa_done, 1)
            dve.tensor_tensor(wb[:], raw[:], wa[:].bitcast(F32), ALU.subtract).then_inc(w_done, 1)
            dve.wait_ge(g_ps, 1)
            dve.tensor_copy(gbias[:], psg[:]).then_inc(g_done, 1)
            dve.wait_ge(v_set, 2)

            def take(i, slot):
                dve.wait_ge(xa_done, i + 1)
                dve.tensor_tensor(xb[:, slot], psx[:], xa[:, slot].bitcast(F32), ALU.subtract).then_inc(xb_done, 1)

            take(0, 0)

            def chunk(b, hf, more):
                i = CPB * b + hf
                for n in range(NB):
                    if n == TURN and more:
                        take(i + 1, 1 - hf)
                    if kinds[n] == "mod":
                        continue
                    if kinds[n] == "q":
                        s, j = split.index(n), n // 2
                        dve.wait_ge(mm_done, NB * i + n + 1)
                        dve.wait_ge(ev_act, NA * i + nth[n - 1] + 1)
                        dve.wait_ge(b_done, NS * i + s + 1)
                        dve.scalar_tensor_tensor(out=t[:, s % 4], in0=pso[:, n % 2], scalar=bias[:, 0, j:j + 1],
                                                 in1=mod[:, j], op0=ALU.add, op1=ALU.mult).then_inc(ev_dve, 1)
                        dve.wait_ge(ev_dve, 2 + ND * i + nth[n] + 1)
                    if kinds[n] == "lin":
                        s = split.index(n)
                        dve.wait_ge(ev_act, NA * i + nth[n] + 1)
                    if kinds[n] != "v":
                        dve.wait_ge(part_out[s % 4], 16 * (NS // 4 * i + s // 4 + 1))
                        dve.tensor_copy(ab[:, s % 4, 0].bitcast(FR), t[:, s % 4]).then_inc(a_done, 1)
                        continue
                    tt = n - NB + NT
                    dve.wait_ge(mm_done, NB * i + n + 1)
                    if tt == 0:
                        dve.wait_ge(v_out[hf], VS * b + VS)
                    dve.tensor_tensor(v16[:, hf, tt, :, 0:HD], pso[:, n % 2, 0:H].rearrange("p (h d) -> p h d", h=NH),
                                      vbias[:, 0:H].rearrange("p (h d) -> p h d", h=NH), ALU.add)
                    dve.tensor_tensor(v64[:, hf, tt], pso[:, n % 2, H:2 * H], vbias[:, H:2 * H], ALU.add).then_inc(ev_dve, 1)

            with dve.Fori(0, B - 1) as b:
                for hf in range(CPB):
                    chunk(b, hf, True)
            for hf in range(CPB):
                chunk(B - 1, hf, hf == 0)


def attend_narrow(nc, scr):
    with ExitStack() as stack:
        k = Kit(nc, stack, "an")
        ONE, LAST = 4 * HD, 6 * HD
        MROW = LAST - 1
        NSTEP = CPB * KC
        RING = 3
        NST = GH * NSTEP
        qs, ks = k.sb("qs", [LAST, NG, GH, S], FR), k.sb("ks", [LAST, NG, GH, S], FR)
        vs = k.sb("vs", [P, NG, KC, GH * AH])
        probs = k.sb("probs", [P, 2, GH, CH])
        ev = k.sb("ev", [P, CPB, CH])
        m1 = k.sb("m1", [P, CPB, GH * NT])
        mneg, mturn = k.sb("mneg", [P, 32]), k.sb("mturn", [P, 32])
        mrows = k.sb("mrows", [P, CPB, 32], FR)
        pst = k.ps("pst", [P, RING, CH])
        psm = k.ps("psm", [P, 2, 2, CH])
        pacc = k.ps("pacc", [P, CH])
        filled, filled_first, mneg_set = k.sem("filled"), k.sem("filled_first"), k.sem("mneg_set")
        loaded = [k.sem(f"loaded{n}") for n in range(NG)]
        mrow_in = [[k.sem(f"mrow_in{n}{h}") for h in range(CPB)] for n in range(NG)]
        m_out = [k.sem(f"m_out{h}") for h in range(CPB)]
        ev_out = [k.sem(f"ev_out{h}") for h in range(CPB)]
        mx_ready, mx_done, m_chain, m_ready, row_moved = (
            k.sem(n) for n in ("mx_ready", "mx_done", "m_chain", "m_ready", "row_moved"))
        st_ready, exp_done, pv_done = (k.sem(n) for n in ("st_ready", "exp_done", "pv_done"))
        acc_act, acc_dve = k.sem("acc_act"), k.sem("acc_dve")
        LOADS = 9
        PV0 = NSTEP * (NG - 1) + 2
        mx_list = [(hq, j, i) for hq in range(CPB) for j in range(GH) for i in range(NT)]
        NM = len(mx_list)
        block = stack.enter_context(nc.Block())

        def last_use(n):
            return n - RING if n >= RING else max(m for m in range(NST) if m % RING == n) - NST

        @block.sync
        def _(sp):
            def load(G, slot):
                sp.wait_ge(pv_done, PV0 + NSTEP * (G - NG + 1))
                for r, (qp, kp) in enumerate(((0, 0), (0, 1), (1, 0), (1, 1))):
                    for dst, src, part in ((qs, scr["q"], qp), (ks, scr["k"], kp)):
                        sp.dma_start(dst[r * HD:(r + 1) * HD, slot].bitcast(F32),
                                     src[part, bass.ds(G * GH * HD, GH * HD)].rearrange("(j d) n -> d j n", j=GH))\
                            .then_inc(loaded[slot], 16)
                sp.dma_start(vs[:, slot], scr["v"][bass.ds(G * S, S)].rearrange("(c p) n -> p c n", p=P))\
                    .then_inc(loaded[slot], 16)

            def max_row(G, slot, uses, hq):
                sp.wait_ge(m_ready, CPB * G + hq + 1)
                turned = scr["m"][hq].rearrange("(c b r) -> b c r", b=4, r=32)
                for q in range(4):
                    sp.dma_start(turned[q], mrows[32 * q:32 * q + GH * NT, hq].bitcast(F32)).then_inc(m_out[hq], 16)
                sp.wait_ge(m_out[hq], 64 * G + 64)
                sp.dma_start(qs[MROW:LAST, slot, :, hq * CH:(hq + 1) * CH].bitcast(F32),
                             scr["m"][hq:hq + 1].rearrange("o (j n) -> o j n", j=GH)).then_inc(mrow_in[slot][hq], 16)
                sp.wait_ge(mrow_in[slot][hq], 16 * uses + 16)
                sp.sem_inc(row_moved, 1)

            def store(G, qh):
                if qh == 0:
                    sp.wait_ge(acc_act, G + 2)
                else:
                    sp.wait_ge(acc_dve, G + 2)
                sp.dma_start(scr["craw"][bass.ds(G * P, P), qh * CH:(qh + 1) * CH], ev[:, qh]).then_inc(ev_out[qh], 16)

            def group(b, g, ahead):
                G = b * NG + g
                if ahead >= 2:
                    load(G + 2, (g + 2) % NG)
                if ahead >= 1:
                    max_row(G + 1, (g + 1) % NG, b + (g + 1) // NG, 0)
                store(G, 0)
                if ahead >= 1:
                    max_row(G + 1, (g + 1) % NG, b + (g + 1) // NG, 1)
                store(G, 1)

            for qh in range(CPB):
                sp.sem_inc(ev_out[qh], 16)
            load(0, 0)
            load(1, 1)
            for hq in range(CPB):
                max_row(0, 0, 0, hq)
            with sp.Fori(0, B - 1) as b:
                for g in range(NG):
                    group(b, g, 2)
            for g in range(NG):
                group(B - 1, g, NG - 1 - g)
            for qh in range(CPB):
                sp.wait_ge(ev_out[qh], 16 + 16 * B * NG)

        @block.gpsimd
        def _(pool):
            pool.memset(qs[ONE:LAST, 0].bitcast(F32), 0.0).then_inc(filled, 1)
            for slot in range(1, NG):
                pool.memset(qs[ONE:LAST, slot].bitcast(F32), 0.0).then_inc(filled, 1)
                pool.memset(ks[ONE:LAST, slot].bitcast(F32), 1.0).then_inc(filled, 1)

        @block.tensor
        def _(pe):
            def maxima(G, slot, uses, n, kh):
                hq, j, i = mx_list[n]
                if n == 0 and kh == 0:
                    pe.wait_ge(filled, 2 * slot + 1)
                    pe.wait_ge(filled_first, 1)
                    pe.wait_ge(loaded[slot], 16 * LOADS * uses + 16 * LOADS)
                if kh == 0:
                    pe.wait_ge(mx_done, NM * G + n + 1)
                q0 = (hq * NT + i) * P
                last = pe.matmul(psm[:, n % 2, kh], qs[0:MROW, slot, j, q0:q0 + P], ks[0:MROW, slot, j, kh * CH:(kh + 1) * CH],
                                 start=True, stop=True)
                if kh == 1:
                    last.then_inc(mx_ready, 1)

            def values(G, slot, s):
                qh, kc = divmod(s, KC)
                pe.wait_ge(exp_done, RING + GH * (NSTEP * G + s + 1))
                if kc == 0:
                    pe.wait_ge(*((acc_dve, G + 1) if qh == 0 else (acc_act, G + 2)))
                for j in range(GH):
                    last = pe.matmul(pacc[j * AH:(j + 1) * AH], vs[:, slot, kc, j * AH:(j + 1) * AH],
                                     probs[:, s % 2, j], start=(kc == 0), stop=(kc == KC - 1))
                last.then_inc(pv_done, 1)

            def group(b, g, more):
                G = b * NG + g
                nxt = (G + 1, (g + 1) % NG, b + (g + 1) // NG)
                for s in range(NSTEP):
                    qh, kc = divmod(s, KC)
                    if kc == 0:
                        pe.wait_ge(mrow_in[g][qh], 16 * b + 16)
                    for j in range(GH):
                        n = GH * s + j
                        pe.wait_ge(exp_done, RING + NST * G + last_use(n) + 1)
                        pe.matmul(pst[:, n % RING], ks[:, g, j, kc * P:(kc + 1) * P], qs[:, g, j, qh * CH:(qh + 1) * CH],
                                  start=True, stop=True).then_inc(st_ready, 1)
                        if s > 0 and j == 2:
                            values(G, g, s - 1)
                        if more and j % 2 == 0:
                            for kh in range(2):
                                maxima(*nxt, 2 * s + j // 2, kh)
                values(G, g, NSTEP - 1)

            pe.sem_inc(pv_done, PV0)
            for n in range(NM):
                for kh in range(2):
                    maxima(0, 0, 0, n, kh)
            with pe.Fori(0, B - 1) as b:
                for g in range(NG):
                    group(b, g, True)
            for g in range(NG):
                group(B - 1, g, g < NG - 1)

        @block.scalar
        def _(act):
            def group(b, g):
                G = b * NG + g
                for s in range(NSTEP):
                    for j in range(GH):
                        act.wait_ge(st_ready, GH * (NSTEP * G + s) + j + 1)
                        if j == 0:
                            act.wait_ge(pv_done, PV0 + NSTEP * G + s - 1)
                        act.activation(probs[:, s % 2, j], pst[:, (GH * s + j) % RING], ACT.Exp, scale=HD ** -0.5).then_inc(exp_done, 1)
                    if s == KC:
                        act.wait_ge(pv_done, PV0 + NSTEP * G + KC)
                        act.wait_ge(ev_out[0], 16 * G + 16)
                        act.activation(ev[:, 0], pacc[:], ACT.Copy).then_inc(acc_act, 1)

            act.sem_inc(exp_done, RING)
            act.sem_inc(acc_act, 1)
            with act.Fori(0, B) as b:
                for g in range(NG):
                    group(b, g)

        @block.vector
        def _(dve):
            def maxima(G, lo, hi):
                for n in range(lo, hi):
                    hq, j, i = mx_list[n]
                    dve.wait_ge(mx_ready, NM * G + n + 1)
                    col = j * NT + i
                    dve.tensor_reduce(m1[:, hq, col:col + 1], psm[:, n % 2], AX.XY, ALU.max).then_inc(mx_done, 1)

            def finish(G, hq, first):
                dve.wait_ge(mx_done, 2 + NM * G + (hq + 1) * NM // CPB)
                dve.tensor_scalar(mneg[:, 0:GH * NT], m1[:, hq], -1.0, None, ALU.mult).then_inc(m_chain, 1)
                dve.wait_ge(m_chain, 2 * (CPB * G + hq) + 1)
                dve.transpose(mturn[:], mneg[:]).then_inc(m_chain, 1)
                dve.wait_ge(m_chain, 2 * (CPB * G + hq) + 2)
                if not first:
                    dve.wait_ge(row_moved, CPB * (G - 1) + hq + 1)
                dve.tensor_copy(mrows[:, hq], mturn[:]).then_inc(m_ready, 1)

            def group(b, g, more):
                G = b * NG + g
                if more:
                    for hq in range(CPB):
                        maxima(G + 1, hq * NM // CPB, (hq + 1) * NM // CPB)
                        finish(G + 1, hq, False)
                dve.wait_ge(pv_done, PV0 + NSTEP * G + NSTEP)
                dve.wait_ge(ev_out[1], 16 * G + 16)
                dve.tensor_copy(ev[:, 1], pacc[:]).then_inc(acc_dve, 1)

            dve.sem_inc(mx_done, 2)
            dve.sem_inc(acc_dve, 1)
            dve.memset(mneg[:], 0.0).then_inc(mneg_set, 1)
            dve.memset(ks[ONE:LAST, 0].bitcast(F32), 1.0).then_inc(filled_first, 1)
            dve.wait_ge(mneg_set, 1)
            for hq in range(CPB):
                maxima(0, hq * NM // CPB, (hq + 1) * NM // CPB)
                finish(0, hq, True)
            with dve.Fori(0, B - 1) as b:
                for g in range(NG):
                    group(b, g, True)
            for g in range(NG):
                group(B - 1, g, g < NG - 1)


def attend_wide(nc, src, name):
    with ExitStack() as stack:
        k = Kit(nc, stack, name)
        HP = 2
        NP = BH // HP
        NSTEP = CPB * KC
        MROW = P - 1
        RING = 4
        ADD0 = RING
        ONES = 32
        PV0 = NSTEP * (NP - 1) + RING
        MAX_LOADS, LOADS = 4, 3
        qs, ks = k.sb("qs", [P, NP, 2, HP, S], FR), k.sb("ks", [P, NP, 2, HP, S], FR)
        vs = k.sb("vs", [P, NP, KC, HP * BHD])
        ones = k.sb("ones", [P, ONES])
        probs = k.sb("probs", [P, RING, HP, CH])
        sums = k.sb("sums", [P, CPB, HP, CH])
        ev, evd = k.sb("ev", [P, CPB, CH]), k.sb("evd", [HP * ONES, CPB, CH])
        m1 = k.sb("m1", [P, CPB, HP * NT])
        mneg, mturn = k.sb("mneg", [P, 32]), k.sb("mturn", [P, 32])
        mrows = k.sb("mrows", [P, CPB, 32], FR)
        pst = k.ps("pst", [P, HP, CH])
        psm = k.ps("psm", [P, 2, 2, CH])
        pacc = k.ps("pacc", [P, CH])
        pden = k.ps("pden", [P, CH])
        filled_q, filled_k, mneg_set = k.sem("filled_q"), k.sem("filled_k"), k.sem("mneg_set")
        loaded_max = [k.sem(f"loaded_max{n}") for n in range(NP)]
        loaded = [k.sem(f"loaded{n}") for n in range(NP)]
        mrow_in = [[k.sem(f"mrow_in{n}{h}") for h in range(CPB)] for n in range(NP)]
        m_out = [k.sem(f"m_out{h}") for h in range(CPB)]
        ev_out = [k.sem(f"ev_out{h}") for h in range(CPB)]
        ones_set = k.sem("ones_set")
        mx_ready, mx_done, m_chain, m_ready, row_moved = (
            k.sem(n) for n in ("mx_ready", "mx_done", "m_chain", "m_ready", "row_moved"))
        st_ready, exp_done, pv_done, acc_out, den_ready, den_out = (
            k.sem(n) for n in ("st_ready", "exp_done", "pv_done", "acc_out", "den_ready", "den_out"))
        sum_done = [k.sem(f"sum_done{j}") for j in range(HP)]
        mx_list = [(hq, j, i) for hq in range(CPB) for j in range(HP) for i in range(NT)]
        NM = len(mx_list)
        HALF = NM // CPB
        FROM = 6
        upto = [0 if s < FROM else 2 * -(-(s - FROM + 1) * NM // (NSTEP - FROM)) for s in range(NSTEP)]
        block = stack.enter_context(nc.Block())

        def adds_before(G, s):
            x = s - RING
            x += x % KC == 0
            return ADD0 + (KC - 1) * (CPB * G + x // KC) + x % KC

        @block.sync
        def _(sp):
            def load(G, slot):
                sp.wait_ge(pv_done, PV0 + NSTEP * (G - NP + 1))
                for dst, src_, n, r, part in ((qs, "q", 0, 0, 0), (ks, "k", 0, 0, 0), (qs, "q", 0, 1, 0), (ks, "k", 0, 1, 1),
                                              (qs, "q", 1, 0, 1), (ks, "k", 1, 0, 0)):
                    sp.dma_start(dst[r * BHD:(r + 1) * BHD, slot, n].bitcast(F32),
                                 src[src_][part, bass.ds(G * P, P)].rearrange("(j d) n -> d j n", j=HP))\
                        .then_inc(loaded[slot] if n else loaded_max[slot], 16)

            def load_v(b, slot):
                sp.dma_start(vs[:, slot], src["v"][bass.ds(b * S, S), slot * P:(slot + 1) * P]
                             .rearrange("(c p) n -> p c n", p=P)).then_inc(loaded[slot], 16)

            def max_row(G, slot, uses, hq):
                sp.wait_ge(m_ready, CPB * G + hq + 1)
                turned = src["m"][hq].rearrange("(c b r) -> b c r", b=4, r=32)
                for q in range(4):
                    sp.dma_start(turned[q], mrows[32 * q:32 * q + HP * NT, hq].bitcast(F32)).then_inc(m_out[hq], 16)
                sp.wait_ge(m_out[hq], 64 * G + 64)
                sp.dma_start(qs[MROW:P, slot, 1, :, hq * CH:(hq + 1) * CH].bitcast(F32),
                             src["m"][hq:hq + 1].rearrange("o (j n) -> o j n", j=HP)).then_inc(mrow_in[slot][hq], 16)
                sp.wait_ge(mrow_in[slot][hq], 16 * uses + 16)
                sp.sem_inc(row_moved, 1)

            def store(G, qh):
                sp.wait_ge(acc_out, CPB * G + qh + 2)
                sp.wait_ge(den_out, CPB * G + qh + 2)
                sp.dma_start(src["out"][bass.ds(G * P, P), qh * CH:(qh + 1) * CH], ev[:, qh]).then_inc(ev_out[qh], 16)
                for j in range(HP):
                    sp.dma_start(src["den"][bass.ds(G * HP + j, 1), qh * CH:(qh + 1) * CH],
                                 evd[j * ONES:j * ONES + 1, qh]).then_inc(ev_out[qh], 16)

            def group(b, g, ahead):
                G = b * NP + g
                store(G, 0)
                if ahead >= 1:
                    max_row(G + 1, (g + 1) % NP, b + (g + 1) // NP, 0)
                if ahead >= 2:
                    load(G + NP, g)
                    load_v(b + 1, g)
                store(G, 1)
                if ahead >= 1:
                    max_row(G + 1, (g + 1) % NP, b + (g + 1) // NP, 1)

            for qh in range(CPB):
                sp.sem_inc(ev_out[qh], 48)
            for slot in range(NP):
                load(slot, slot)
                load_v(0, slot)
            for hq in range(CPB):
                max_row(0, 0, 0, hq)
            with sp.Fori(0, B - 1) as b:
                for g in range(NP):
                    group(b, g, 2)
            for g in range(NP):
                group(B - 1, g, NP - 1 - g)
            for qh in range(CPB):
                sp.wait_ge(ev_out[qh], 48 + 48 * B * NP)

        def add_up(eng, j, G, s):
            qh, kc = divmod(s, KC)
            if kc == 0:
                return
            eng.wait_ge(exp_done, 2 + HP * (NSTEP * G + s) + j + 1)
            adds = (KC - 1) * (CPB * G + qh)
            if kc == 1:
                eng.wait_ge(den_ready, CPB * G + qh + 1)
                before = probs[:, (s - 1) % RING, j]
            else:
                eng.wait_ge(sum_done[j], ADD0 + adds + kc - 1)
                before = sums[:, qh, j]
            eng.tensor_tensor(sums[:, qh, j], before, probs[:, s % RING, j], ALU.add).then_inc(sum_done[j], 1)

        @block.gpsimd
        def _(pool):
            for slot in range(NP):
                pool.memset(qs[BHD:P, slot, 1].bitcast(F32), 0.0).then_inc(filled_q, 1)
            pool.sem_inc(sum_done[1], ADD0)
            pool.wait_ge(filled_q, NP)
            with pool.Fori(0, B) as b:
                for g in range(NP):
                    for s in range(NSTEP):
                        add_up(pool, 1, b * NP + g, s)

        @block.tensor
        def _(pe):
            def maxima(G, slot, uses, lo, hi):
                for u in range(lo, hi):
                    n, kh = divmod(u, 2)
                    hq, j, i = mx_list[n]
                    if u == 0:
                        pe.wait_ge(filled_q, slot + 1)
                        pe.wait_ge(filled_k, slot + 1)
                        pe.wait_ge(loaded_max[slot], 16 * MAX_LOADS * uses + 16 * MAX_LOADS)
                    if kh == 0:
                        pe.wait_ge(mx_done, NM * G + n + 1)
                    q0 = (hq * NT + i) * P
                    last = pe.matmul(psm[:, n % 2, kh], qs[:, slot, 0, j, q0:q0 + P], ks[:, slot, 0, j, kh * CH:(kh + 1) * CH],
                                     start=True, stop=True)
                    if kh == 1:
                        last.then_inc(mx_ready, 1)

            def values(G, slot, s):
                qh, kc = divmod(s, KC)
                pe.wait_ge(exp_done, 2 + HP * (NSTEP * G + s + 1))
                if kc == 0:
                    pe.wait_ge(acc_out, CPB * G + qh + 1)
                for j in range(HP):
                    last = pe.matmul(pacc[j * BHD:(j + 1) * BHD], vs[:, slot, kc, j * BHD:(j + 1) * BHD], probs[:, s % RING, j],
                                     start=(kc == 0), stop=(kc == KC - 1))
                last.then_inc(pv_done, 1)

            def row_sums(G, qh):
                for j in range(HP):
                    pe.wait_ge(sum_done[j], ADD0 + (KC - 1) * (CPB * G + qh + 1))
                pe.wait_ge(den_out, CPB * G + qh + 1)
                for j in range(HP):
                    last = pe.matmul(pden[j * ONES:(j + 1) * ONES], ones[:], sums[:, qh, j], start=True, stop=True)
                last.then_inc(den_ready, 1)

            def group(b, g, more):
                G = b * NP + g
                nxt = (G + 1, (g + 1) % NP, b + (g + 1) // NP)
                pe.wait_ge(loaded[g], 16 * LOADS * b + 16 * LOADS)
                for s in range(NSTEP):
                    qh, kc = divmod(s, KC)
                    if kc == 0:
                        pe.wait_ge(mrow_in[g][qh], 16 * b + 16)
                    lo, hi = (upto[s - 1] if s else 0), upto[s]
                    for j in range(HP):
                        pe.wait_ge(exp_done, HP * (NSTEP * G + s) + j + 1)
                        for n in range(2):
                            last = pe.matmul(pst[:, j], ks[:, g, n, j, kc * P:(kc + 1) * P],
                                             qs[:, g, n, j, qh * CH:(qh + 1) * CH], start=(n == 0), stop=(n == 1))
                        last.then_inc(st_ready, 1)
                        if more:
                            mid = (lo + hi) // 2
                            maxima(*nxt, *((lo, mid) if j == 0 else (mid, hi)))
                        if s > 0 and j == 1:
                            values(G, g, s - 1)
                    if s == KC + 2:
                        row_sums(G, 0)
                values(G, g, NSTEP - 1)
                row_sums(G, 1)

            pe.sem_inc(pv_done, PV0)
            pe.sem_inc(den_ready, 2)
            pe.wait_ge(ones_set, 1)
            maxima(0, 0, 0, 0, 2 * NM)
            with pe.Fori(0, B - 1) as b:
                for g in range(NP):
                    group(b, g, True)
            for g in range(NP):
                group(B - 1, g, g < NP - 1)

        @block.scalar
        def _(act):
            def copy_out(G, qh):
                act.wait_ge(pv_done, PV0 + NSTEP * G + KC * (qh + 1))
                act.wait_ge(ev_out[qh], 48 * G + 48)
                act.activation(ev[:, qh], pacc[:], ACT.Copy).then_inc(acc_out, 1)

            act.sem_inc(exp_done, 2)
            act.sem_inc(acc_out, 1)
            with act.Fori(0, B) as b:
                for g in range(NP):
                    G = b * NP + g
                    for s in range(NSTEP):
                        qh, kc = divmod(s, KC)
                        for j in range(HP):
                            act.wait_ge(st_ready, HP * (NSTEP * G + s) + j + 1)
                            if j == 0:
                                act.wait_ge(pv_done, PV0 + NSTEP * G + s - RING + 1)
                            act.wait_ge(sum_done[j], adds_before(G, s))
                            act.activation(probs[:, s % RING, j], pst[:, j], ACT.Exp, scale=BHD ** -0.5).then_inc(exp_done, 1)
                        if s == KC:
                            copy_out(G, 0)
                    copy_out(G, 1)

        @block.vector
        def _(dve):
            def maxima(G, lo, hi):
                for n in range(lo // 2, hi // 2):
                    hq, j, i = mx_list[n]
                    dve.wait_ge(mx_ready, NM * G + n + 1)
                    col = j * NT + i
                    dve.tensor_reduce(m1[:, hq, col:col + 1], psm[:, n % 2], AX.XY, ALU.max).then_inc(mx_done, 1)
                    if n % HALF == HALF - 1:
                        finish(G, hq)

            def finish(G, hq):
                dve.wait_ge(mx_done, 2 + NM * G + (hq + 1) * HALF)
                dve.tensor_scalar(mneg[:, 0:HP * NT], m1[:, hq], -1.0, None, ALU.mult).then_inc(m_chain, 1)
                dve.wait_ge(m_chain, 2 * (CPB * G + hq) + 1)
                dve.transpose(mturn[:], mneg[:]).then_inc(m_chain, 1)
                dve.wait_ge(m_chain, 2 * (CPB * G + hq) + 2)
                if not (isinstance(G, int) and G == 0):
                    dve.wait_ge(row_moved, CPB * (G - 1) + hq + 1)
                dve.tensor_copy(mrows[:, hq], mturn[:]).then_inc(m_ready, 1)

            def copy_out(G, qh):
                dve.wait_ge(den_ready, 2 + CPB * G + qh + 1)
                dve.wait_ge(ev_out[qh], 48 * G + 48)
                dve.tensor_copy(evd[:, qh], pden[0:HP * ONES]).then_inc(den_out, 1)

            def group(b, g, more):
                G = b * NP + g
                for s in range(NSTEP):
                    add_up(dve, 0, G, s)
                    if s == KC + 3:
                        copy_out(G, 0)
                    if more:
                        maxima(G + 1, upto[s - 1] if s else 0, upto[s])
                copy_out(G, 1)

            dve.sem_inc(mx_done, 2)
            dve.sem_inc(den_out, 1)
            dve.sem_inc(sum_done[0], ADD0)
            dve.memset(ones[:], 1.0).then_inc(ones_set, 1)
            dve.memset(mneg[:], 0.0).then_inc(mneg_set, 1)
            for slot in range(NP):
                dve.memset(ks[BHD:P, slot, 1].bitcast(F32), 1.0).then_inc(filled_k, 1)
            dve.wait_ge(mneg_set, 1)
            maxima(0, 0, 2 * NM)
            with dve.Fori(0, B - 1) as b:
                for g in range(NP):
                    group(b, g, True)
            for g in range(NP):
                group(B - 1, g, g < NP - 1)


def selector_steps(pool, sel, blocks, made):
    for n, (row0, width, col0) in enumerate(blocks):
        view = sel[0:32, n]
        pool.affine_select(out=view, in_=view, compare_op=ALU.is_ge, fill=0.0, base=col0 + width * row0,
                           pattern=[[1, P]], channel_multiplier=-width).then_inc(made, 1)
        pool.wait_ge(made, 2 * n + 2)
        pool.affine_select(out=view, in_=view, compare_op=ALU.is_ge, fill=0.0, base=width - 1 - col0 - width * row0,
                           pattern=[[-1, P]], channel_multiplier=width).then_inc(made, 1)
        pool.wait_ge(made, 2 * n + 3)


def join_attention(nc, A, scr):
    with ExitStack() as stack:
        k = Kit(nc, stack, "jo")
        NR = NH + BH
        raw = k.sb("raw", [P, KH, 4 * H])
        wa, wb = k.sb("wa", [P, KH, 4 * H], FR), k.sb("wb", [P, KH, 4 * H], FR)
        W0, Q0, K0, V0 = 0, H, 2 * H, 3 * H
        boraw, bo = k.sb("boraw", [P, KH]), k.sb("bo", [P, KH])
        bias = k.sb("bias", [P, 2, KH])
        vbias = k.sb("vbias", [P, H])
        self32, sel = k.sb("self32", [32, 4, P]), k.sb("sel", [P, 4, P], FR)
        NSELF, NWIDE = B * NH * S // P, B * BH * S // P
        den, rden = k.sb("den", [P, NSELF + NWIDE]), k.sb("rden", [P, NSELF + NWIDE])
        recip = k.sb("recip", [P, 2, NSELF + NWIDE])
        rsplit = k.sb("rsplit", [P, 2, CH], FR)
        r16, c64 = k.sb("r16", [P, 2, KH, CH]), k.sb("c64", [P, 2, KH, CH])
        rn, cn = k.sb("rn", [P, 2, KH, CH]), k.sb("cn", [P, 2, KH, CH])
        cna, cnb = k.sb("cna", [P, 2, KH, CH], FR), k.sb("cnb", [P, 2, KH, CH], FR)
        rb = k.sb("rb", [P, 2, KH, CH])
        comb = k.sb("comb", [P, 2, KH, CH])
        coa, cob = k.sb("coa", [P, 2, KH, CH], FR), k.sb("cob", [P, 2, KH, CH], FR)
        t = k.sb("t", [P, 4, CH])
        ab = k.sb("ab", [P, 4, 2, CH])
        v64 = k.sb("v64", [P, CPB, NT, H])
        pb, pw, po = k.ps("pb", [P, 2, CH]), k.ps("pw", [P, 2, KH, CH]), k.ps("po", [P, 2, CH])
        w_in, small_in = k.sem("w_in"), k.sem("small_in")
        raw_in = [k.sem(f"raw_in{n}") for n in range(2)]
        wa_done, w_done, bo_done, sel_set, sel_made, sel_done, rs_zero = (k.sem(n) for n in (
            "wa_done", "w_done", "bo_done", "sel_set", "sel_made", "sel_done", "rs_zero"))
        den_in, recip_done, recip_split, recip_out, r_in, pb_ready, pb_done = (k.sem(n) for n in (
            "den_in", "recip_done", "recip_split", "recip_out", "r_in", "pb_ready", "pb_done"))
        cna_done, cnb_done, pw_ready, rb_done, comb_done, coa_done, cob_done = (k.sem(n) for n in (
            "cna_done", "cnb_done", "pw_ready", "rb_done", "comb_done", "coa_done", "cob_done"))
        po_ready, t_done, a_done, b_done, v_done = (k.sem(n) for n in ("po_ready", "t_done", "a_done", "b_done", "v_done"))
        comb_out = [k.sem(f"comb_out{n}") for n in range(2)]
        part_out = [k.sem(f"part_out{n}") for n in range(4)]
        v_out = [k.sem(f"v_out{n}") for n in range(2)]
        RAWS = KH + 1
        craw_v = scr["craw"].rearrange("(x r) n -> x r n", r=AH)
        dest = [(scr["mq"], 0), (scr["mq"], 1), (scr["mk"], 0), (scr["mk"], 1)]
        spread = [(hf, n) for first in (KH, 0) for hf in range(CPB) for n in range(first, first + KH)]
        NSP = len(spread)
        block = stack.enter_context(nc.Block())

        @block.sync
        def _(sp):
            sp.dma_start(den[:, 0:NSELF], craw_v[:, HD].rearrange("x (k n) -> x k n", n=NSELF)).then_inc(den_in, 16)
            sp.dma_start(den[:, NSELF:NSELF + NWIDE], scr["cden"].rearrange("x (k n) -> (x k) n", n=NWIDE)).then_inc(den_in, 16)
            mc = A["L0_attn_mc_Win"].rearrange("(k p) n -> p k n", p=P)
            sp.dma_start(raw[:, :, W0:W0 + H], A["L0_attn_ca_Wout"].rearrange("(k p) n -> p k n", p=P)).then_inc(w_in, 16)
            sp.dma_start(raw[:, :, Q0:Q0 + 3 * H], mc).then_inc(w_in, 16)
            sp.dma_start(boraw[:], column(A["L0_attn_ca_bout"]), allow_slow_non_contiguous=True).then_inc(small_in, 16)
            sp.dma_start(bias[:, 0], column(A["L0_attn_mc_bin"][0:H]), allow_slow_non_contiguous=True).then_inc(small_in, 16)
            sp.dma_start(bias[:, 1], column(A["L0_attn_mc_bin"][H:2 * H]), allow_slow_non_contiguous=True).then_inc(small_in, 16)
            sp.dma_start(vbias[:], rows(A["L0_attn_mc_bin"][2 * H:3 * H])).then_inc(small_in, 16)
            for n in range(4):
                sp.sem_inc(part_out[n], 16)
            for n in range(2):
                sp.sem_inc(v_out[n], 16)
                sp.sem_inc(comb_out[n], 16)

            def load(b, hf):
                sp.wait_ge(pb_done, NSP * b + NSP)
                cols = slice(hf * CH, (hf + 1) * CH)
                for c in range(KH):
                    sp.dma_start(r16[:, hf, c], craw_v[bass.ds(b * NH + c * NH // KH, NH // KH), 0:HD, cols]).then_inc(raw_in[hf], 16)
                sp.dma_start(c64[:, hf], scr["cout"][bass.ds(b * H, H), cols].rearrange("(c p) n -> p c n", p=P))\
                    .then_inc(raw_in[hf], 16)

            def load_reciprocals(b):
                sp.wait_ge(pb_done, NSP * b + NSP)
                for part in range(2):
                    for src, row, n in ((scr["rself"], 0, NH), (scr["rwide"], NH, BH)):
                        sp.dma_start(rsplit[32 * part + row:32 * part + row + n].rearrange("p c n -> p (c n)").bitcast(F32),
                                     src[part, bass.ds(b * n, n)]).then_inc(r_in, 16)

            def store_joined(b, hf):
                sp.wait_ge(comb_done, KH * (2 * b + hf) + KH)
                sp.dma_start(scr["comb"][bass.ds(b * H, H), hf * CH:(hf + 1) * CH].rearrange("(c p) n -> p c n", p=P),
                             comb[:, hf]).then_inc(comb_out[hf], 16)

            def store_projected(b, hf):
                i = 2 * b + hf
                for s in range(4):
                    sp.wait_ge(b_done, 4 + 4 * i + s + 1)
                    dst, j = dest[s]
                    sp.dma_start(dst[:, bass.ds(b * H + j * P, P), hf * CH:(hf + 1) * CH].rearrange("a p n -> p a n"), ab[:, s])\
                        .then_inc(part_out[s], 16)
                sp.wait_ge(v_done, NT * i + NT)
                sp.dma_start(scr["mv"][bass.ds(b * S + hf * CH, CH)].rearrange("(t p) c -> p t c", p=P), v64[:, hf])\
                    .then_inc(v_out[hf], 16)

            def batch(b, ahead):
                if ahead >= 2:
                    for hf in range(CPB):
                        load(b + 2, hf)
                    load_reciprocals(b + 2)
                for hf in range(CPB):
                    store_projected(b, hf)
                    if ahead >= 1:
                        store_joined(b + 1, hf)

            sp.wait_ge(recip_split, 2)
            for part in range(2):
                sp.dma_start(scr["rself"][part].rearrange("x (k n) -> (x k) n", n=NSELF), recip[:, part, 0:NSELF]).then_inc(recip_out, 16)
                sp.dma_start(scr["rwide"][part].rearrange("x (k n) -> (x k) n", n=NWIDE), recip[:, part, NSELF:NSELF + NWIDE])\
                    .then_inc(recip_out, 16)
            for hf in range(CPB):
                load(0, hf)
            sp.wait_ge(recip_out, 64)
            sp.wait_ge(rs_zero, 1)
            load_reciprocals(0)
            for hf in range(CPB):
                load(1, hf)
            load_reciprocals(1)
            for hf in range(CPB):
                store_joined(0, hf)
            with sp.Fori(0, B - 2) as b:
                batch(b, 2)
            for b in range(B - 2, B):
                batch(b, B - 1 - b)
            for n in range(4):
                sp.wait_ge(part_out[n], 16 + 16 * NCH)
            for n in range(2):
                sp.wait_ge(v_out[n], 16 + 16 * B)
                sp.wait_ge(comb_out[n], 16 + 16 * B)

        @block.gpsimd
        def _(pool):
            pool.memset(self32[:], 1.0).then_inc(sel_made, 1)
            pool.wait_ge(sel_made, 1)
            selector_steps(pool, self32, ((0, HD, 0), (0, HD, P), (NH, BHD, 0), (NH, BHD, P)), sel_made)
            pool.sem_inc(b_done, 4)

            def join(b, hf):
                for c in range(KH):
                    pool.wait_ge(coa_done, KH * (2 * b + hf) + c + 1)
                    pool.tensor_tensor(cob[:, hf, c], comb[:, hf, c], coa[:, hf, c].bitcast(F32), ALU.subtract)\
                        .then_inc(cob_done, 1)

            def project(b, hf):
                for s in range(4):
                    pool.wait_ge(a_done, 4 * (2 * b + hf) + s + 1)
                    pool.tensor_tensor(ab[:, s, 1], t[:, s], ab[:, s, 0], ALU.subtract).then_inc(b_done, 1)

            def batch(b, more):
                for hf in range(CPB):
                    project(b, hf)
                    if more:
                        join(b + 1, hf)

            for hf in range(CPB):
                join(0, hf)
            with pool.Fori(0, B - 1) as b:
                batch(b, True)
            batch(B - 1, False)

        @block.tensor
        def _(pe):
            pe.wait_ge(w_done, 1)
            pe.wait_ge(sel_done, 2)

            def spread_sums(b):
                for m, (hf, n) in enumerate(spread):
                    pe.wait_ge(r_in, 64 * b + 64)
                    pe.wait_ge(pb_done, NSP + NSP * b + m - 1)
                    pe.matmul(pb[:, m % 2], sel[:, n], rsplit[:, hf], start=True, stop=True).then_inc(pb_ready, 1)

            def join(b, hf):
                pe.wait_ge(cnb_done, KH * (2 * b + hf) + KH)
                for c in range(KH):
                    w = slice(W0 + c * P, W0 + (c + 1) * P)
                    mm3(pe, pw[:, hf, c], halves(wa, w), halves(wb, w), [cna[:, hf, x] for x in range(KH)],
                        [cnb[:, hf, x] for x in range(KH)]).then_inc(pw_ready, 1)

            def project(b, hf):
                i = 2 * b + hf
                pe.wait_ge(cob_done, KH * i + KH)
                xa, xb = [coa[:, hf, c] for c in range(KH)], [cob[:, hf, c] for c in range(KH)]
                for n in range(4 + NT):
                    if 2 <= n < 6:
                        pe.wait_ge(t_done, 4 * i + n - 1)
                    elif n >= 6:
                        pe.wait_ge(v_done, NT * i + n - 5)
                    if n < 4:
                        w = slice(Q0 + n * P, Q0 + (n + 1) * P)
                        mm3(pe, po[:, n % 2], halves(wa, w), halves(wb, w), xa, xb).then_inc(po_ready, 1)
                    else:
                        tok = slice((n - 4) * P, (n - 3) * P)
                        mm3(pe, po[:, n % 2, 0:H], [x[:, tok] for x in xa], [x[:, tok] for x in xb],
                            halves(wa, slice(V0, V0 + H)), halves(wb, slice(V0, V0 + H))).then_inc(po_ready, 1)

            def batch(b, more):
                if more:
                    spread_sums(b + 1)
                for hf in range(CPB):
                    project(b, hf)
                    if more:
                        join(b + 1, hf)
                    pe.wait_ge(v_done, NT * (2 * b + hf) + NT)

            spread_sums(0)
            for hf in range(CPB):
                join(0, hf)
            with pe.Fori(0, B - 1) as b:
                batch(b, True)
            batch(B - 1, False)

        @block.scalar
        def _(act):
            act.wait_ge(small_in, 64)
            act.wait_ge(bo_done, 1)

            def spread_sums(b):
                for m, (hf, n) in enumerate(spread):
                    act.wait_ge(pb_done, NSP + NSP * b + m + 1)
                    if n >= KH:
                        act.activation(cna[:, hf, n - KH], cn[:, hf, n - KH], ACT.Copy).then_inc(cna_done, 1)
                    else:
                        act.activation(rb[:, hf, n], rn[:, hf, n], ACT.Identity, bias=bo[:, n:n + 1]).then_inc(rb_done, 1)

            def join(b, hf):
                for c in range(KH):
                    act.wait_ge(comb_done, KH * (2 * b + hf) + c + 1)
                    act.activation(coa[:, hf, c], comb[:, hf, c], ACT.Copy).then_inc(coa_done, 1)

            def project(b, hf):
                i = 2 * b + hf
                for s in range(4):
                    act.wait_ge(po_ready, (4 + NT) * i + s + 1)
                    act.wait_ge(b_done, 4 * i + s + 1)
                    act.activation(t[:, s], po[:, s % 2], ACT.Identity, bias=bias[:, s // 2, s % 2:s % 2 + 1])\
                        .then_inc(t_done, 1)

            def batch(b, more):
                if more:
                    spread_sums(b + 1)
                for hf in range(CPB):
                    project(b, hf)
                    if more:
                        join(b + 1, hf)

            spread_sums(0)
            for hf in range(CPB):
                join(0, hf)
            with act.Fori(0, B - 1) as b:
                batch(b, True)
            batch(B - 1, False)

        @block.vector
        def _(dve):
            dve.sem_inc(pb_done, NSP)
            dve.memset(rsplit[:].bitcast(F32), 0.0).then_inc(rs_zero, 1)
            dve.memset(sel[:].bitcast(F32), 0.0).then_inc(sel_set, 1)
            dve.wait_ge(den_in, 32)
            dve.reciprocal(rden[:], den[:]).then_inc(recip_done, 1)
            dve.wait_ge(recip_done, 1)
            dve.tensor_copy(recip[:, 0].bitcast(FR), rden[:]).then_inc(recip_split, 1)
            dve.wait_ge(recip_split, 1)
            dve.tensor_tensor(recip[:, 1], rden[:], recip[:, 0], ALU.subtract).then_inc(recip_split, 1)
            dve.wait_ge(w_in, 32)
            dve.tensor_copy(wa[:], raw[:]).then_inc(wa_done, 1)
            dve.wait_ge(wa_done, 1)
            dve.tensor_tensor(wb[:], raw[:], wa[:].bitcast(F32), ALU.subtract).then_inc(w_done, 1)
            dve.wait_ge(small_in, 64)
            dve.tensor_scalar(bo[:], boraw[:], CAUSAL_W, None, ALU.mult).then_inc(bo_done, 1)
            dve.wait_ge(sel_made, 9)
            dve.wait_ge(sel_set, 1)
            dve.tensor_copy(sel[0:32], self32[:]).then_inc(sel_done, 1)
            dve.tensor_copy(sel[32:64], self32[:]).then_inc(sel_done, 1)
            dve.wait_ge(rs_zero, 1)

            def spread_sums(b):
                for hf in range(CPB):
                    dve.wait_ge(raw_in[hf], 16 * RAWS * (b + 1))
                for m, (hf, n) in enumerate(spread):
                    if m == NSP // 2:
                        for x in range(2 * KH):
                            dve.wait_ge(cna_done, 2 * KH * b + x + 1)
                            at = (slice(None), x // KH, x % KH)
                            dve.tensor_tensor(cnb[at], cn[at], cna[at].bitcast(F32), ALU.subtract).then_inc(cnb_done, 1)
                    dve.wait_ge(pb_ready, NSP * b + m + 1)
                    if n >= KH:
                        dve.tensor_tensor(cn[:, hf, n - KH], c64[:, hf, n - KH], pb[:, m % 2], ALU.mult).then_inc(pb_done, 1)
                    else:
                        dve.scalar_tensor_tensor(out=rn[:, hf, n], in0=r16[:, hf, n], scalar=1.0 - CAUSAL_W,
                                                 in1=pb[:, m % 2], op0=ALU.mult, op1=ALU.mult).then_inc(pb_done, 1)

            def join(b, hf):
                i = 2 * b + hf
                dve.wait_ge(comb_out[hf], 16 * b + 16)
                for c in range(KH):
                    dve.wait_ge(rb_done, KH * i + c + 1)
                    dve.wait_ge(pw_ready, KH * i + c + 1)
                    dve.scalar_tensor_tensor(out=comb[:, hf, c], in0=pw[:, hf, c], scalar=CAUSAL_W, in1=rb[:, hf, c],
                                             op0=ALU.mult, op1=ALU.add).then_inc(comb_done, 1)

            def project(b, hf):
                i = 2 * b + hf
                for s in range(4):
                    dve.wait_ge(t_done, 4 * i + s + 1)
                    dve.wait_ge(part_out[s], 16 * i + 16)
                    dve.tensor_copy(ab[:, s, 0].bitcast(FR), t[:, s]).then_inc(a_done, 1)
                dve.wait_ge(v_out[hf], 16 * b + 16)
                for tt in range(NT):
                    dve.wait_ge(po_ready, (4 + NT) * i + 4 + tt + 1)
                    dve.tensor_tensor(v64[:, hf, tt], po[:, tt % 2, 0:H], vbias[:], ALU.add).then_inc(v_done, 1)

            def batch(b, more):
                if more:
                    spread_sums(b + 1)
                for hf in range(CPB):
                    project(b, hf)
                    if more:
                        join(b + 1, hf)

            spread_sums(0)
            for hf in range(CPB):
                join(0, hf)
            with dve.Fori(0, B - 1) as b:
                batch(b, True)
            batch(B - 1, False)


def project_and_norm(nc, A, scr, ident, cross, keep=None):
    with ExitStack() as stack:
        k = Kit(nc, stack, "pc" if cross else "ps")
        NR, width = (NH, HD) if cross else (BH, BHD)
        NW = H if cross else 3 * H
        Y0, W0, Q0 = 0, H, 2 * H
        raw = k.sb("raw", [P, KH, NW])
        wa, wb = k.sb("wa", [P, KH, NW], FR), k.sb("wb", [P, KH, NW], FR)
        small_raw, small = k.sb("small_raw", [P, 2, KH]), k.sb("small", [P, 2, KH])
        obias = k.sb("obias", [P, H])
        eps = k.sb("eps", [P, 1])
        self32, sel = k.sb("self32", [32, KH, P]), k.sb("sel", [P, KH, P], FR)
        NDEN = B * NR * S // P
        den, rden, recip = k.sb("den", [P, NDEN]), k.sb("rden", [P, NDEN]), k.sb("recip", [P, 2, NDEN])
        rsplit = k.sb("rsplit", [P, 2, CH], FR)
        c64 = k.sb("c64", [P, 2, KH, CH])
        xt = k.sb("xt", [P, 2, NT, H])
        cn = k.sb("cn", [P, 2, KH, CH])
        cna, cnb = k.sb("cna", [P, 2, KH, CH], FR), k.sb("cnb", [P, 2, KH, CH], FR)
        res = k.sb("res", [P, CPB * NT, H])
        stats, mv, std, rstd = (
            k.sb("stats", [P, CPB * NT, 6]), k.sb("mv", [P, CPB * NT, 2]), k.sb("std", [P, CPB * NT]), k.sb("rstd", [P, CPB * NT]))
        x1 = k.sb("x1", [P, 2, NT, H])
        if not cross:
            comb = k.sb("comb", [P, 2, KH, CH])
            z = k.sb("z", [P, 2, KH, CH])
            za, zb = k.sb("za", [P, 2, KH, CH], FR), k.sb("zb", [P, 2, KH, CH], FR)
            xa, xb = k.sb("xa", [P, 2, KH, CH], FR), k.sb("xb", [P, 2, KH, CH], FR)
            t, ab = k.sb("t", [P, 2, KH, CH]), k.sb("ab", [P, 2, KH, 2, CH])
        pb, pw, po, px = (k.ps("pb", [P, 2, CH]), k.ps("pw", [P, KH, CH]), k.ps("po", [P, 2, CH]), k.ps("px", [P, KH, CH]))
        turned = (px, pw if cross else px)
        w_in, small_in = k.sem("w_in"), k.sem("small_in")
        raw_in = [k.sem(f"raw_in{n}") for n in range(2)]
        comb_in = [k.sem(f"comb_in{n}") for n in range(2)]
        res_in = [k.sem(f"res_in{n}") for n in range(2)]
        names = ("wa_done", "w_done", "small_done", "sel_set", "sel_made", "sel_done", "rs_zero", "eps_set",
                 "den_in", "recip_done", "recip_split", "recip_out", "r_in", "pb_ready", "pb_done", "cna_done", "cnb_done", "pw_ready", "mixed", "z_done",
                 "za_done", "zb_done", "xo_done", "y_ready", "y_done", "stats_done", "stats_seen", "rstd_done", "var_done", "std_done", "x1_done",
                 "xT_ready", "xa_done", "xb_done", "po_ready", "t_done", "a_done", "b_done")
        (wa_done, w_done, small_done, sel_set, sel_made, sel_done, rs_zero, eps_set, den_in, recip_done, recip_split, recip_out, r_in, pb_ready, pb_done,
         cna_done, cnb_done, pw_ready, mixed, z_done, za_done, zb_done, xo_done, y_ready, y_done, stats_done, stats_seen, rstd_done, var_done,
         std_done, x1_done, xT_ready, xa_done, xb_done, po_ready, t_done, a_done, b_done) = (k.sem(n) for n in names)
        x1_out = [k.sem(f"x1_out{n}") for n in range(2)]
        part_out = [[k.sem(f"part_out{n}{s}") for s in range(KH)] for n in range(2)]
        RAWS = KH if cross else 1
        wname = "L0_xattn_Wo" if cross else "L0_attn_Wo"
        residual = scr["x1"] if cross else A["x"].rearrange("b s h -> (b s) h")
        block = stack.enter_context(nc.Block())

        @block.sync
        def _(sp):
            if cross:
                craw_v = scr["craw"].rearrange("(x r) n -> x r n", r=AH)
                sp.dma_start(den[:], craw_v[:, HD].rearrange("x (k n) -> x k n", n=NDEN)).then_inc(den_in, 16)
            else:
                sp.dma_start(den[:], scr["cden"].rearrange("x (k n) -> (x k) n", n=NDEN)).then_inc(den_in, 16)
            sp.dma_start(raw[:, :, Y0:Y0 + H], A[wname].rearrange("(k p) n -> p k n", p=P)).then_inc(w_in, 16)
            sp.dma_start(obias[:], rows(A["L0_xattn_bo" if cross else "L0_attn_bo"])).then_inc(small_in, 16)
            if not cross:
                sp.dma_start(raw[:, :, W0:W0 + H], A["L0_attn_mc_Wout"].rearrange("(k p) n -> p k n", p=P)).then_inc(w_in, 16)
                sp.dma_start(raw[:, :, Q0:Q0 + H], A["L0_xattn_Wq"].rearrange("(k p) n -> p k n", p=P)).then_inc(w_in, 16)
                sp.dma_start(small_raw[:, 0], column(A["L0_attn_mc_bout"]), allow_slow_non_contiguous=True).then_inc(small_in, 16)
                sp.dma_start(small_raw[:, 1], column(A["L0_xattn_bq"]), allow_slow_non_contiguous=True).then_inc(small_in, 16)
            for n in range(2):
                sp.sem_inc(x1_out[n], 16)
                if not cross:
                    for s in range(KH):
                        sp.sem_inc(part_out[n][s], 16)

            def load(b, hf):
                sp.wait_ge(pb_done, 4 * b + 4)
                cols = slice(hf * CH, (hf + 1) * CH)
                if cross:
                    for c in range(KH):
                        sp.dma_start(c64[:, hf, c], craw_v[bass.ds(b * NH + c * NH // KH, NH // KH), 0:HD, cols])\
                            .then_inc(raw_in[hf], 16)
                else:
                    sp.dma_start(c64[:, hf], scr["cout"][bass.ds(b * H, H), cols].rearrange("(c p) n -> p c n", p=P))\
                        .then_inc(raw_in[hf], 16)

            def load_reciprocals(b):
                sp.wait_ge(pb_done, 4 * b + 4)
                for part in range(2):
                    sp.dma_start(rsplit[32 * part:32 * part + NR].rearrange("p c n -> p (c n)").bitcast(F32),
                                 scr["recip"][part, bass.ds(b * NR, NR)]).then_inc(r_in, 16)

            def load_joined(b, hf):
                sp.wait_ge(mixed, 4 * b + 2 * hf + 2)
                sp.dma_start(comb[:, hf], scr["comb"][bass.ds(b * H, H), hf * CH:(hf + 1) * CH]
                             .rearrange("(c p) n -> p c n", p=P)).then_inc(comb_in[hf], 16)

            def load_residual(b, hf):
                sp.wait_ge(x1_done, NT * (2 * b + hf) + NT)
                sp.dma_start(xt[:, hf], residual[bass.ds(b * S + hf * CH, CH)].rearrange("(t p) h -> p t h", p=P))\
                    .then_inc(res_in[hf], 16)

            def batch(b, ahead):
                if cross and ahead >= 1:
                    for hf in range(CPB):
                        load_residual(b + 1, hf)
                if ahead >= 2:
                    for hf in range(CPB):
                        load(b + 2, hf)
                    load_reciprocals(b + 2)
                for hf in range(CPB):
                    if not cross:
                        sp.wait_ge(x1_done, 8 + NT * (2 * b + hf) + NT)
                        sp.dma_start(scr["x1"][bass.ds(b * S + hf * CH, CH)].rearrange("(t p) h -> p t h", p=P), x1[:, hf])\
                            .then_inc(x1_out[hf], 16)
                        if ahead >= 1:
                            load_residual(b + 1, hf)
                if cross:
                    return
                if ahead >= 2:
                    for hf in range(CPB):
                        load_joined(b + 2, hf)
                for hf in range(CPB):
                    for s in range(KH):
                        sp.wait_ge(b_done, 4 + KH * (2 * b + hf) + s + 1)
                        sp.dma_start(scr["xq"][:, bass.ds(b * H + s * P, P), hf * CH:(hf + 1) * CH]
                                     .rearrange("a p n -> p a n"), ab[:, hf, s]).then_inc(part_out[hf][s], 16)

            sp.wait_ge(recip_split, 2)
            sp.dma_start(scr["recip"].rearrange("a x (k n) -> (x k) a n", n=NDEN), recip[:]).then_inc(recip_out, 16)
            for hf in range(CPB):
                load(0, hf)
            sp.wait_ge(recip_out, 16)
            sp.wait_ge(rs_zero, 1)
            load_reciprocals(0)
            for hf in range(CPB):
                if not cross:
                    load_joined(0, hf)
                load_residual(0, hf)
            load_reciprocals(1)
            for hf in range(CPB):
                load(1, hf)
                if not cross:
                    load_joined(1, hf)
            with sp.Fori(0, B - 2) as b:
                batch(b, 2)
            for b in range(B - 2, B):
                batch(b, B - 1 - b)
            if not cross:
                for n in range(2):
                    sp.wait_ge(x1_out[n], 16 + 16 * B)
                    for s in range(KH):
                        sp.wait_ge(part_out[n][s], 16 + 16 * B)

        @block.gpsimd
        def _(pool):
            pool.memset(self32[:], 1.0).then_inc(sel_made, 1)
            pool.wait_ge(sel_made, 1)
            selector_steps(pool, self32, ((0, width, 0), (0, width, P)), sel_made)
            pool.sem_inc(b_done, 4)
            pool.wait_ge(small_in, 16 if cross else 48)

            def mix(b, hf):
                for c in range(KH):
                    pool.wait_ge(za_done, KH * (2 * b + hf) + c + 1)
                    pool.tensor_tensor(zb[:, hf, c], z[:, hf, c], za[:, hf, c].bitcast(F32), ALU.subtract).then_inc(zb_done, 1)

            def batch(b, more):
                for hf in range(CPB):
                    pool.wait_ge(res_in[hf], 16 * b + 16)
                    pool.tensor_tensor(xt[:, hf], xt[:, hf], obias[:].unsqueeze(1).broadcast_to([P, NT, H]), ALU.add)\
                        .then_inc(xo_done, 1)
                if cross:
                    return
                if more:
                    for hf in range(CPB):
                        mix(b + 1, hf)
                for hf in range(CPB):
                    for s in range(KH):
                        pool.wait_ge(a_done, KH * (2 * b + hf) + s + 1)
                        pool.tensor_tensor(ab[:, hf, s, 1], t[:, hf, s], ab[:, hf, s, 0], ALU.subtract).then_inc(b_done, 1)

            if not cross:
                for hf in range(CPB):
                    mix(0, hf)
            with pool.Fori(0, B - 1) as b:
                batch(b, True)
            batch(B - 1, False)

        @block.tensor
        def _(pe):
            pe.wait_ge(w_done, 1)
            pe.wait_ge(sel_done, 2)

            def spread_sums(b):
                for hf in range(CPB):
                    i = 2 * b + hf
                    pe.wait_ge(r_in, 32 * b + 32)
                    for n in range(KH):
                        pe.wait_ge(pb_done, 4 + 2 * i + n - 1)
                        pe.matmul(pb[:, n], sel[:, n], rsplit[:, hf], start=True, stop=True).then_inc(pb_ready, 1)

            def mix(b, hf):
                i = 2 * b + hf
                pe.wait_ge(cnb_done, KH * i + KH)
                pe.wait_ge(z_done, KH * i + 2)
                for c in range(KH):
                    w = slice(W0 + c * P, W0 + (c + 1) * P)
                    mm3(pe, pw[:, c], halves(wa, w), halves(wb, w), [cna[:, hf, x] for x in range(KH)],
                        [cnb[:, hf, x] for x in range(KH)]).then_inc(pw_ready, 1)

            def normalise(b, hf):
                i = 2 * b + hf
                if cross:
                    pe.wait_ge(cnb_done, KH * i + KH)
                    la, lb = [cna[:, hf, c] for c in range(KH)], [cnb[:, hf, c] for c in range(KH)]
                else:
                    pe.wait_ge(zb_done, KH * i + KH)
                    la, lb = [za[:, hf, c] for c in range(KH)], [zb[:, hf, c] for c in range(KH)]
                    pe.wait_ge(t_done, 2 + KH * 2 * b)
                for tt in range(NT):
                    pe.wait_ge(y_done, NT * i + tt + 1)
                    tok = slice(tt * P, (tt + 1) * P)
                    mm3(pe, po[:, tt % 2, 0:H], [x[:, tok] for x in la], [x[:, tok] for x in lb],
                        halves(wa, slice(Y0, Y0 + H)), halves(wb, slice(Y0, Y0 + H))).then_inc(y_ready, 1)

            def turn(b, hf):
                i = 2 * b + hf
                pe.wait_ge(y_done, 2 + NT * (2 * b + CPB))
                pe.wait_ge(xb_done, i + 1)
                pe.wait_ge(x1_done, 8 + NT * i + NT)
                for kh in range(KH):
                    for tt in range(NT):
                        last = pe.transpose(turned[hf][:, kh, tt * P:(tt + 1) * P], x1[:, hf, tt, kh * P:(kh + 1) * P], ident[:])
                last.then_inc(xT_ready, 1)

            def queries(b, hf):
                i = 2 * b + hf
                pe.wait_ge(xb_done, i + 2)
                for n in range(KH):
                    pe.wait_ge(t_done, KH * i + n + 1)
                    w = slice(Q0 + n * P, Q0 + (n + 1) * P)
                    mm3(pe, po[:, n], halves(wa, w), halves(wb, w), halves(xa[:, hf]), halves(xb[:, hf])).then_inc(po_ready, 1)

            def batch(b, more):
                if more and not cross:
                    spread_sums(b + 1)
                for hf in range(CPB):
                    normalise(b, hf)
                if more and cross:
                    spread_sums(b + 1)
                for hf in range(CPB):
                    if more and not cross:
                        mix(b + 1, hf)
                    turn(b, hf)
                if not cross:
                    for hf in range(CPB):
                        queries(b, hf)

            spread_sums(0)
            if not cross:
                for hf in range(CPB):
                    mix(0, hf)
            with pe.Fori(0, B - 1) as b:
                batch(b, True)
            batch(B - 1, False)

        @block.scalar
        def _(act):
            act.sem_inc(t_done, 2)
            act.sem_inc(mixed, 4)
            act.wait_ge(small_in, 16 if cross else 48)
            act.wait_ge(eps_set, 1)
            if not cross:
                act.wait_ge(small_done, 2)

            def spread_sums(b):
                for hf in range(CPB):
                    i = 2 * b + hf
                    for c in range(KH):
                        act.wait_ge(pb_done, 4 + 2 * i + c + 1)
                        act.activation(cna[:, hf, c], cn[:, hf, c], ACT.Copy).then_inc(cna_done, 1)

            def mix(b, hf):
                i = 2 * b + hf
                act.wait_ge(comb_in[hf], 16 * b + 16)
                for c in range(KH):
                    act.activation(z[:, hf, c], comb[:, hf, c], ACT.Identity, bias=small[:, 0, c:c + 1], scale=1.0 - META_W)\
                        .then_inc(mixed, 1)
                for c in range(KH):
                    act.wait_ge(z_done, 2 + KH * i + c + 1)
                    act.activation(za[:, hf, c], z[:, hf, c], ACT.Copy).then_inc(za_done, 1)

            def normalise(b):
                act.wait_ge(var_done, CPB * NT * b + CPB * NT)
                act.activation(std[:], mv[:, :, 1], ACT.Sqrt, bias=eps[:]).then_inc(std_done, 1)

            def turn(b, hf):
                act.wait_ge(xT_ready, 2 * b + hf + 1)
                dst = keep[0][:, :, bass.ds(b * S + hf * CH, CH)] if cross else xa[:, hf]
                act.activation(dst, turned[hf][:], ACT.Copy).then_inc(xa_done, 1)

            def queries(b, hf):
                i = 2 * b + hf
                for s in range(KH):
                    act.wait_ge(po_ready, KH * i + s + 1)
                    act.wait_ge(b_done, KH * i + s + 1)
                    act.activation(t[:, hf, s], po[:, s], ACT.Identity, bias=small[:, 1, s:s + 1], scale=HD ** -0.5)\
                        .then_inc(t_done, 1)

            def batch(b, more):
                if more and not cross:
                    spread_sums(b + 1)
                normalise(b)
                if more and cross:
                    spread_sums(b + 1)
                for hf in range(CPB):
                    if more and not cross:
                        mix(b + 1, hf)
                    turn(b, hf)
                if not cross:
                    for hf in range(CPB):
                        queries(b, hf)

            spread_sums(0)
            if not cross:
                for hf in range(CPB):
                    mix(0, hf)
            with act.Fori(0, B - 1) as b:
                batch(b, True)
            batch(B - 1, False)

        @block.vector
        def _(dve):
            dve.sem_inc(pb_done, 4)
            dve.sem_inc(y_done, 2)
            dve.sem_inc(x1_done, 8)
            dve.sem_inc(xb_done, 2 if cross else 1)
            dve.memset(rsplit[:].bitcast(F32), 0.0).then_inc(rs_zero, 1)
            dve.memset(sel[:].bitcast(F32), 0.0).then_inc(sel_set, 1)
            dve.memset(eps[:], EPS).then_inc(eps_set, 1)
            dve.wait_ge(den_in, 16)
            dve.reciprocal(rden[:], den[:]).then_inc(recip_done, 1)
            dve.wait_ge(recip_done, 1)
            dve.tensor_copy(recip[:, 0].bitcast(FR), rden[:]).then_inc(recip_split, 1)
            dve.wait_ge(recip_split, 1)
            dve.tensor_tensor(recip[:, 1], rden[:], recip[:, 0], ALU.subtract).then_inc(recip_split, 1)
            dve.wait_ge(w_in, 16 if cross else 48)
            dve.tensor_copy(wa[:], raw[:]).then_inc(wa_done, 1)
            dve.wait_ge(wa_done, 1)
            dve.tensor_tensor(wb[:], raw[:], wa[:].bitcast(F32), ALU.subtract).then_inc(w_done, 1)
            if not cross:
                dve.wait_ge(small_in, 48)
                dve.tensor_scalar(small[:, 0], small_raw[:, 0], META_W, None, ALU.mult).then_inc(small_done, 1)
                dve.tensor_scalar(small[:, 1], small_raw[:, 1], HD ** -0.5, None, ALU.mult).then_inc(small_done, 1)
            dve.wait_ge(sel_made, 5)
            dve.wait_ge(sel_set, 1)
            dve.tensor_copy(sel[0:32], self32[:]).then_inc(sel_done, 1)
            dve.tensor_copy(sel[32:64], self32[:]).then_inc(sel_done, 1)
            dve.wait_ge(rs_zero, 1)

            def spread_sums(b):
                for hf in range(CPB):
                    dve.wait_ge(raw_in[hf], 16 * RAWS * (b + 1))
                for hf in range(CPB):
                    for n in range(KH):
                        dve.wait_ge(pb_ready, 2 * (2 * b + hf) + n + 1)
                        dve.tensor_tensor(cn[:, hf, n], c64[:, hf, n], pb[:, n], ALU.mult).then_inc(pb_done, 1)
                for hf in range(CPB):
                    for c in range(KH):
                        dve.wait_ge(cna_done, KH * (2 * b + hf) + c + 1)
                        dve.tensor_tensor(cnb[:, hf, c], cn[:, hf, c], cna[:, hf, c].bitcast(F32), ALU.subtract).then_inc(cnb_done, 1)

            def mix(b, hf):
                i = 2 * b + hf
                for c in range(KH):
                    dve.wait_ge(mixed, 4 + KH * i + c + 1)
                    dve.wait_ge(pw_ready, KH * i + c + 1)
                    dve.scalar_tensor_tensor(out=z[:, hf, c], in0=pw[:, c], scalar=META_W, in1=z[:, hf, c],
                                             op0=ALU.mult, op1=ALU.add).then_inc(z_done, 1)

            def normalise(b):
                NB = CPB * NT
                for hf in range(CPB):
                    if not cross:
                        dve.wait_ge(x1_out[hf], 16 * b + 16)
                dve.wait_ge(x1_done, 8 + NB * b)
                for n in range(NB):
                    if n % NT == 0:
                        dve.wait_ge(xo_done, CPB * b + n // NT + 1)
                    dve.wait_ge(y_ready, NB * b + n + 1)
                    dve.tensor_tensor(res[:, n], po[:, n % 2, 0:H], xt[:, n // NT, n % NT], ALU.add).then_inc(y_done, 1)
                for n in range(NB):
                    dve.wait_ge(y_done, 2 + NB * b + n + 1)
                    dve.bn_stats(stats[:, n], res[:, n]).then_inc(stats_done, 1)
                dve.wait_ge(stats_done, NB * b + NB)
                dve.sem_inc(stats_seen, 1)
                for n in range(NB):
                    dve.bn_aggr(mv[:, n], stats[:, n]).then_inc(var_done, 1)
                dve.wait_ge(std_done, b + 1)
                dve.reciprocal(rstd[:], std[:]).then_inc(rstd_done, 1)
                dve.wait_ge(rstd_done, b + 1)
                for n in range(NB):
                    dve.tensor_scalar(x1[:, n // NT, n % NT], res[:, n], mv[:, n, 0:1], rstd[:, n:n + 1], ALU.subtract, ALU.mult)\
                        .then_inc(x1_done, 1)

            def turn(b, hf):
                dve.wait_ge(xa_done, 2 * b + hf + 1)
                if cross:
                    tok = bass.ds(b * S + hf * CH, CH)
                    dve.tensor_tensor(keep[1][:, :, tok], turned[hf][:], keep[0][:, :, tok].bitcast(F32), ALU.subtract).then_inc(xb_done, 1)
                    if hf == 0:
                        dve.wait_ge(x1_done, 8 + CPB * NT * b + CPB * NT)
                        dve.tensor_copy(keep[2][:, bass.ds(CPB * NT * b, CPB * NT)], x1[:].rearrange("p a t h -> p (a t) h"))
                else:
                    dve.tensor_tensor(xb[:, hf], turned[hf][:], xa[:, hf].bitcast(F32), ALU.subtract).then_inc(xb_done, 1)

            def queries(b, hf):
                i = 2 * b + hf
                for s in range(KH):
                    dve.wait_ge(t_done, 2 + KH * i + s + 1)
                    dve.wait_ge(part_out[hf][s], 16 * b + 16)
                    dve.tensor_copy(ab[:, hf, s, 0].bitcast(FR), t[:, hf, s]).then_inc(a_done, 1)

            def batch(b, more):
                if more and not cross:
                    spread_sums(b + 1)
                normalise(b)
                if more and cross:
                    spread_sums(b + 1)
                for hf in range(CPB):
                    if more and not cross:
                        mix(b + 1, hf)
                    turn(b, hf)
                if not cross:
                    for hf in range(CPB):
                        queries(b, hf)

            if not cross:
                dve.sem_inc(z_done, 2)
            spread_sums(0)
            if not cross:
                for hf in range(CPB):
                    mix(0, hf)
            with dve.Fori(0, B - 1) as b:
                batch(b, True)
            batch(B - 1, False)


def context_projections(nc, A, scr, ident, dist, distT):
    with ExitStack() as stack:
        k = Kit(nc, stack, "cx")
        NE_ = 2 * B
        HB = NE_ // 2
        raw = k.sb("raw", [P, KH, 2 * H])
        wa, wb = k.sb("wa", [P, KH, 2 * H], FR), k.sb("wb", [P, KH, 2 * H], FR)
        kbias, vbias = k.sb("kbias", [P, KH]), k.sb("vbias", [P, H])
        scaling, negated, nabs, tiny = (k.sb(n, [P, 1]) for n in ("scaling", "negated", "nabs", "tiny"))
        ctx = k.sb("ctx", [E2, NE_, H])
        xa, xb = k.sb("xa", [P, KH, NE_, EP], FR), k.sb("xb", [P, KH, NE_, EP], FR)
        t, ab = k.sb("t", [P, 4, HB, EP]), k.sb("ab", [P, 4, 2, HB, EP])
        v16 = k.sb("v16", [EP, NE_, NH, AH])
        px, po, pd = k.ps("px", [P, 2, HB, P]), k.ps("po", [P, 2, CH]), k.ps("pd", [P, 2, NT, P])
        w_in, small_in, scale_in, ctx_in = k.sem("w_in"), k.sem("small_in"), k.sem("scale_in"), k.sem("ctx_in")
        dist_in = [k.sem(f"dist_in{b}") for b in range(B)]
        names = ("zeroed", "ones_set", "wa_done", "w_done", "s_chain", "ln_done", "scaled", "px_ready", "xa_done",
                 "xb_done", "k_ready", "t_done", "a_done", "b_done", "v_ready", "v_done", "pd_ready", "pd_act", "pd_dve",
                 "stored")
        (zeroed, ones_set, wa_done, w_done, s_chain, ln_done, scaled, px_ready, xa_done, xb_done, k_ready, t_done, a_done,
         b_done, v_ready, v_done, pd_ready, pd_act, pd_dve, stored) = (k.sem(n) for n in names)
        k_units = [(j, u) for j in range(KH) for u in range(2)]
        x_units = [(kh, u) for kh in range(KH) for u in range(2)]
        d_units = [(b, e, hq) for b in range(B) for e in range(2) for hq in range(CPB)]
        block = stack.enter_context(nc.Block())

        @block.sync
        def _(sp):
            sp.dma_start(ctx[:], A["ctx_1024"].rearrange("b (c e) h -> e (b c) h", c=2)).then_inc(ctx_in, 16)
            for n, w in enumerate(("Wk", "Wv")):
                sp.dma_start(raw[:, :, n * H:(n + 1) * H], A["L0_xattn_" + w].rearrange("(k p) n -> p k n", p=P)).then_inc(w_in, 16)
            for b in range(B):
                sp.dma_start(dist[:, b], A["fside_BxSxS2_0"][b].rearrange("(t p) n -> p t n", p=P)).then_inc(dist_in[b], 16)
            sp.dma_start(scaling[:], rows(A["L0_xattn_distance_scaling"])).then_inc(scale_in, 16)
            sp.dma_start(kbias[:], column(A["L0_xattn_bk"]), allow_slow_non_contiguous=True).then_inc(small_in, 16)
            sp.dma_start(vbias[:], rows(A["L0_xattn_bv"])).then_inc(small_in, 16)
            for s, (j, u) in enumerate(k_units):
                sp.wait_ge(b_done, s + 1)
                for part in range(2):
                    for n in range(2):
                        row = (2 * u + n) * H + j * P
                        sp.dma_start(scr["xk"][part, row:row + P], ab[:, s, part, 2 * n:2 * n + 2].rearrange("p e n -> p (e n)"))\
                            .then_inc(stored, 16)
            for n in range(NE_):
                sp.wait_ge(v_done, n + 1)
                sp.dma_start(scr["xv"].rearrange("(b g e p) c -> b e p g c", b=B, g=NG, e=2)[n // 2, n % 2],
                             v16[:, n].rearrange("p (g h) c -> p g (h c)", g=NG)).then_inc(stored, 16)
            sp.wait_ge(stored, 16 * (4 * len(k_units) + NE_))

        @block.gpsimd
        def _(pool):
            pool.memset(xa[:].bitcast(F32), 0.0).then_inc(zeroed, 1)
            pool.memset(xb[:].bitcast(F32), 0.0).then_inc(zeroed, 1)
            pool.memset(t[:], 0.0).then_inc(zeroed, 1)
            pool.memset(v16[:], 0.0).then_inc(zeroed, 1)
            pool.memset(distT[:], 0.0).then_inc(zeroed, 1)
            pool.wait_ge(zeroed, 5)
            pool.memset(v16[0:E2, :, :, HD:HD + 1], 1.0).then_inc(ones_set, 1)
            for s in range(len(k_units)):
                pool.wait_ge(a_done, s + 1)
                pool.tensor_tensor(ab[:, s, 1], t[:, s], ab[:, s, 0], ALU.subtract).then_inc(b_done, 1)

        @block.tensor
        def _(pe):
            pe.wait_ge(ctx_in, 16)
            for n, (kh, u) in enumerate(x_units):
                if n >= 2:
                    pe.wait_ge(xb_done, n - 1)
                for e in range(HB):
                    last = pe.transpose(px[:, n % 2, e, 0:E2], ctx[:, HB * u + e, kh * P:(kh + 1) * P], ident[0:E2, 0:E2])
                last.then_inc(px_ready, 1)
            pe.wait_ge(xb_done, len(x_units))
            pe.wait_ge(w_done, 1)
            for n, (j, u) in enumerate(k_units):
                if n >= 2:
                    pe.wait_ge(t_done, n - 1)
                w, blocks = slice(j * P, (j + 1) * P), slice(HB * u, HB * u + HB)
                mm3(pe, po[:, n % 2, 0:HB * EP].rearrange("p (e n) -> p e n", n=EP), halves(wa, w), halves(wb, w),
                    halves(xa, blocks), halves(xb, blocks)).then_inc(k_ready, 1)
            for n in range(NE_):
                if n < 2:
                    pe.wait_ge(t_done, len(k_units) - 1 + n)
                else:
                    pe.wait_ge(v_done, n - 1)
                w = slice(H, 2 * H)
                mm3(pe, po[0:EP, n % 2, 0:H], halves(xa, n), halves(xb, n), halves(wa, w), halves(wb, w)).then_inc(v_ready, 1)
            for n, (b, e, hq) in enumerate(d_units):
                pe.wait_ge(scaled, b + 1)
                if n >= 2:
                    pe.wait_ge((pd_act, pd_dve)[n % 2], n // 2)
                for i in range(NT):
                    last = pe.transpose(pd[0:E2, n % 2, i], dist[:, b, hq * NT + i, e * E2:(e + 1) * E2], ident[:])
                last.then_inc(pd_ready, 1)

        @block.scalar
        def _(act):
            act.wait_ge(zeroed, 5)
            for n, (kh, u) in enumerate(x_units):
                act.wait_ge(px_ready, n + 1)
                act.activation(xa[:, kh, HB * u:HB * u + HB, 0:E2], px[:, n % 2, :, 0:E2], ACT.Copy).then_inc(xa_done, 1)
            act.wait_ge(s_chain, 1)
            for b in range(B):
                act.wait_ge(dist_in[b], 16)
                act.activation(dist[:, b], dist[:, b], ACT.Ln, bias=tiny[:]).then_inc(ln_done, 1)
            act.wait_ge(small_in, 32)
            for n, (j, u) in enumerate(k_units):
                act.wait_ge(k_ready, n + 1)
                act.activation(t[:, n, :, 0:E2], po[:, n % 2, 0:HB * EP].rearrange("p (e n) -> p e n", n=EP)[:, :, 0:E2],
                               ACT.Identity, bias=kbias[:, j:j + 1]).then_inc(t_done, 1)
            for n, (b, e, hq) in enumerate(d_units):
                if n % 2 == 0:
                    act.wait_ge(pd_ready, n + 1)
                    act.activation(distT[0:E2, b, e, hq * CH:(hq + 1) * CH], pd[0:E2, n % 2].rearrange("p i n -> p (i n)"),
                                   ACT.Copy).then_inc(pd_act, 1)

        @block.vector
        def _(dve):
            dve.memset(tiny[:], 1e-9).then_inc(s_chain, 1)
            dve.wait_ge(w_in, 32)
            dve.tensor_copy(wa[:], raw[:]).then_inc(wa_done, 1)
            dve.wait_ge(wa_done, 1)
            dve.tensor_tensor(wb[:], raw[:], wa[:].bitcast(F32), ALU.subtract).then_inc(w_done, 1)
            for n, (kh, u) in enumerate(x_units):
                dve.wait_ge(xa_done, n + 1)
                blocks = slice(HB * u, HB * u + HB)
                dve.tensor_tensor(xb[:, kh, blocks, 0:E2], px[:, n % 2, :, 0:E2], xa[:, kh, blocks, 0:E2].bitcast(F32), ALU.subtract)\
                    .then_inc(xb_done, 1)
            dve.wait_ge(scale_in, 16)
            dve.tensor_scalar(negated[:], scaling[:], -1.0, None, ALU.mult).then_inc(s_chain, 1)
            dve.wait_ge(s_chain, 2)
            dve.tensor_tensor(nabs[:], scaling[:], negated[:], ALU.min).then_inc(s_chain, 1)
            dve.wait_ge(s_chain, 3)
            for b in range(B):
                dve.wait_ge(ln_done, b + 1)
                dve.tensor_scalar(dist[:, b], dist[:, b], nabs[:, 0:1], None, ALU.mult).then_inc(scaled, 1)
            for n in range(len(k_units)):
                dve.wait_ge(t_done, n + 1)
                dve.tensor_copy(ab[:, n, 0].bitcast(FR), t[:, n]).then_inc(a_done, 1)
            dve.wait_ge(ones_set, 1)
            dve.wait_ge(small_in, 32)
            for n in range(NE_):
                dve.wait_ge(v_ready, n + 1)
                dve.tensor_tensor(v16[0:E2, n, :, 0:HD], po[0:E2, n % 2, 0:H].rearrange("p (h d) -> p h d", h=NH),
                                  vbias[0:E2].rearrange("p (h d) -> p h d", h=NH), ALU.add).then_inc(v_done, 1)
            for n, (b, e, hq) in enumerate(d_units):
                if n % 2:
                    dve.wait_ge(pd_ready, n + 1)
                    dve.tensor_copy(distT[0:E2, b, e, hq * CH:(hq + 1) * CH], pd[0:E2, n % 2].rearrange("p i n -> p (i n)"))\
                        .then_inc(pd_dve, 1)


def attend_cross(nc, scr, dist, distT):
    with ExitStack() as stack:
        k = Kit(nc, stack, "ac")
        ONE, LAST = 4 * HD, 6 * HD
        MROW = LAST - 1
        NSTEP = CPB * 2
        qs, ks = k.sb("qs", [LAST, NG, GH, S], FR), k.sb("ks", [LAST, NG, GH, 2, EP], FR)
        vs = k.sb("vs", [EP, NG, 2, GH * AH])
        probs = k.sb("probs", [EP, 2, GH, CH])
        ev = k.sb("ev", [P, CPB, CH])
        bias = k.sb("bias", [P, S // P, S2])
        m1 = k.sb("m1", [P, CPB, GH * NT])
        mneg, mturn = k.sb("mneg", [P, 32]), k.sb("mturn", [P, 32])
        mrows = k.sb("mrows", [P, CPB, 32], FR)
        pst = k.ps("pst", [P, 2, 2, CH])
        psm = k.ps("psm", [P, 2, 2, 2, P])
        pacc = k.ps("pacc", [P, CPB, CH])
        filled_q, filled_k, zeroed, mneg_set, bias_done, mx_seen = (
            k.sem(n) for n in ("filled_q", "filled_k", "zeroed", "mneg_set", "bias_done", "mx_seen"))
        loaded = [k.sem(f"loaded{n}") for n in range(NG)]
        mrow_in = [[k.sem(f"mrow_in{n}{h}") for h in range(CPB)] for n in range(NG)]
        m_out = [k.sem(f"m_out{h}") for h in range(CPB)]
        ev_out = [k.sem(f"ev_out{h}") for h in range(CPB)]
        mx_ready, mx_done, m_chain, m_ready, row_moved = (
            k.sem(n) for n in ("mx_ready", "mx_done", "m_chain", "m_ready", "row_moved"))
        st_ready, add_done, exp_done, pv_done, acc_out = (
            k.sem(n) for n in ("st_ready", "add_done", "exp_done", "pv_done", "acc_out"))
        LOADS = 9
        PV0 = NSTEP * (NG - 1) + 2
        mx_list = [(hq, jp, i) for hq in range(CPB) for jp in range(GH // 2) for i in range(NT)]
        NM = len(mx_list)
        PER = NM // NSTEP
        block = stack.enter_context(nc.Block())

        @block.sync
        def _(sp):
            def load(G, slot):
                sp.wait_ge(pv_done, PV0 + NSTEP * (G - NG + 1))
                for r, (qp, kp) in enumerate(((0, 0), (0, 1), (1, 0), (1, 1))):
                    sp.dma_start(qs[r * HD:(r + 1) * HD, slot].bitcast(F32),
                                 scr["xq"][qp, bass.ds(G * GH * HD, GH * HD)].rearrange("(j d) n -> d j n", j=GH))\
                        .then_inc(loaded[slot], 16)
                    sp.dma_start(ks[r * HD:(r + 1) * HD, slot].rearrange("p j e n -> p j (e n)").bitcast(F32),
                                 scr["xk"][kp, bass.ds(G * GH * HD, GH * HD)].rearrange("(j d) n -> d j n", j=GH))\
                        .then_inc(loaded[slot], 16)
                sp.dma_start(vs[:, slot], scr["xv"][bass.ds(G * 2 * EP, 2 * EP)].rearrange("(e p) n -> p e n", p=EP))\
                    .then_inc(loaded[slot], 16)

            def max_row(G, slot, uses, hq):
                sp.wait_ge(m_ready, CPB * G + hq + 1)
                turned = scr["m"][hq].rearrange("(c b r) -> b c r", b=4, r=32)
                for q in range(4):
                    sp.dma_start(turned[q], mrows[32 * q:32 * q + GH * NT, hq].bitcast(F32)).then_inc(m_out[hq], 16)
                sp.wait_ge(m_out[hq], 64 * G + 64)
                sp.dma_start(qs[MROW:LAST, slot, :, hq * CH:(hq + 1) * CH].bitcast(F32),
                             scr["m"][hq:hq + 1].rearrange("o (j n) -> o j n", j=GH)).then_inc(mrow_in[slot][hq], 16)
                sp.wait_ge(mrow_in[slot][hq], 16 * uses + 16)
                sp.sem_inc(row_moved, 1)

            def store(G, qh):
                sp.wait_ge(acc_out, CPB * G + qh + 3)
                sp.dma_start(scr["craw"][bass.ds(G * P, P), qh * CH:(qh + 1) * CH], ev[:, qh]).then_inc(ev_out[qh], 16)

            def group(b, g, ahead):
                G = b * NG + g
                if ahead >= 2:
                    load(G + 2, (g + 2) % NG)
                if ahead >= 1:
                    max_row(G + 1, (g + 1) % NG, b + (g + 1) // NG, 0)
                store(G, 0)
                if ahead >= 1:
                    max_row(G + 1, (g + 1) % NG, b + (g + 1) // NG, 1)
                store(G, 1)

            for qh in range(CPB):
                sp.sem_inc(ev_out[qh], 16)
            load(0, 0)
            load(1, 1)
            for hq in range(CPB):
                max_row(0, 0, 0, hq)
            with sp.Fori(0, B - 1) as b:
                for g in range(NG):
                    group(b, g, 2)
            for g in range(NG):
                group(B - 1, g, NG - 1 - g)
            for qh in range(CPB):
                sp.wait_ge(ev_out[qh], 16 + 16 * B * NG)

        @block.gpsimd
        def _(pool):
            for slot in range(NG):
                pool.memset(qs[ONE:LAST, slot].bitcast(F32), 0.0).then_inc(filled_q, 1)

        @block.tensor
        def _(pe):
            def maxima(G, slot, uses, lo, hi):
                for n in range(lo, hi):
                    hq, jp, i = mx_list[n]
                    if n == 0:
                        pe.wait_ge(filled_q, slot + 1)
                        pe.wait_ge(loaded[slot], 16 * LOADS * uses + 16 * LOADS)
                    pe.wait_ge(mx_done, 2 * (NM * G + n + 1))
                    q0 = (hq * NT + i) * P
                    for jj in range(2):
                        j = 2 * jp + jj
                        last = pe.matmul(psm[:, n % 2, jj, :, 0:EP], qs[0:MROW, slot, j, q0:q0 + P],
                                         ks[0:MROW, slot, j], start=True, stop=True)
                    last.then_inc(mx_ready, 1)

            def values(G, slot, s):
                qh, e = divmod(s, 2)
                pe.wait_ge(exp_done, NSTEP * G + s + 1)
                if e == 0:
                    pe.wait_ge(acc_out, CPB * G + qh + 1)
                for j in range(GH):
                    last = pe.matmul(pacc[j * AH:(j + 1) * AH, qh], vs[:, slot, e, j * AH:(j + 1) * AH],
                                     probs[:, s % 2, j], start=(e == 0), stop=(e == 1))
                last.then_inc(pv_done, 1)

            def group(b, g, more):
                G = b * NG + g
                nxt = (G + 1, (g + 1) % NG, b + (g + 1) // NG)
                for s in range(NSTEP):
                    qh, e = divmod(s, 2)
                    if e == 0:
                        pe.wait_ge(mrow_in[g][qh], 16 * b + 16)
                    for hp in range(2):
                        pe.wait_ge(add_done, 2 * NSTEP * G + 2 * s + hp + 1)
                        for jj in range(2):
                            j = 2 * hp + jj
                            last = pe.matmul(pst[0:EP, hp, jj], ks[:, g, j, e], qs[:, g, j, qh * CH:(qh + 1) * CH],
                                             start=True, stop=True)
                        last.then_inc(st_ready, 1)
                        if more:
                            maxima(*nxt, PER * s + hp, PER * s + hp + 1)
                    if s > 0:
                        values(G, g, s - 1)
                    if more:
                        maxima(*nxt, PER * s + 2, PER * s + PER)
                values(G, g, NSTEP - 1)

            pe.sem_inc(pv_done, PV0)
            pe.wait_ge(filled_k, 1)
            maxima(0, 0, 0, 0, NM)
            with pe.Fori(0, B - 1) as b:
                for g in range(NG):
                    group(b, g, True)
            for g in range(NG):
                group(B - 1, g, g < NG - 1)

        @block.scalar
        def _(act):
            def copy_out(G, qh):
                act.wait_ge(pv_done, PV0 + NSTEP * G + 2 * qh + 2)
                act.wait_ge(ev_out[qh], 16 * G + 16)
                act.activation(ev[:, qh], pacc[:, qh], ACT.Copy).then_inc(acc_out, 1)

            act.sem_inc(acc_out, 2)
            with act.Fori(0, B) as b:
                for g in range(NG):
                    G = b * NG + g
                    for s in range(NSTEP):
                        act.wait_ge(add_done, 2 + 2 * (NSTEP * G + s + 1))
                        act.activation(probs[:, s % 2], probs[:, s % 2], ACT.Exp).then_inc(exp_done, 1)
                        if s == 3:
                            copy_out(G, 0)
                    copy_out(G, 1)

        @block.vector
        def _(dve):
            def take_bias(b):
                src = dist[:, b] if isinstance(b, int) else dist[:, bass.ds(b, 1)].rearrange("p o t n -> p (o t) n")
                dve.tensor_copy(bias[:], src).then_inc(bias_done, 1)

            def maxima(G, lo, hi):
                for n in range(lo, hi):
                    hq, jp, i = mx_list[n]
                    dve.wait_ge(mx_ready, NM * G + n + 1)
                    dve.sem_inc(mx_seen, 1)
                    for jj in range(2):
                        col = (2 * jp + jj) * NT + i
                        scores = psm[:, n % 2, jj, :, 0:E2]
                        added = bias[:, hq * NT + i].rearrange("p (e n) -> p e n", e=2)
                        dve.tensor_tensor_reduce(out=scores, in0=scores, in1=added, scale=1.0, scalar=LOWEST, op0=ALU.add,
                                                 op1=ALU.max, accum_out=m1[:, hq, col:col + 1]).then_inc(mx_done, 1)
                    if n % (NM // CPB) == NM // CPB - 1:
                        finish(G, hq)

            def finish(G, hq):
                dve.wait_ge(mx_done, 4 + 2 * (NM * G + (hq + 1) * NM // CPB))
                dve.tensor_scalar(mneg[:, 0:GH * NT], m1[:, hq], -1.0, None, ALU.mult).then_inc(m_chain, 1)
                dve.wait_ge(m_chain, 2 * (CPB * G + hq) + 1)
                dve.transpose(mturn[:], mneg[:]).then_inc(m_chain, 1)
                dve.wait_ge(m_chain, 2 * (CPB * G + hq) + 2)
                if not (isinstance(G, int) and G == 0):
                    dve.wait_ge(row_moved, CPB * (G - 1) + hq + 1)
                dve.tensor_copy(mrows[:, hq], mturn[:]).then_inc(m_ready, 1)

            def group(b, g, more):
                G = b * NG + g
                if more and g == NG - 1:
                    take_bias(b + 1)
                    dve.wait_ge(bias_done, b + 2)
                for s in range(NSTEP):
                    qh, e = divmod(s, 2)
                    for hp in range(2):
                        dve.wait_ge(st_ready, 2 * NSTEP * G + 2 * s + hp + 1)
                        if hp == 0:
                            dve.wait_ge(pv_done, PV0 + NSTEP * G + s - 1)
                        cols = slice(qh * CH, (qh + 1) * CH)
                        added = distT[:, b, e, cols] if isinstance(b, int) else \
                            distT[:, bass.ds(b, 1), e, cols].rearrange("p o n -> p (o n)")
                        dve.tensor_tensor(probs[:, s % 2, 2 * hp:2 * hp + 2], pst[0:EP, hp],
                                          added.unsqueeze(1).broadcast_to([EP, 2, CH]), ALU.add).then_inc(add_done, 1)
                        if more:
                            maxima(G + 1, PER * s + hp * PER // 2, PER * s + (hp + 1) * PER // 2)

            dve.sem_inc(mx_done, 4)
            dve.sem_inc(add_done, 2)
            dve.memset(ks[ONE:LAST].bitcast(F32), 0.0).then_inc(zeroed, 1)
            dve.wait_ge(zeroed, 1)
            dve.memset(mneg[:], 0.0).then_inc(mneg_set, 1)
            dve.wait_ge(mneg_set, 1)
            dve.memset(ks[ONE:LAST, :, :, :, 0:E2].bitcast(F32), 1.0).then_inc(filled_k, 1)
            take_bias(0)
            dve.wait_ge(bias_done, 1)
            maxima(0, 0, NM)
            with dve.Fori(0, B - 1) as b:
                for g in range(NG):
                    group(b, g, True)
            for g in range(NG):
                group(B - 1, g, g < NG - 1)


G0, U0, D0 = 0, KH * D, 2 * KH * D
EW = D0 + FB * H


def load_weights(sp, raw, gate, up, down, loaded):
    for src, at, n in ((gate, G0, KH * D), (up, U0, KH * D), (down, D0, FB * H)):
        sp.dma_start(raw[:, at:at + n].rearrange("p (k n) -> p k n", n=src.shape[-1]),
                     src.rearrange("(k p) n -> p k n", p=P)).then_inc(loaded, 16)


def load_expert(sp, A, raw, e, loaded):
    gate, up, down = (A["L0_ffn_w_" + n].rearrange("e k n -> (e k) n") for n in ("gate", "up", "down"))
    load_weights(sp, raw, gate[bass.ds(e * H, H)], up[bass.ds(e * H, H)], down[bass.ds(e * D, D)], loaded)


def route(nc, A, ident, xa, xb, weight, expert_weights):
    with ExitStack() as stack:
        k = Kit(nc, stack, "ro")
        TT = TOK // P
        raw, wa, wb = k.sb("raw", [P, KH, NE]), k.sb("wa", [P, KH, NE], FR), k.sb("wb", [P, KH, NE], FR)
        lt = k.sb("lt", [NE, 2, CH])
        grid = [P, TT, NE]
        logits, prob, masked, equal, ranked, first, second = (
            k.sb(n, grid) for n in ("logits", "prob", "masked", "equal", "ranked", "first", "second"))
        rank = k.sb("rank", [P, NE])
        top, total, high1, high2, pick, share1, share2 = (
            k.sb(n, [P, TT]) for n in ("top", "total", "high1", "high2", "pick", "share1", "share2"))
        pl, pt = k.ps("pl", [NE, 2, CH]), k.ps("pt", [P, 2, CH // NE, NE])
        w_in, wa_done, w_done, rank_set, l_ready, l_done, t_ready, t_done, chain, exp_done = (k.sem(n) for n in (
            "w_in", "wa_done", "w_done", "rank_set", "l_ready", "l_done", "t_ready", "t_done", "chain", "exp_done"))
        expert_raw, expert_a, expert_b = expert_weights
        experts_in = [k.sem(f"experts_in{e}") for e in range(2)]
        expert_a_done, expert_b_done = k.sem("expert_a_done"), k.sem("expert_b_done")
        block = stack.enter_context(nc.Block())

        @block.sync
        def _(sp):
            sp.dma_start(raw[:], A["L0_ffn_gate_w"].rearrange("(k p) n -> p k n", p=P)).then_inc(w_in, 16)
            for e in range(2):
                load_expert(sp, A, expert_raw[:, e], e, experts_in[e])
            for e in range(2):
                sp.wait_ge(experts_in[e], 48)

        @block.gpsimd
        def _(pool):
            for e in range(NE):
                pool.memset(rank[:, e:e + 1], float(NE - e)).then_inc(rank_set, 1)
            pool.memset(weight[:, NE], 1.0).then_inc(rank_set, 1)
            pool.wait_ge(rank_set, NE + 1)
            pool.wait_ge(expert_a_done, 1)
            pool.tensor_tensor(expert_b[:, 0], expert_raw[:, 0], expert_a[:, 0].bitcast(F32), ALU.subtract)\
                .then_inc(expert_b_done, 1)
            pool.wait_ge(expert_b_done, 1)

        @block.tensor
        def _(pe):
            def turn(c):
                pe.wait_ge(l_done, c + 1)
                if c >= 2:
                    pe.wait_ge(t_done, c - 1)
                for tt in range(NT):
                    last = pe.transpose(pt[:, c % 2, tt], lt[:, c % 2, tt * P:(tt + 1) * P], ident[0:NE, 0:NE])
                last.then_inc(t_ready, 1)

            pe.wait_ge(w_done, 1)
            for c in range(NCH):
                if c >= 2:
                    pe.wait_ge(l_done, c - 1)
                tok = slice(c * CH, (c + 1) * CH)
                mm3(pe, pl[:, c % 2], halves(wa), halves(wb), halves(xa, tok), halves(xb, tok)).then_inc(l_ready, 1)
                if c >= 1:
                    turn(c - 1)
            turn(NCH - 1)

        @block.scalar
        def _(act):
            for c in range(NCH):
                act.wait_ge(l_ready, c + 1)
                if c >= 2:
                    act.wait_ge(t_ready, c - 1)
                act.activation(lt[:, c % 2], pl[:, c % 2], ACT.Copy).then_inc(l_done, 1)
            act.wait_ge(chain, 2)
            act.activation(prob[:], prob[:], ACT.Exp).then_inc(exp_done, 1)
            act.wait_ge(experts_in[0], 48)
            act.activation(expert_a[:, 0], expert_raw[:, 0], ACT.Copy).then_inc(expert_a_done, 1)

        @block.vector
        def _(dve):
            count = [0]

            def link(instruction):
                instruction.then_inc(chain, 1)
                count[0] += 1
                dve.wait_ge(chain, count[0])

            def over(v):
                return v[:].unsqueeze(2).broadcast_to(grid)

            def pick_first(src, high, onehot):
                link(dve.tensor_reduce(high[:], src[:], AX.X, ALU.max))
                link(dve.tensor_tensor(equal[:], src[:], over(high), ALU.is_equal))
                link(dve.tensor_tensor(ranked[:], equal[:], rank[:].unsqueeze(1).broadcast_to(grid), ALU.mult))
                link(dve.tensor_reduce(pick[:], ranked[:], AX.X, ALU.max))
                link(dve.tensor_tensor(onehot[:], ranked[:], over(pick), ALU.is_equal))

            dve.wait_ge(w_in, 16)
            dve.tensor_copy(wa[:], raw[:]).then_inc(wa_done, 1)
            dve.wait_ge(wa_done, 1)
            dve.tensor_tensor(wb[:], raw[:], wa[:].bitcast(F32), ALU.subtract).then_inc(w_done, 1)
            for c in range(NCH):
                dve.wait_ge(t_ready, c + 1)
                dve.tensor_copy(logits[:, c * NT:(c + 1) * NT], pt[:, c % 2, 0:NT]).then_inc(t_done, 1)
            dve.wait_ge(t_done, NCH)
            link(dve.tensor_reduce(top[:], logits[:], AX.X, ALU.max))
            link(dve.tensor_tensor(prob[:], logits[:], over(top), ALU.subtract))
            dve.wait_ge(exp_done, 1)
            link(dve.tensor_reduce(total[:], prob[:], AX.X, ALU.add))
            link(dve.reciprocal(total[:], total[:]))
            link(dve.tensor_tensor(prob[:], prob[:], over(total), ALU.mult))
            dve.wait_ge(rank_set, NE + 1)
            pick_first(prob, high1, first)
            link(dve.scalar_tensor_tensor(out=masked[:], in0=first[:], scalar=-2.0, in1=prob[:], op0=ALU.mult, op1=ALU.add))
            pick_first(masked, high2, second)
            link(dve.tensor_tensor(total[:], high1[:], high2[:], ALU.add))
            link(dve.tensor_scalar(total[:], total[:], 1e-20, None, ALU.add))
            link(dve.reciprocal(total[:], total[:]))
            link(dve.tensor_tensor(share1[:], high1[:], total[:], ALU.mult))
            link(dve.tensor_tensor(share2[:], high2[:], total[:], ALU.mult))
            link(dve.tensor_tensor(first[:], first[:], over(share1), ALU.mult))
            link(dve.tensor_tensor(second[:], second[:], over(share2), ALU.mult))
            link(dve.tensor_tensor(weight[:, 0:NE].rearrange("p e t -> p t e"), first[:], second[:], ALU.add))


def run_experts(nc, A, xa, xb, acc, weight, expert_weights, out):
    with ExitStack() as stack:
        k = Kit(nc, stack, "ex")
        PIECE = EW // NCH
        raw, wa, wb = expert_weights
        stats, mv = k.sb("stats", [P, NT, 6]), k.sb("mv", [P, NT, 2])
        std, rstd, eps = k.sb("std", [P, NT]), k.sb("rstd", [P, NT]), k.sb("eps", [P, 1])
        eps_set, acc_seen, stats_done, stats_seen, mv_done, std_done, rstd_done, norm_done, stored = (k.sem(n) for n in (
            "eps_set", "acc_seen", "stats_done", "stats_seen", "mv_done", "std_done", "rstd_done", "norm_done", "stored"))
        gated, hid = k.sb("gated", [P, 2, CH]), k.sb("hid", [P, 2, CH])
        ha, hb = k.sb("ha", [P, FB, CH], FR), k.sb("hb", [P, FB, CH], FR)
        pg, pu, py = k.ps("pg", [P, 2, CH]), k.ps("pu", [P, 2, CH]), k.ps("py", [P, NT, CH])
        w_in = [k.sem(f"w_in{n}") for n in range(2)]
        piece_a, piece_b, g_ready, u_ready, gated_done, hid_done, a_done, b_done, y_ready, acc_done = (k.sem(n) for n in (
            "piece_a", "piece_b", "g_ready", "u_ready", "gated_done", "hid_done", "a_done", "b_done", "y_ready", "acc_done"))
        block = stack.enter_context(nc.Block())

        def matrix(w, slot, first, n, cols):
            return w[:, slot, first + n * cols:first + (n + 1) * cols]

        @block.sync
        def _(sp):
            for n in range(2):
                sp.sem_inc(w_in[n], 48)
            with sp.Fori(0, NE // 2 - 1) as ep:
                for n in range(2):
                    sp.wait_ge(piece_b, NCH * (2 * ep + n + 1))
                    load_expert(sp, A, raw[:, n], 2 * ep + n + 2, w_in[n])
            sp.wait_ge(piece_b, NCH * (NE - 1))
            load_weights(sp, raw[:, 0], A["L0_ffn_ws_gate"], A["L0_ffn_ws_up"], A["L0_ffn_ws_down"], w_in[0])
            for c in range(NCH):
                sp.wait_ge(norm_done, NT * (c + 1))
                sp.dma_start(out[c * CH:(c + 1) * CH].rearrange("(t p) h -> p t h", p=P), acc[:, c * NT:(c + 1) * NT])\
                    .then_inc(stored, 16)
            sp.wait_ge(stored, 16 * NCH)

        def pieces(c):
            return bass.ds(c * PIECE, PIECE)

        @block.gpsimd
        def _(pool):
            def split(e, slot, c):
                pool.wait_ge(piece_a, NCH * e + c + 1)
                pool.tensor_tensor(wb[:, slot, pieces(c)], raw[:, slot, pieces(c)], wa[:, slot, pieces(c)].bitcast(F32),
                                   ALU.subtract).then_inc(piece_b, 1)

            def expert(e, n, more):
                with pool.Fori(0, NCH) as c:
                    t = NCH * e + c
                    for f in range(FB):
                        pool.wait_ge(a_done, FB * t + f + 1)
                        pool.tensor_tensor(hb[:, f], hid[:, f % 2], ha[:, f].bitcast(F32), ALU.subtract).then_inc(b_done, 1)
                    if more:
                        split(e + 1, 1 - n, c)

            pool.sem_inc(b_done, 2)
            pool.sem_inc(piece_b, NCH)
            with pool.Fori(0, NE // 2) as ep:
                for n in range(2):
                    expert(2 * ep + n, n, True)
            expert(NE, 0, False)

        @block.tensor
        def _(pe):
            def expert(e, slot):
                with pe.Fori(0, NCH) as c:
                    pe.wait_ge(piece_b, NCH * e + NCH)
                    t = NCH * e + c
                    tok = bass.ds(c * CH, CH)
                    for f in range(FB):
                        for out, first, free, ready in ((pg, G0, gated_done, g_ready), (pu, U0, hid_done, u_ready)):
                            pe.wait_ge(free, FB * t + f + 1)
                            la, lb = ([matrix(w, slot, first, n, D)[:, f * P:(f + 1) * P] for n in range(KH)] for w in (wa, wb))
                            mm3(pe, out[:, f % 2], la, lb, halves(xa, tok), halves(xb, tok)).then_inc(ready, 1)
                    pe.wait_ge(acc_done, NT * t + NT)
                    for f in range(FB):
                        pe.wait_ge(b_done, 2 + FB * t + f + 1)
                        for tt in range(NT):
                            cols = slice(tt * P, (tt + 1) * P)
                            da, db = matrix(wa, slot, D0, f, H), matrix(wb, slot, D0, f, H)
                            for n, (x, y) in enumerate(((ha, da), (ha, db), (hb, da))):
                                last = pe.matmul(py[:, tt, 0:H], x[:, f, cols], y, start=(f == 0 and n == 0),
                                                 stop=(f == FB - 1 and n == 2))
                            if f == FB - 1:
                                last.then_inc(y_ready, 1)

            with pe.Fori(0, NE // 2) as ep:
                for n in range(2):
                    expert(2 * ep + n, n)
            expert(NE, 0)

        @block.scalar
        def _(act):
            def gates(t):
                for f in range(FB):
                    act.wait_ge(g_ready, FB * t + f + 1)
                    act.wait_ge(hid_done, FB * t + f + 1)
                    act.activation(gated[:, f % 2], pg[:, f % 2], ACT.Silu).then_inc(gated_done, 1)

            def deviations(c):
                act.wait_ge(mv_done, NT * c + NT)
                act.activation(std[:], mv[:, :, 1], ACT.Sqrt, bias=eps[:]).then_inc(std_done, 1)

            act.sem_inc(gated_done, 2)
            act.wait_ge(eps_set, 1)
            with act.Fori(0, NE) as e:
                with act.Fori(0, NCH) as c:
                    gates(NCH * e + c)
            gates(NCH * NE)
            with act.Fori(0, NCH - 1) as c:
                gates(NCH * NE + c + 1)
                deviations(c)
            deviations(NCH - 1)

        @block.vector
        def _(dve):
            def split(e, slot, c):
                dve.tensor_copy(wa[:, slot, pieces(c)], raw[:, slot, pieces(c)]).then_inc(piece_a, 1)

            def hidden(t):
                for f in range(FB):
                    dve.wait_ge(gated_done, 2 + FB * t + f + 1)
                    dve.wait_ge(u_ready, FB * t + f + 1)
                    dve.wait_ge(b_done, FB * t + f + 1)
                    dve.tensor_tensor(hid[:, f % 2], gated[:, f % 2], pu[:, f % 2], ALU.mult).then_inc(hid_done, 1)
                    dve.wait_ge(hid_done, 2 + FB * t + f + 1)
                    dve.tensor_copy(ha[:, f], hid[:, f % 2]).then_inc(a_done, 1)

            def accumulate(e, c):
                t = NCH * e + c
                for tt in range(NT):
                    dve.wait_ge(y_ready, NT * t + tt + 1)
                    tile = acc[:, bass.ds(NT * c + tt, 1)].rearrange("p o n -> p (o n)")
                    share = weight[:].rearrange("p e t -> p (e t)")[:, bass.ds(TOK // P * e + NT * c + tt, 1)]
                    dve.scalar_tensor_tensor(out=tile, in0=py[:, tt, 0:H], scalar=share, in1=tile, op0=ALU.mult, op1=ALU.add)\
                        .then_inc(acc_done, 1)

            def expert(e, n, uses):
                with dve.Fori(0, NCH) as c:
                    hidden(NCH * e + c)
                    dve.wait_ge(w_in[1 - n], 48 * uses)
                    split(e + 1, 1 - n, c)
                    accumulate(e, c)

            def statistics(c):
                dve.wait_ge(acc_done, 4 + NT * (NCH * NE + c + 1))
                dve.sem_inc(acc_seen, 1)
                for tt in range(NT):
                    dve.bn_stats(stats[:, tt], acc[:, bass.ds(NT * c + tt, 1)].rearrange("p o n -> p (o n)")).then_inc(stats_done, 1)
                dve.wait_ge(stats_done, NT * c + NT)
                dve.sem_inc(stats_seen, 1)
                for tt in range(NT):
                    dve.bn_aggr(mv[:, tt], stats[:, tt]).then_inc(mv_done, 1)

            def normalise(c):
                dve.wait_ge(std_done, c + 1)
                dve.reciprocal(rstd[:], std[:]).then_inc(rstd_done, 1)
                dve.wait_ge(rstd_done, c + 1)
                for tt in range(NT):
                    tile = acc[:, bass.ds(NT * c + tt, 1)].rearrange("p o n -> p (o n)")
                    dve.tensor_scalar(tile, tile, mv[:, tt, 0:1], rstd[:, tt:tt + 1], ALU.subtract, ALU.mult).then_inc(norm_done, 1)

            dve.sem_inc(hid_done, 2)
            dve.sem_inc(acc_done, 4)
            dve.sem_inc(piece_a, NCH)
            dve.memset(eps[:], EPS).then_inc(eps_set, 1)
            with dve.Fori(0, NE // 2) as ep:
                for n in range(2):
                    expert(2 * ep + n, n, ep + 1 + n)
            hidden(NCH * NE)
            accumulate(NE, 0)
            statistics(0)
            with dve.Fori(0, NCH - 1) as c:
                hidden(NCH * NE + c + 1)
                normalise(c)
                accumulate(NE, c + 1)
                statistics(c + 1)
            normalise(NCH - 1)


def clear_semaphores(nc):
    nc.all_engine_barrier(sems_to_clear=range(min(nc.free_semaphores), max(nc.free_semaphores) + 1))


def decoder_layer(nc, A, out):
    scr = {name: nc.dram_tensor("scr_" + name, shape, F32, kind="Internal").ap() for name, shape in dict(
        q=[2, B * H, S], k=[2, B * H, S], v=[B * NG * S, GH * AH], m=[CPB, GH * CH], craw=[B * NH * AH, S],
        cq=[2, B * H, S], ck=[2, B * H, S], cv=[TOK, H], cm=[CPB, 2 * CH], cout=[B * H, S], cden=[B * BH, S],
        mq=[2, B * H, S], mk=[2, B * H, S], mv=[TOK, H], mm=[CPB, 2 * CH], mout=[B * H, S], mden=[B * BH, S],
        rself=[2, B * NH, S], rwide=[2, B * BH, S], comb=[B * H, S], x1=[TOK, H], xq=[2, B * H, S], xk=[2, B * H, 2 * EP], xv=[B * NG * 2 * EP, GH * AH],
        xm=[CPB, GH * CH], xcraw=[B * NH * AH, S]).items()}

    def named(**names):
        return {key: scr[name] for key, name in names.items()}

    with ExitStack() as stack:
        ident = Kit(nc, stack, "all").sb("ident", [P, P])
        identity_phase(nc, ident)
        input_projections(nc, A, scr, ident)
        attend_narrow(nc, scr)
        attend_wide(nc, named(q="cq", k="ck", v="cv", m="cm", out="cout", den="cden"), "ca")
        join_attention(nc, A, scr)
        attend_wide(nc, named(q="mq", k="mk", v="mv", m="mm", out="mout", den="mden"), "mc")
        clear_semaphores(nc)
        project_and_norm(nc, A, named(comb="comb", cout="mout", cden="mden", x1="x1", xq="xq", recip="rwide"), ident, False)
        clear_semaphores(nc)
        with ExitStack() as inner:
            k = Kit(nc, inner, "bias")
            dist, distT = k.sb("dist", [P, B, S // P, S2]), k.sb("distT", [EP, B, 2, S])
            context_projections(nc, A, scr, ident, dist, distT)
            attend_cross(nc, named(xq="xq", xk="xk", xv="xv", m="xm", craw="xcraw"), dist, distT)
        k = Kit(nc, stack, "x2")
        xa, xb = k.sb("a", [P, KH, TOK], FR), k.sb("b", [P, KH, TOK], FR)
        acc = k.sb("acc", [P, TOK // P, H])
        weight = k.sb("weight", [P, NE + 1, TOK // P])
        project_and_norm(nc, A, named(craw="xcraw", x1="x1", recip="rself"), ident, True, (xa, xb, acc))
        clear_semaphores(nc)
        k = Kit(nc, stack, "ew")
        expert_weights = k.sb("raw", [P, 2, EW]), k.sb("a", [P, 2, EW], FR), k.sb("b", [P, 2, EW], FR)
        route(nc, A, ident, xa, xb, weight, expert_weights)
        run_experts(nc, A, xa, xb, acc, weight, expert_weights, out)


INPUTS = ["x", "ctx_1024", "fside_BxSxS2_0"] + [f"L0_attn_{n}" for n in (
    "cons_vec", "Wq", "bq", "Wk", "bk", "Wv", "bv", "cg_W", "cg_b", "am_W", "am_b", "ca_Win", "ca_bin", "ca_Wout",
    "ca_bout", "mc_Win", "mc_bin", "mc_Wout", "mc_bout", "Wo", "bo")] + [f"L0_xattn_{n}" for n in (
        "Wq", "bq", "Wk", "bk", "Wv", "bv", "Wo", "bo", "distance_scaling")] + [f"L0_ffn_{n}" for n in (
            "gate_w", "w_gate", "w_up", "w_down", "ws_gate", "ws_up", "ws_down")]


def kernel(**inputs):
    import numpy as np
    import concourse.bacc as bacc
    from concourse.bass_utils import run_bass_kernel_spmd

    nc = bacc.Bacc("TRN2", target_bir_lowering=False, num_devices=1)
    arrays, dram = {}, {}
    for name in INPUTS:
        a = np.asarray(inputs[name])
        if name in ("L0_xattn_Wq", "L0_xattn_Wk", "L0_xattn_Wv", "L0_xattn_Wo"):
            a = a.T
        if a.ndim == 0:
            a = a.reshape(1)
        a = np.ascontiguousarray(a)
        arrays[f"in_{name}_dram"] = a
        dram[name] = nc.dram_tensor(f"in_{name}_dram", a.shape, mybir.dt.from_np(a.dtype), kind="ExternalInput").ap()
    out = nc.dram_tensor("out_0_dram", (B, S, H), F32, kind="ExternalOutput").ap()
    decoder_layer(nc, dram, out.rearrange("b s h -> (b s) h"))
    r = run_bass_kernel_spmd(nc, [arrays], core_ids=[0])
    return r.results[0]["out_0_dram"]
```
